# Optimizing a Trainium2 kernel written in Bass

```python
import numpy as np
import jax
import jax.numpy as jnp

def _softmax(x, axis=-1):
    return jax.nn.softmax(x, axis=axis)

def _gelu(x):
    return jax.nn.gelu(x, approximate=True)

def _silu(x):
    return jax.nn.silu(x)

def _sigmoid(x):
    return jax.nn.sigmoid(x)

def _layernorm(x, axis=-1, eps=1e-05):
    m = jnp.mean(x, axis=axis, keepdims=True)
    v = jnp.var(x, axis=axis, keepdims=True)
    return (x - m) / jnp.sqrt(v + eps)

def _scatter_add(tgt, idx, src, axis=0):
    return tgt.at[idx].add(src)

def _segment_sum(src, seg, n):
    return jax.ops.segment_sum(src, seg, n)
kernel_name = 'mk_gnn_resnorm_d4_gnn_r32_4f6c92'

def setup_inputs(seed: int=0):
    np.random.seed(seed)
    _w = jnp.asarray

    def _rec_inputs():
        import jax
        import jax.numpy as jnp
        _gk = jax.random.key(seed)
        x = -0.000202 + 1 * jax.random.normal(jax.random.fold_in(_gk, 1), (50000, 128), jnp.float32)
        src = jax.random.randint(jax.random.fold_in(_gk, 2), (25000,), 0, 50000, jnp.int32)
        dst = jnp.minimum((50000 * jax.random.uniform(jax.random.fold_in(_gk, 3), (25000,)) ** 2.0).astype(jnp.int32), 49999)
        _o = jnp.argsort(dst, stable=True)
        src = src[_o]
        dst = dst[_o]
        edge_attr_64 = 0.000189758 + 1.00013 * jax.random.normal(jax.random.fold_in(_gk, 12), (25000, 64), jnp.float32)
        return (x, src, dst, edge_attr_64)
    x, src, dst, edge_attr_64 = _rec_inputs()

    def _L0_gnn_setup():
        import jax, jax.numpy as jnp
        import numpy as np
        N_NODES = 50000
        NEG_SLOPE = 0.2

        def gat_layer(x, W, attn_l, attn_r, bias, src, dst, num_nodes):
            H, D = attn_l.shape
            feat = (x @ W).reshape(num_nodes, H, D)
            el = jnp.sum(feat * attn_l[None], axis=-1)
            er = jnp.sum(feat * attn_r[None], axis=-1)
            e = jax.nn.leaky_relu(el[src] + er[dst], NEG_SLOPE)
            m = jax.ops.segment_max(e, dst, num_segments=num_nodes)
            ee = jnp.exp(e - m[dst])
            s = jax.ops.segment_sum(ee, dst, num_segments=num_nodes)
            alpha = ee / s[dst]
            msg = feat[src] * alpha[:, :, None]
            rst = jax.ops.segment_sum(msg, dst, num_segments=num_nodes)
            return rst + bias.reshape(1, H, D)
        key = jax.random.key(seed)
        ks = jax.random.split(key, 12)
        in_dim, hid, heads, out_dim = (128, 16, 4, 128)
        n_edges = 25000
        x = jax.random.normal(ks[0], (N_NODES, in_dim), dtype=jnp.float32)
        src = jax.random.randint(ks[1], (n_edges,), 0, N_NODES, dtype=jnp.int32)
        dst = jax.random.randint(ks[2], (n_edges,), 0, N_NODES, dtype=jnp.int32)
        sc1 = 1.0 / np.sqrt(in_dim)
        W1 = jax.random.normal(ks[3], (in_dim, heads * hid), dtype=jnp.float32) * sc1
        al1 = jax.random.normal(ks[4], (heads, hid), dtype=jnp.float32) * 0.1
        ar1 = jax.random.normal(ks[5], (heads, hid), dtype=jnp.float32) * 0.1
        b1 = jnp.zeros((heads * hid,), dtype=jnp.float32)
        in2 = heads * hid
        sc2 = 1.0 / np.sqrt(in2)
        W2 = jax.random.normal(ks[6], (in2, out_dim), dtype=jnp.float32) * sc2
        al2 = jax.random.normal(ks[7], (1, out_dim), dtype=jnp.float32) * 0.1
        ar2 = jax.random.normal(ks[8], (1, out_dim), dtype=jnp.float32) * 0.1
        b2 = jnp.zeros((out_dim,), dtype=jnp.float32)
        return {'x': x, 'src': src, 'dst': dst, 'W1': W1, 'al1': al1, 'ar1': ar1, 'b1': b1, 'W2': W2, 'al2': al2, 'ar2': ar2, 'b2': b2}
    _L0_gnn_all = _L0_gnn_setup()
    _L0_gnn_in = {k: v for k, v in _L0_gnn_all.items() if k in ('W1', 'al1', 'ar1', 'b1', 'W2', 'al2', 'ar2', 'b2')}
    del _L0_gnn_all

    def _L1_gnn_setup():
        import jax, jax.numpy as jnp
        import numpy as np
        N = 50000
        E = 20000
        D = 128
        key = jax.random.key(seed)
        k1, k2, k3, k4 = jax.random.split(key, 4)
        x = jax.random.normal(k1, (N, D), dtype=jnp.float32)
        edge_index = jax.random.randint(k2, (2, E), 0, N, dtype=jnp.int64)
        W = jax.random.normal(k3, (D, D), dtype=jnp.float32) * (1.0 / np.sqrt(D))
        b = jax.random.normal(k4, (D,), dtype=jnp.float32) * 0.01
        return {'x': x, 'edge_index': edge_index, 'W': W, 'b': b}
    _L1_gnn_all = _L1_gnn_setup()
    _L1_gnn_in = {k: v for k, v in _L1_gnn_all.items() if k in ('W', 'b')}
    del _L1_gnn_all

    def _L2_gnn_setup():
        import jax, jax.numpy as jnp
        import numpy as np
        NODE_DIM, EDGE_DIM, OUT_DIM = (128, 64, 128)
        N_NODES, N_EDGES = (50000, 25000)
        key = jax.random.key(seed)
        ks = jax.random.split(key, 12)
        x = jax.random.normal(ks[0], (N_NODES, NODE_DIM), dtype=jnp.float32)
        edge_index = jax.random.randint(ks[1], (2, N_EDGES), 0, N_NODES, dtype=jnp.int64)
        edge_attr = jax.random.normal(ks[2], (N_EDGES, EDGE_DIM), dtype=jnp.float32)
        s = 0.05
        W1 = jax.random.normal(ks[3], (NODE_DIM + EDGE_DIM, OUT_DIM), dtype=jnp.float32) * s
        b1 = jnp.zeros((OUT_DIM,), dtype=jnp.float32)
        W2 = jax.random.normal(ks[4], (OUT_DIM, OUT_DIM), dtype=jnp.float32) * s
        b2 = jnp.zeros((OUT_DIM,), dtype=jnp.float32)
        Wm = jax.random.normal(ks[5], (OUT_DIM, OUT_DIM), dtype=jnp.float32) * s
        bm = jnp.zeros((OUT_DIM,), dtype=jnp.float32)
        Wx = jax.random.normal(ks[6], (OUT_DIM, OUT_DIM), dtype=jnp.float32) * s
        bx = jnp.zeros((OUT_DIM,), dtype=jnp.float32)
        Ws = jax.random.normal(ks[7], (OUT_DIM, OUT_DIM), dtype=jnp.float32) * s
        bs = jnp.zeros((OUT_DIM,), dtype=jnp.float32)
        return {'x': x, 'edge_index': edge_index, 'edge_attr': edge_attr, 'W1': W1, 'b1': b1, 'W2': W2, 'b2': b2, 'Wm': Wm, 'bm': bm, 'Wx': Wx, 'bx': bx, 'Ws': Ws, 'bs': bs}
    _L2_gnn_all = _L2_gnn_setup()
    _L2_gnn_in = {k: v for k, v in _L2_gnn_all.items() if k in ('W1', 'b1', 'W2', 'b2', 'Wm', 'bm', 'Wx', 'bx', 'Ws', 'bs')}
    del _L2_gnn_all

    def _L3_gnn_setup():
        import jax, jax.numpy as jnp
        import numpy as np
        N = 50000
        E = 25000
        IN = 128
        H = 1
        C = 128
        NEG_SLOPE = 0.2
        key = jax.random.key(seed)
        k1, k2, k3, k4, k5 = jax.random.split(key, 5)
        x = jax.random.normal(k1, (N, IN), jnp.float32)
        src = jax.random.randint(k2, (E,), 0, N)
        dst = jax.random.randint(k3, (E,), 0, N)
        loops = jnp.arange(N)
        edge_index = jnp.stack([jnp.concatenate([src, loops]), jnp.concatenate([dst, loops])]).astype(jnp.int64)
        W = jax.random.normal(k4, (IN, H * C), jnp.float32) * np.float32(1.0 / np.sqrt(IN))
        att = jax.random.normal(k5, (H, 2 * C), jnp.float32) * np.float32(0.1)
        bias = jnp.zeros((H * C,), jnp.float32)
        return {'x': x, 'edge_index': edge_index, 'W': W, 'att': att, 'bias': bias}
    _L3_gnn_all = _L3_gnn_setup()
    _L3_gnn_in = {k: v for k, v in _L3_gnn_all.items() if k in ('W', 'att', 'bias')}
    del _L3_gnn_all
    return {'x': x, 'src': src, 'dst': dst, 'edge_attr_64': edge_attr_64, 'L0_gnn_W1': _L0_gnn_in['W1'], 'L0_gnn_al1': _L0_gnn_in['al1'], 'L0_gnn_ar1': _L0_gnn_in['ar1'], 'L0_gnn_b1': _L0_gnn_in['b1'], 'L0_gnn_W2': _L0_gnn_in['W2'], 'L0_gnn_al2': _L0_gnn_in['al2'], 'L0_gnn_ar2': _L0_gnn_in['ar2'], 'L0_gnn_b2': _L0_gnn_in['b2'], 'L1_gnn_W': _L1_gnn_in['W'], 'L1_gnn_b': _L1_gnn_in['b'], 'L2_gnn_W1': _L2_gnn_in['W1'], 'L2_gnn_b1': _L2_gnn_in['b1'], 'L2_gnn_W2': _L2_gnn_in['W2'], 'L2_gnn_b2': _L2_gnn_in['b2'], 'L2_gnn_Wm': _L2_gnn_in['Wm'], 'L2_gnn_bm': _L2_gnn_in['bm'], 'L2_gnn_Wx': _L2_gnn_in['Wx'], 'L2_gnn_bx': _L2_gnn_in['bx'], 'L2_gnn_Ws': _L2_gnn_in['Ws'], 'L2_gnn_bs': _L2_gnn_in['bs'], 'L3_gnn_W': _L3_gnn_in['W'], 'L3_gnn_att': _L3_gnn_in['att'], 'L3_gnn_bias': _L3_gnn_in['bias']}

def reference(x, src, dst, edge_attr_64, L0_gnn_W1, L0_gnn_al1, L0_gnn_ar1, L0_gnn_b1, L0_gnn_W2, L0_gnn_al2, L0_gnn_ar2, L0_gnn_b2, L1_gnn_W, L1_gnn_b, L2_gnn_W1, L2_gnn_b1, L2_gnn_W2, L2_gnn_b2, L2_gnn_Wm, L2_gnn_bm, L2_gnn_Wx, L2_gnn_bx, L2_gnn_Ws, L2_gnn_bs, L3_gnn_W, L3_gnn_att, L3_gnn_bias):
    import jax
    import jax.numpy as jnp

    def _L0_gnn_ref(x, src, dst, W1, al1, ar1, b1, W2, al2, ar2, b2):
        import jax, jax.numpy as jnp
        import numpy as np
        N_NODES = 50000
        NEG_SLOPE = 0.2

        def gat_layer(x, W, attn_l, attn_r, bias, src, dst, num_nodes):
            H, D = attn_l.shape
            feat = (x @ W).reshape(num_nodes, H, D)
            el = jnp.sum(feat * attn_l[None], axis=-1)
            er = jnp.sum(feat * attn_r[None], axis=-1)
            e = jax.nn.leaky_relu(el[src] + er[dst], NEG_SLOPE)
            m = jax.ops.segment_max(e, dst, num_segments=num_nodes)
            ee = jnp.exp(e - m[dst])
            s = jax.ops.segment_sum(ee, dst, num_segments=num_nodes)
            alpha = ee / s[dst]
            msg = feat[src] * alpha[:, :, None]
            rst = jax.ops.segment_sum(msg, dst, num_segments=num_nodes)
            return rst + bias.reshape(1, H, D)
        h = gat_layer(x, W1, al1, ar1, b1, src, dst, N_NODES)
        h = jax.nn.elu(h.reshape(N_NODES, -1))
        h = gat_layer(h, W2, al2, ar2, b2, src, dst, N_NODES)
        return h[:, 0, :]

    def _L1_gnn_ref(x, edge_index, W, b):
        import jax, jax.numpy as jnp
        import numpy as np
        N = 50000
        E = 20000
        D = 128
        src = edge_index[0]
        dst = edge_index[1]
        n = x.shape[0]
        deg = jax.ops.segment_sum(jnp.ones((dst.shape[0],), dtype=x.dtype), dst, num_segments=n)
        deg_inv = jnp.where(deg > 0, 1.0 / deg, 0.0)
        edge_weight = deg_inv[dst]
        h = x @ W.T
        msg = h[src] * edge_weight[:, None]
        out = jax.ops.segment_sum(msg, dst, num_segments=n)
        return out + b

    def _L2_gnn_ref(x, edge_index, edge_attr, W1, b1, W2, b2, Wm, bm, Wx, bx, Ws, bs):
        import jax, jax.numpy as jnp
        import numpy as np
        NODE_DIM, EDGE_DIM, OUT_DIM = (128, 64, 128)
        N_NODES, N_EDGES = (50000, 25000)
        num_nodes = x.shape[0]
        src, dst = (edge_index[0], edge_index[1])
        combined = jnp.concatenate([x[dst], edge_attr], axis=-1)
        messages = jax.nn.relu(combined @ W1 + b1) @ W2 + b2
        agg_sum = jax.ops.segment_sum(messages, dst, num_segments=num_nodes)
        count = jax.ops.segment_sum(jnp.ones((messages.shape[0],), dtype=messages.dtype), dst, num_segments=num_nodes)
        agg_mean = agg_sum / jnp.maximum(count, 1.0)[:, None]
        agg_max = jax.ops.segment_max(messages, dst, num_segments=num_nodes)
        agg_max = jnp.where(jnp.isneginf(agg_max), 0.0, agg_max)
        out = agg_mean @ Wm + bm + (agg_max @ Wx + bx) + (agg_sum @ Ws + bs)
        return out

    def _L3_gnn_ref(x, edge_index, W, att, bias):
        import jax, jax.numpy as jnp
        import numpy as np
        N = 50000
        E = 25000
        IN = 128
        H = 1
        C = 128
        NEG_SLOPE = 0.2
        h = (x @ W).reshape(-1, H, C)
        src, dst = (edge_index[0], edge_index[1])
        hi = h[dst]
        hj = h[src]
        alpha = jnp.einsum('ehc,hc->eh', hi, att[:, :C]) + jnp.einsum('ehc,hc->eh', hj, att[:, C:])
        alpha = jax.nn.leaky_relu(alpha, NEG_SLOPE)
        m = jax.ops.segment_max(alpha, dst, num_segments=N)
        m = jnp.where(jnp.isfinite(m), m, 0.0)
        a = jnp.exp(alpha - m[dst])
        s = jax.ops.segment_sum(a, dst, num_segments=N)
        a = a / (s[dst] + 1e-16)
        out = jax.ops.segment_sum(hj * a[:, :, None], dst, num_segments=N)
        return out.reshape(-1, H * C) + bias
    edge_index = jnp.stack([src, dst])
    x = _layernorm(x + _L0_gnn_ref(x, src, dst, L0_gnn_W1, L0_gnn_al1, L0_gnn_ar1, L0_gnn_b1, L0_gnn_W2, L0_gnn_al2, L0_gnn_ar2, L0_gnn_b2), axis=-1)
    x = _layernorm(x + _L1_gnn_ref(x, edge_index, L1_gnn_W, L1_gnn_b), axis=-1)
    x = _layernorm(x + _L2_gnn_ref(x, edge_index, edge_attr_64, L2_gnn_W1, L2_gnn_b1, L2_gnn_W2, L2_gnn_b2, L2_gnn_Wm, L2_gnn_bm, L2_gnn_Wx, L2_gnn_bx, L2_gnn_Ws, L2_gnn_bs), axis=-1)
    x = _layernorm(x + _L3_gnn_ref(x, edge_index, L3_gnn_W, L3_gnn_att, L3_gnn_bias), axis=-1)
    return x

_drawn_inputs = setup_inputs


def setup_inputs(seed=0):
    import zlib

    import numpy as np

    out = dict(_drawn_inputs(seed))
    spreads = {'L0_gnn_b1': (0.0, 0.1),
     'L0_gnn_b2': (0.0, 0.1),
     'L2_gnn_b1': (0.0, 0.384),
     'L2_gnn_b2': (0.0, 0.1),
     'L2_gnn_bm': (0.0, 0.1),
     'L2_gnn_bx': (0.0, 0.1),
     'L2_gnn_bs': (0.0, 0.1),
     'L3_gnn_bias': (0.0, 0.1)}
    factors = {'L0_gnn_al1': 5.143, 'L0_gnn_ar1': 8.0, 'L0_gnn_ar2': 8.0, 'L1_gnn_b': 5.986}
    for name, (base, spread) in spreads.items():
        noise = np.random.default_rng([zlib.crc32(name.encode()), seed]).standard_normal(out[name].shape)
        drawn = base * np.exp(spread * noise) if base else spread * noise
        out[name] = jnp.asarray(drawn.astype(out[name].dtype))
    for name, factor in factors.items():
        out[name] = (out[name] * factor).astype(out[name].dtype)
    return out
```

```python
from contextlib import ExitStack

import concourse.bass as bass
from concourse import mybir

F32 = mybir.dt.float32
BF16 = mybir.dt.bfloat16
I32 = mybir.dt.int32
U32 = mybir.dt.uint32
U8 = mybir.dt.uint8
ALU = mybir.AluOpType
ACT = mybir.ActivationFunctionType
X = mybir.AxisListType.X

P = 128
N, E, F = 50000, 25000, 128
HEADS, HID = 4, 16
HF = HEADS * HID
FW = HF + HEADS
HW = HF + 1
EF = 64
GT = 4
GE = GT * P
NG = -(-E // GE)
NT = NG * GT
CH = 2 * P
NQ = NT * P // CH
EP = NT * P
RING = 4
BODIES = NG // RING
NJ = N // P
NTAIL = N - NJ * P
DK = 8
DLAST = NJ - (NG - 1) * DK
SKIP = 1 << 16
BIG = 1.0e38
FAR = -3.0e38
EPS = 1e-5
SLOPE = 0.2
assert NG % RING == 1 and NQ * 2 == NT and 0 < DLAST < DK


def program(nc, x, src, dst, ea, W1, al1, ar1, b1, W2, al2, ar2, b2, L1W, L1b,
            M1, m1, M2, m2, Mm, bm, Mx, bx, Ms, bs, W3, att, b4, out):
    def dram(name, shape, dt=F32):
        return nc.dram_tensor(name, shape, dt, kind="Internal").ap()

    hidden_t = dram("hidden_t", (N, HW))
    x1_t = dram("x1_t", (N, F))
    x3_t = dram("x3_t", (N, F))
    xd_e = dram("xd_e", (NG, P, GT * F))
    x1_e = dram("x1_e", (NG, P, GT * F))
    x2_e = dram("x2_e", (NG, P, GT * F))
    x3_e = dram("x3_e", (NG, P, GT * F))
    xs_e = dram("xs_e", (NG, P, GT * F))
    cont_d = dram("cont_d", (2, EP), U8)

    with ExitStack() as ctx:
        def sb(name, shape, dt=F32):
            return ctx.enter_context(nc.sbuf_tensor(name, shape, dt))

        def sem(name):
            return ctx.enter_context(nc.semaphore(name))

        bank = [ctx.enter_context(nc.psum_tensor(f"bank{n}", [P, 512], F32)) for n in range(8)]

        ident = sb("ident", [P, P])
        before = sb("before", [P, NQ])
        after = sb("after", [P, NQ])
        ones = sb("ones", [P, P])
        W1x = sb("W1x", [P, FW])
        W1r = sb("W1r", [P, HEADS])
        W2_s = sb("W2_s", [HF, F])
        W2x = sb("W2x", [HF, HF + 2])
        L1T = sb("L1T", [P, F])
        raw = sb("raw", [P, F])
        M1a = sb("M1a", [P, F])
        M1b = sb("M1b", [EF, F])
        M2_s = sb("M2_s", [P, F])
        Mm_s = sb("Mm_s", [P, F])
        Mx_s = sb("Mx_s", [P, F])
        Ms_s = sb("Ms_s", [P, F])
        W3_s = sb("W3_s", [P, F])
        W3T = sb("W3T", [P, F])
        bias = sb("bias", [P, 4, F])
        biasc = sb("biasc", [P, 4, F])
        brow = sb("brow", [1, 3, F])
        bT = sb("bT", [P, 4])
        BB = sb("BB", [P, 16])
        tmpw = sb("tmpw", [P, F])
        b1c = sb("b1c", [HF, 4])
        m1c = sb("m1c", [P, 1])
        m2c = sb("m2c", [P, 1])
        attc = sb("attc", [P, 2])
        attb = sb("attb", [P, 2, F])
        hcol = sb("hcol", [HF, P])
        wmean = sb("wmean", [P, 4])

        cv = sb("cv", [P, 10, CH])
        first = sb("first", [P, CH])
        last = sb("last", [P, CH])
        contb = sb("contb", [P, 2, CH], U8)
        keepf = sb("keepf", [P, CH])
        keepb = sb("keepb", [P, CH])
        penf = sb("penf", [P, CH])
        penb = sb("penb", [P, CH])
        head = sb("head", [P, CH])
        tail = sb("tail", [P, CH])
        headp = sb("headp", [P, CH])
        tailp = sb("tailp", [P, CH])
        linkf = sb("linkf", [P, NQ])
        linkb = sb("linkb", [P, NQ])
        linkfp = sb("linkfp", [P, NQ])
        linkbp = sb("linkbp", [P, NQ])
        endd = sb("endd", [P, 2])
        cont = sb("cont", [P, EP], U8)
        idx = sb("idx", [P, 4, NT + 8], I32)
        SRC, DST, LAST, FIRST = range(4)
        lastR = sb("lastR", [P, NT])
        invR = sb("invR", [P, NT])
        ixr = sb("ixr", [P, RING, 2, GT], I32)

        big = sb("big", [P, NT * FW + DK * F])
        feat = big[:, 0:NT * FW].rearrange("p (t f) -> p t f", f=FW)
        def part(start, n):
            return big[:, start * GE:start * GE + n]

        bload = part(0, 2 * F).rearrange("p (n f) -> p n f", f=F)
        alb = part(1, 2 * F).rearrange("p (n f) -> p n f", f=F)
        e_src, e_dst, e_prev, e_next = (part(2 + n, CH).bitcast(I32) for n in range(4))
        hconst = part(6, 10 * HW).rearrange("p (n f) -> p n f", f=HW)
        X2T = part(0, 2 * GE).rearrange("p (s e) -> p s e", s=2)
        MX = part(2, 2 * GE).rearrange("p (s e) -> p s e", s=2)
        xd2 = sb("xd2", [P, DK * F])
        zA = part(4, 2 * GE).rearrange("p (s t f) -> p s t f", s=2, f=F)
        eaT = part(6, 2 * GE)[0:EF].rearrange("p (s e) -> p s e", s=2)
        neg = part(8, GE).bitcast(BF16).rearrange("p (s e) -> p s e", s=2)
        slim = [cv[:, n:n + 1, :] for n in range(9)]
        xload = sb("xload", [P, 2, GT, F])
        xloadf = xload[:, :, :, :].rearrange("p r t f -> p r (t f)")
        ring = sb("ring", [P, RING, 2, GT, F])
        ringf = ring[:, :, :, :, :].rearrange("p r a t f -> p r a (t f)")
        outr = sb("outr", [P, RING, GT, F])
        outf = outr[:, :, :, :].rearrange("p r t f -> p r (t f)")
        xT = sb("xT", [P, 2, 2, GE])
        msg = sb("msg", [P, 2, GT, F])
        G = sb("G", [P, 2, GE])
        z = sb("z", [P, 2, GT, F])
        hT = sb("hT", [P, 2, 3, GE])
        blocks = [t.rearrange("p n -> p n") for t in (
            msg[:, :, :, :].rearrange("p s t f -> p (s t f)"), G[:, :, :].rearrange("p s e -> p (s e)"),
            z[:, :, :, :].rearrange("p s t f -> p (s t f)"), xload[:, :, :, :].rearrange("p s t f -> p (s t f)"),
            outf[:, 0:2, :].rearrange("p s e -> p (s e)"), outf[:, 2:4, :].rearrange("p s e -> p (s e)"),
            hT[:, 0, 0:2, :].rearrange("p s e -> p (s e)"), hT[:, 1, 1:3, :].rearrange("p s e -> p (s e)"),
            big[:, NT * FW:NT * FW + DK * F], xd2[:, :])]
        kf = [t.rearrange("p (k f) -> p k f", f=F) for t in blocks]
        u, y, xin, dxT = kf[0:4], kf[4:7], kf[7:9], blocks[9]
        wide = [t.rearrange("p (h c) -> p h c", h=HEADS) for t in blocks[0:7]]
        sd = sb("sd", [P, DK])
        epsc = sb("epsc", [P, 1])
        stats = sb("stats", [P, DK, 6])
        mv = sb("mv", [P, 2, DK, 2])
        rn = sb("rn", [P, 2, GT, 2])
        rho = sb("rho", [P, 2, 4, DK])
        small = sb("small", [P, 16, DK])
        dots = sb("dots", [P, DK, 4])
        logit = sb("logit", [P, NT, 1])
        alpha = sb("alpha", [P, NT, HEADS])
        own = sb("own", [P, NT])
        carry = sb("carry", [P, 4, HEADS])
        R1 = G

        idle = sem("idle")
        phase = sem("phase")
        sems = {}

        def sem_of(name):
            if name not in sems:
                sems[name] = sem(name)
            return sems[name]

        def S(name):
            return sem_of(shared(name)[0])

        SHARED = {
            "in": (4, {"a": 2 * GT * 16, "c": GT * 16, "e": GT * 16, "g": GT * 16}),
            "out": (4, {"a": 16, "d": 16, "e": 16, "f": 16, "g": 16}),
            "sc": (4, {"b": GT * 16, "d": GT * 16, "f": GT * 16, "h": GT * 16}),
            "ld": (2, {"d": 16, "e": 16, "g": 16, "h": 16}),
            "ix": (1, {"a": 2, "b": 1, "c": 1, "d": 1, "e": 1, "f": 1, "g": 1, "h": 1}),
            "tr": (1, {"a": 1, "b": 1, "d": 1, "e": 1, "f": 1, "h": 1}),
            "scan": (1, {"b": 1, "d": 1, "e": 1, "h": 1}),
            "mm": (1, {"a": 1, "b": 1, "d": 1, "e": 1, "h": 1}),
            "z": (1, {"d": 1, "e": 1, "f": 1, "h": 1}),
            "var": (1, {"d": 1, "e": 1, "f": 1, "h": 1}),
            "sd": (1, {"d": 1, "e": 1, "f": 1, "h": 1}),
            "st": (1, {"d": 1, "e": 1, "f": 1, "h": 1}),
            "row": (1, {"b": 1, "d": 1, "e": 1, "f": 1, "h": 1}),
            "msg": (1, {"b": 1, "d": 1, "f": 1, "h": 1}),
        }

        def shared(name):
            tag, _, kind = name.partition("_")
            slot = kind[-1] if kind[-1:].isdigit() else ""
            kind = kind[:-1] if slot else kind
            ways, users = SHARED.get(kind, (0, {}))
            if tag not in users or bool(slot) != (ways > 1):
                return name, 0
            uses = len(range(int(slot), NG, ways)) if slot else NG + (kind == "ix")
            start = 0
            for t, per in users.items():
                if t == tag:
                    return "g_" + kind + slot, start
                start += per * uses

        def wait(eng, name, n):
            sem_name, start = shared(name)
            eng.wait_ge(sem_of(sem_name), n + start)
            if eng is nc.sync and not isinstance(n, int):
                pause(eng)

        def pause(eng):
            eng.sem_inc(idle, 1)

        phases = {}

        def barrier(eng):
            phases[eng] = phases.get(eng, 0) + 1
            eng.drain().then_inc(phase, 1)
            eng.wait_ge(phase, 5 * phases[eng])

        def groups(eng, step):
            for j in range(RING):
                step(0, j)
            with eng.Fori(1, BODIES) as i:
                for j in range(RING):
                    step(i, j)
            step(BODIES, 0)

        def count(eng, name, i, j, lag=0, per=1):
            n = RING * i + j + 1 - lag
            if isinstance(n, int) and n <= 0:
                return
            wait(eng, name, n * per)

        def slot_done(eng, name, i, j, per, lag=0):
            n = i + 1 - lag
            if isinstance(n, int) and n <= 0:
                return
            wait(eng, f"{name}{j}", n * per)

        class Chain:

            def __init__(self, eng, name):
                self.eng, self.sem, self.n, self.base, self.per = eng, S(name), 0, 0, None

            def at(self, i, j):
                if self.per is None and not (i == 0 and j == 0 and isinstance(i, int)):
                    self.per = self.n
                if self.per is not None:
                    assert self.n == self.per, (self.n, self.per)
                    self.base = (RING * i + j) * self.per
                self.n = 0

            def do(self, ins):
                ins.then_inc(self.sem, 1)
                self.n += 1
                return ins

            def hold(self):
                self.eng.wait_ge(self.sem, self.base + self.n)

            def link(self, ins):
                self.do(ins)
                self.hold()

        def four(g):
            return bass.ds(g * GT, GT)

        def col(v):
            return v.rearrange("(p a) -> p a", a=1)

        def rowof(v):
            return v.rearrange("(a n) -> a n", a=1)

        FULL = E // CH
        REST = E - FULL * CH

        def prep_sync(sp):
            w = S("weights")
            loads = [
                (W1x[:, 0:HF], W1), (W2_s[:], W2), (raw[:], L1W),
                (M1a[:], M1[0:F, :]), (M1b[:], M1[F:F + EF, :]), (M2_s[:], M2), (Mm_s[:], Mm), (Mx_s[:], Mx),
                (Ms_s[:], Ms), (W3_s[:], W3),
                (bias[:, 0, :], b2.partition_broadcast(P)), (bias[:, 1, :], L1b.partition_broadcast(P)),
                (bias[:, 2, :], bm.partition_broadcast(P)), (bias[:, 3, :], b4.partition_broadcast(P)),
                (bload[:, 0, :], bx.partition_broadcast(P)), (bload[:, 1, :], bs.partition_broadcast(P)),
                (alb[:, 0, 0:HF], al1.rearrange("h d -> (h d)").partition_broadcast(P)),
                (alb[:, 0, HF:], ar1.rearrange("h d -> (h d)").partition_broadcast(P)),
                (hT[0:HF, 0, 0, 0:F], al2.rearrange("h d -> (h d)").partition_broadcast(HF)),
                (hT[0:HF, 0, 1, 0:F], ar2.rearrange("h d -> (h d)").partition_broadcast(HF)),
                (b1c[:, 0:1], col(b1)), (m1c[:], col(m1)), (m2c[:], col(m2)),
                (attc[:, 0:1], col(att[0, 0:F])), (attc[:, 1:2], col(att[0, F:])),
            ]
            for to, frm in loads:
                sp.dma_start(to, frm).then_inc(w, 16)
            prep_sync.loads = len(loads)
            sp.wait_ge(S("pads"), 1)
            edges = [
                (e_src[0:FULL, :], src[0:FULL * CH].rearrange("(q c) -> q c", c=CH)),
                (e_src[FULL:FULL + 1, 0:REST], rowof(src[FULL * CH:E])),
                (e_dst[0:FULL, :], dst[0:FULL * CH].rearrange("(q c) -> q c", c=CH)),
                (e_dst[FULL:FULL + 1, 0:REST], rowof(dst[FULL * CH:E])),
                (e_prev[0:1, 1:CH], rowof(dst[0:CH - 1])),
                (e_prev[1:FULL, :], dst[CH - 1:FULL * CH - 1].rearrange("(q c) -> q c", c=CH)),
                (e_prev[FULL:FULL + 1, 0:REST + 1], rowof(dst[FULL * CH - 1:E])),
                (e_next[0:FULL, :], dst[1:FULL * CH + 1].rearrange("(q c) -> q c", c=CH)),
                (e_next[FULL:FULL + 1, 0:REST - 1], rowof(dst[FULL * CH + 1:E])),
            ]
            for to, frm in edges:
                sp.dma_start(to, frm).then_inc(S("edges"), 16)
            sp.wait_ge(S("cont_made"), 2)
            sp.dma_start(cont_d[0, :].rearrange("(q c) -> q c", c=CH), contb[0:NQ, 0, :]).then_inc(S("cont_out"), 16)
            sp.dma_start(cont_d[1, :].rearrange("(q c) -> q c", c=CH), contb[0:NQ, 1, :]) \
                .then_inc(S("cont_out"), 16)
            sp.wait_ge(S("cont_out"), 32)
            sp.dma_start(cont[:], cont_d[0, :].partition_broadcast(P)).then_inc(S("cont_in"), 16)
            sp.wait_ge(S("hconst"), 1)
            main = hidden_t[0:NJ * P, :].rearrange("(p j) f -> p j f", p=P)
            with sp.Fori(0, NJ // 10) as i:
                sp.dma_start(main[:, bass.ds(i * 10, 10), :], hconst[:]).then_inc(S("hfill"), 16)
            sp.dma_start(hidden_t[NJ * P:N, :], hconst[0:NTAIL, 0, :]).then_inc(S("hfill"), 16)
            sp.wait_ge(S("cont_in"), 16)
            sp.wait_ge(S("hfill"), 16 * (NJ // 10 + 1))

        def prep_pool(pool):
            made = S("shapes")
            nc.gpsimd.memset(ident[:], 0.0).then_inc(made, 1)
            nc.gpsimd.memset(before[:], 1.0).then_inc(made, 1)
            nc.gpsimd.memset(after[:], 1.0).then_inc(made, 1)
            pool.wait_ge(made, 3)
            nc.gpsimd.affine_select(out=ident[:], in_=ident[:], compare_op=ALU.not_equal, fill=1.0, base=0,
                                    pattern=[[-1, P]], channel_multiplier=1).then_inc(made, 1)
            nc.gpsimd.affine_select(out=before[:], in_=before[:], compare_op=ALU.is_gt, fill=0.0, base=0,
                                    pattern=[[1, NQ]], channel_multiplier=-1).then_inc(made, 1)
            nc.gpsimd.affine_select(out=after[:], in_=after[:], compare_op=ALU.is_gt, fill=0.0, base=0,
                                    pattern=[[-1, NQ]], channel_multiplier=1).then_inc(made, 1)

        def prep_tensor(pe):
            pe.wait_ge(S("shapes"), 6)
            pe.wait_ge(S("weights"), 16 * LOADS)
            nc.tensor.transpose(bank[0][:, 0:P], raw[:], ident[:])
            nc.tensor.transpose(bank[0][:, P:2 * P], W3_s[:], ident[:]).then_inc(S("wt"), 1)
            pe.wait_ge(S("biasc"), 1)
            for n in range(4):
                ins = nc.tensor.transpose(bank[1][:, n * P:(n + 1) * P], biasc[:, n, :], ident[:])
            ins.then_inc(S("bt"), 1)
            pe.wait_ge(S("attb"), 1)
            for n in range(2):
                ins = nc.tensor.matmul(bank[2][:, n * P:(n + 1) * P], attb[:, n, :], W3T[:], start=True, stop=True)
            ins.then_inc(S("wa"), 1)
            pe.wait_ge(S("bcols"), 1)
            for n in range(4):
                ins = nc.tensor.matmul(bank[3][:, 4 * n:4 * n + 4], raw4[n], bT[:], start=True, stop=True)
            ins.then_inc(S("bb"), 1)
            pe.wait_ge(S("hcol"), 1)
            nc.tensor.matmul(bank[4][:, 0:HW], hcol[:], W2x[:, 0:HW], start=True, stop=True).then_inc(S("hrow0"), 1)
            pe.wait_ge(S("ends"), 1)
            nc.tensor.transpose(bank[5][0:NQ, 0:NQ], cv[0:NQ, 1, 0:1].to_broadcast([NQ, NQ]), ident[0:NQ, 0:NQ])
            nc.tensor.transpose(bank[5][0:NQ, P:P + NQ], cv[0:NQ, 1, CH - 1:CH].to_broadcast([NQ, NQ]),
                                ident[0:NQ, 0:NQ]).then_inc(S("endrows"), 1)
            pe.wait_ge(S("links"), 1)
            nc.tensor.matmul(bank[6][0:NQ, 0:1], linkf[0:NQ, :], cv[0:NQ, 6, CH - 1:CH], start=True, stop=True)
            nc.tensor.matmul(bank[6][0:NQ, 1:2], linkb[0:NQ, :], cv[0:NQ, 7, 0:1],
                             start=True, stop=True).then_inc(S("degc"), 1)
            pe.wait_ge(S("tomake"), 1)
            for m in range(6):
                if m % 2 == 0 and m:
                    pe.wait_ge(S("torow"), m)
                for r in range(2):
                    ins = nc.tensor.transpose(bank[m % 2][:, r * P:r * P + NQ],
                                              rowsrc[m][0:NQ, r * P:(r + 1) * P], ident[0:NQ, 0:NQ])
                ins.then_inc(S("rowps"), 1)

        rowsrc = [cv[:, 0, :], cv[:, 2, :], cv[:, 3, :], cv[:, 4, :], last, cv[:, 5, :]]
        raw4 = [msg[:, 0, n, :] for n in range(4)]

        def prep_vector(v):
            c = Chain(v, "prep_dve")
            for t in (e_src, e_dst, e_prev, e_next):
                c.do(v.memset(t[:], 0 if t is e_src else N))
            c.hold()
            v.memset(e_prev[0:1, 0:1], -1).then_inc(S("pads"), 1)
            v.memset(ones[:], 1.0)
            v.memset(epsc[:], EPS)
            c.do(v.memset(idx[:], 0))
            v.wait_ge(S("weights"), 16 * LOADS)
            v.wait_ge(S("shapes"), 6)
            for n, to in ((0, W1x[:, HF:FW]), (1, W1r[:])):
                c.link(v.tensor_tensor(tmpw[:, 0:HF], W1x[:, 0:HF], alb[:, 0, n * HF:(n + 1) * HF], ALU.mult))
                c.link(v.tensor_reduce(to, tmpw[:, 0:HF].rearrange("p (h d) -> p h d", h=HEADS), X, ALU.add))
            c.do(v.tensor_copy(W2x[:, 0:HF], ident[0:HF, 0:HF]))
            for n in range(2):
                c.link(v.tensor_tensor(tmpw[0:HF, :], W2_s[:], hT[0:HF, 0, n, 0:F], ALU.mult))
                c.link(v.tensor_reduce(W2x[:, HF + n:HF + n + 1], tmpw[0:HF, :], X, ALU.add))
            c.link(v.tensor_tensor(bias[:, 2, :], bias[:, 2, :], bload[:, 0, :], ALU.add))
            c.link(v.tensor_tensor(bias[:, 2, :], bias[:, 2, :], bload[:, 1, :], ALU.add))
            for n, k in ((0, 0), (1, 2), (2, 3)):
                c.do(v.tensor_copy(brow[0:1, n, :], bias[0:1, k, :]))
            c.link(v.tensor_reduce(wmean[:], bias[:], X, ALU.add))
            c.link(v.tensor_scalar(wmean[:], wmean[:], -1.0 / F, None, ALU.mult))
            for n in range(4):
                c.do(v.tensor_scalar(biasc[:, n, :], bias[:, n, :], wmean[:, n:n + 1], None, ALU.add))
            c.hold()
            v.sem_inc(S("biasc"), 1)
            v.wait_ge(S("wt"), 1)
            c.do(v.tensor_copy(L1T[:], bank[0][:, 0:P]))
            c.do(v.tensor_copy(W3T[:], bank[0][:, P:2 * P]))
            for n in range(2):
                c.do(v.tensor_scalar(attb[:, n, :], ones[:], attc[:, n:n + 1], None, ALU.mult))
            c.hold()
            v.sem_inc(S("attb"), 1)
            v.wait_ge(S("bt"), 1)
            c.link(v.tensor_scalar(bT[:], bank[1][:, :].rearrange("p (n m) -> p n m", n=4)[:, :, 0], 1.0 / F, None,
                                   ALU.mult))
            for n in range(4):
                c.do(v.tensor_scalar(raw4[n], ones[:], bank[1][:, n * P:n * P + 1], None, ALU.mult))
            c.hold()
            v.sem_inc(S("bcols"), 1)
            v.wait_ge(S("wa"), 1)
            c.do(v.tensor_copy(attb[:], bank[2][:, 0:2 * P].rearrange("p (n f) -> p n f", n=2)))
            v.wait_ge(S("bb"), 1)
            c.do(v.tensor_copy(BB[:], bank[3][:, 0:16]))
            v.tensor_scalar(b1c[:, 1:2], b1c[:, 0:1], 0.0, None, ALU.min).then_inc(S("b1min"), 1)
            c.do(v.tensor_scalar(b1c[:, 2:3], b1c[:, 0:1], 0.0, None, ALU.max))
            v.wait_ge(S("b1exp"), 1)
            c.hold()
            c.link(v.scalar_tensor_tensor(b1c[:, 3:4], b1c[:, 3:4], -1.0, b1c[:, 2:3], ALU.add, ALU.add))
            v.tensor_scalar(hcol[:], ones[0:HF, :], b1c[:, 3:4], None, ALU.mult).then_inc(S("hcol"), 1)
            v.wait_ge(S("hrow0"), 1)
            for n in range(10):
                c.do(v.tensor_copy(hconst[:, n, :], bank[4][:, 0:HW]))
            c.hold()
            v.sem_inc(S("hconst"), 1)

            v.wait_ge(S("edges"), 16 * 9)
            for n, t in ((0, e_src), (1, e_dst), (8, e_prev), (9, e_next)):
                c.do(v.tensor_copy(cv[:, n, :], t[:]))
            c.hold()
            q = slice(0, NQ)
            v.sem_inc(S("ends"), 1)
            c.do(v.tensor_tensor(first[:], cv[:, 1, :], cv[:, 8, :], ALU.not_equal))
            c.do(v.tensor_tensor(last[:], cv[:, 1, :], cv[:, 9, :], ALU.not_equal))
            v.tensor_tensor(contb[:, 0, :], cv[:, 1, :], cv[:, 8, :], ALU.is_equal).then_inc(S("cont_made"), 1)
            v.tensor_tensor(contb[:, 1, :], cv[:, 1, ::-1], cv[:, 9, ::-1], ALU.is_equal).then_inc(S("cont_made"), 1)
            c.hold()
            c.do(v.tensor_scalar(keepf[:], first[:], -1.0, 1.0, ALU.mult, ALU.add))
            c.do(v.tensor_scalar(keepb[:], last[:], -1.0, 1.0, ALU.mult, ALU.add))
            c.hold()
            c.do(v.memset(keepf[:, 0:1], 0.0))
            c.do(v.memset(keepb[:, CH - 1:CH], 0.0))
            c.do(v.tensor_scalar(head[:], cv[:, 1, :], cv[:, 1, 0:1], None, ALU.is_equal))
            c.do(v.tensor_scalar(tail[:], cv[:, 1, :], cv[:, 1, CH - 1:CH], None, ALU.is_equal))
            c.hold()
            for to, frm in ((penf, keepf), (penb, keepb), (headp, head), (tailp, tail)):
                c.do(v.tensor_scalar(to[:], frm[:], -1.0, BIG, ALU.add, ALU.mult))
            v.wait_ge(S("endrows"), 1)
            c.do(v.scalar_tensor_tensor(linkf[q, :], bank[5][q, 0:NQ], cv[q, 1, CH - 1:CH], before[q, :],
                                        ALU.is_equal, ALU.mult))
            c.do(v.scalar_tensor_tensor(linkb[q, :], bank[5][q, P:P + NQ], cv[q, 1, 0:1], after[q, :],
                                        ALU.is_equal, ALU.mult))
            c.hold()
            c.do(v.tensor_scalar(linkfp[q, :], linkf[q, :], -1.0, BIG, ALU.add, ALU.mult))
            c.do(v.tensor_scalar(linkbp[q, :], linkb[q, :], -1.0, BIG, ALU.add, ALU.mult))
            c.link(v.memset(cv[:, 5, :], 1.0))
            c.do(v.tensor_tensor_scan(cv[q, 6, :], keepf[q, :], cv[q, 5, :], 0.0, ALU.mult, ALU.add))
            c.do(v.tensor_tensor_scan(cv[q, 7, ::-1], keepb[q, ::-1], cv[q, 5, :], 0.0, ALU.mult, ALU.add))
            c.hold()
            v.sem_inc(S("links"), 1)
            v.wait_ge(S("degc"), 1)
            c.link(v.tensor_copy(carry[q, 0, 0:2], bank[6][q, 0:2]))
            c.link(v.scalar_tensor_tensor(cv[q, 6, :], cv[q, 6, :], -1.0, cv[q, 7, :], ALU.add, ALU.add))
            c.link(v.scalar_tensor_tensor(cv[q, 6, :], head[q, :], carry[q, 0, 0:1], cv[q, 6, :], ALU.mult, ALU.add))
            c.link(v.scalar_tensor_tensor(cv[q, 6, :], tail[q, :], carry[q, 0, 1:2], cv[q, 6, :], ALU.mult, ALU.add))
            c.link(v.reciprocal(cv[q, 5, :], cv[q, 6, :]))
            c.do(v.tensor_scalar(cv[:, 2, :], cv[:, 1, :], float(N - 1), None, ALU.min))
            for n, m in ((3, last), (4, first)):
                c.link(v.scalar_tensor_tensor(cv[:, n, :], cv[:, 1, :], -float(SKIP), m[:], ALU.add, ALU.mult))
                c.link(v.tensor_scalar(cv[:, n, :], cv[:, n, :], float(SKIP), None, ALU.add))
            v.sem_inc(S("tomake"), 1)
            for m in range(6):
                v.wait_ge(S("rowps"), m + 1)
                to = idx[:, m, GT:GT + NT] if m < 4 else (lastR if m == 4 else invR)[:, :]
                to = to.rearrange("p (q r) -> p r q", r=2)
                v.tensor_copy(to, bank[m % 2][:, 0:2 * P].rearrange("p (r q) -> p r q", r=2)[:, :, 0:NQ]) \
                    .then_inc(S("torow"), 1)
            v.wait_ge(S("torow"), 6)

        def prep_scalar(a):
            a.wait_ge(S("b1min"), 1)
            nc.scalar.activation(b1c[:, 3:4], b1c[:, 1:2], ACT.Exp).then_inc(S("b1exp"), 1)

        LOADS = 25

        def index_columns(v, name, kinds, gathered, per, i, j, rev=False):
            s = (j + 2) % RING
            uses = i if j < 2 else i + 1
            if not (isinstance(uses, int) and uses == 0):
                wait(v, f"{gathered}{s}", uses * per)
                pause(v)
            g = RING * i + j + 2
            if rev:
                g = NG - 1 - g
            for n, kind in enumerate(kinds):
                v.tensor_copy(ixr[:, s, n, :], idx[:, kind, four(g + 1)]).then_inc(S(name), 1)

        def index_first(v, name, kinds, rev=False):
            for s in range(2):
                g = NG - 1 - s if rev else s
                for n, kind in enumerate(kinds):
                    v.tensor_copy(ixr[:, s, n, :], idx[:, kind, four(g + 1)]).then_inc(S(name), 1)

        def indices(eng, name, kinds, i, j):
            wait(eng, name, (RING * i + j + 1) * kinds)

        def gather(pool, to, table, s, n, done):
            for c in range(GT):
                nc.gpsimd.indirect_dma_start(
                    to(c), None, table, bass.IndirectOffsetOnAxis(ap=ixr[:, s, n, c:c + 1].bitcast(U32), axis=0)
                ).then_inc(done, 16)

        def scatter(pool, frm, table, s, n, done):
            for c in range(GT):
                nc.gpsimd.indirect_dma_start(
                    table, bass.IndirectOffsetOnAxis(ap=ixr[:, s, n, c:c + 1].bitcast(U32), axis=0), frm(c), None,
                    bounds_check=N - 1, oob_is_err=False).then_inc(done, 16)

        def norm_stats(v, c, tag, i, j, zt, to):
            for k in range(GT):
                c.do(v.bn_stats(stats[:, k, :], zt[:, k, :]))
            c.hold()
            pause(v)
            for k in range(GT):
                c.do(v.bn_aggr(mv[:, 0, k, :], stats[:, k, :]))
            c.hold()
            v.sem_inc(S(tag + "_var"), 1)
            count(v, tag + "_sd", i, j)
            c.link(v.reciprocal(to[:, :, 0], sd[:, 0:GT]))
            return v.scalar_tensor_tensor(to[:, :, 1], mv[:, 0, 0:GT, 0], -1.0, to[:, :, 0], ALU.mult, ALU.mult)

        def norm_sqrt(a, tag, i, j):
            count(a, tag + "_var", i, j)
            nc.scalar.activation(sd[:, 0:GT], mv[:, 0, 0:GT, 1], ACT.Sqrt, bias=epsc[:]).then_inc(S(tag + "_sd"), 1)

        def norm_apply(frm, to, sc):
            for k in range(GT):
                ins = nc.scalar.activation(to[:, k, :], frm[:, k, :], ACT.Identity,
                                           bias=sc[:, k, 1:2], scale=sc[:, k, 0:1])
            return ins

        Q = slice(0, NQ)

        def softmax_tensor(pe, turn, nh, lg, work, spread):
            ee, fs, bs_ = work[3], work[4], work[5]
            fm, bm_ = work[1], work[2]
            if spread is not None:
                kind = spread[0]
                link = linkf if kind is first else linkb
                at = slice(CH - 1, CH) if kind is first else slice(0, 1)
                for r in range(2):
                    ins = nc.tensor.transpose(bank[2][Q, r * P:(r + 1) * P],
                                              own[:, :].rearrange("p (q r) -> p r q", r=2)[:, r, :], ident[:])
                ins.then_inc(S("sm_own"), 1)
                pe.wait_ge(S("sm_ownscan"), turn)
                nc.tensor.matmul(bank[3][Q, 0:1], link[Q, :], work[6][Q, 0, at],
                                 start=True, stop=True).then_inc(S("sm_owncarry"), 1)
            for r in range(2):
                for h in range(nh):
                    ins = nc.tensor.transpose(bank[r][Q, h * P:(h + 1) * P],
                                              lg.rearrange("p (q r) h -> p r h q", r=2)[:, r, h, :], ident[:])
            ins.then_inc(S("sm_lg"), 1)
            pe.wait_ge(S("sm_max"), turn + 1)
            for h in range(nh):
                nc.tensor.transpose(bank[4][Q, h * NQ:(h + 1) * NQ], fm[Q, h, CH - 1:CH].to_broadcast([NQ, NQ]),
                                    ident[Q, 0:NQ])
                ins = nc.tensor.transpose(bank[5][Q, h * NQ:(h + 1) * NQ], bm_[Q, h, 0:1].to_broadcast([NQ, NQ]),
                                          ident[Q, 0:NQ])
            ins.then_inc(S("sm_maxrow"), 1)
            pe.wait_ge(S("sm_sum"), turn + 1)
            nc.tensor.matmul(bank[6][Q, 0:nh], linkf[Q, :], fs[Q, :, CH - 1], start=True, stop=True)
            nc.tensor.matmul(bank[6][Q, nh:2 * nh], linkb[Q, :], bs_[Q, :, 0], start=True, stop=True) \
                .then_inc(S("sm_sumcarry"), 1)
            pe.wait_ge(S("sm_alpha"), turn + 1)
            for r in range(2):
                for h in range(nh):
                    ins = nc.tensor.transpose(bank[r][:, h * NQ:(h + 1) * NQ], ee[Q, h, r * P:(r + 1) * P],
                                              ident[Q, 0:NQ])
            ins.then_inc(S("sm_back"), 1)

        def softmax_vector(v, turn, nh, work, spread, guard, to):
            c = Chain(v, f"sm{turn}_dve")
            lg, fm, bm_, ee, fs, bs_, tot = (work[n] for n in range(7))

            def flat(t):
                return t[Q].rearrange("p h c -> p (h c)")

            def scans(to, keep, frm, ini, op0, op1, rev):
                for h in range(nh):
                    o, d0, d1 = to[Q, h, :], keep[Q, :], frm[Q, h, :]
                    if rev:
                        o, d0, d1 = back(o), back(d0), back(d1)
                    c.do(v.tensor_tensor_scan(o, d0, d1, ini, op0, op1))

            def back(ap):
                return ap[:, ::-1]

            if spread is not None:
                kind = spread[0]
                keep, edge = (keepf, head) if kind is first else (keepb, tail)
                v.wait_ge(S("sm_own"), turn)
                c.link(v.tensor_tensor(work[7][Q, 0, :], bank[2][Q, 0:CH], kind[Q, :], ALU.mult))
                d0, d1, o = keep[Q, :], work[7][Q, 0, :], work[6][Q, 0, :]
                if kind is last:
                    d0, d1, o = back(d0), back(d1), back(o)
                c.link(v.tensor_tensor_scan(o, d0, d1, 0.0, ALU.mult, ALU.add))
                v.sem_inc(S("sm_ownscan"), 1)
                v.wait_ge(S("sm_owncarry"), turn)
                c.link(v.tensor_copy(carry[Q, 3, 0:1], bank[3][Q, 0:1]))
                c.link(v.scalar_tensor_tensor(work[7][Q, 0, :], edge[Q, :], carry[Q, 3, 0:1], work[6][Q, 0, :],
                                              ALU.mult, ALU.add))
            v.wait_ge(S("sm_lg"), turn + 1)
            for r in range(2):
                o = lg[Q, :, r * P:(r + 1) * P]
                i_ = bank[r][Q, 0:nh * P].rearrange("p (h c) -> p h c", h=nh)
                if spread is not None:
                    c.do(v.tensor_tensor(o, i_, work[7][Q, :, r * P:(r + 1) * P], ALU.add))
                else:
                    c.do(v.tensor_copy(o, i_))
            c.hold()
            c.link(v.scalar_tensor_tensor(flat(lg), flat(lg), SLOPE, flat(lg), ALU.mult, ALU.max))
            scans(fm, penf, lg, -BIG, ALU.add, ALU.max, False)
            scans(bm_, penb, lg, -BIG, ALU.add, ALU.max, True)
            c.hold()
            v.sem_inc(S("sm_max"), 1)
            v.wait_ge(S("sm_maxrow"), turn + 1)
            for n, pen, b in ((0, linkbp, 4), (1, linkfp, 5)):
                for h in range(nh):
                    c.do(v.tensor_tensor(tot[Q, h, 0:NQ] if n == 0 else tot[Q, h, P:P + NQ],
                                         bank[b][Q, h * NQ:(h + 1) * NQ], pen[Q, :], ALU.add))
            c.hold()
            for n in range(2):
                c.do(v.tensor_reduce(carry[Q, n, 0:nh], tot[Q, :, n * P:n * P + NQ], X, ALU.max))
            c.link(v.tensor_tensor(flat(fm), flat(fm), flat(bm_), ALU.max))
            for n, edge in ((0, headp), (1, tailp)):
                for h in range(nh):
                    c.do(v.scalar_tensor_tensor(fm[Q, h, :], edge[Q, :], carry[Q, n, h:h + 1], fm[Q, h, :],
                                                ALU.add, ALU.max))
                c.hold()
            c.link(v.tensor_tensor(flat(lg), flat(lg), flat(fm), ALU.subtract))
            v.sem_inc(S("sm_centred"), 1)
            v.wait_ge(S("sm_exp"), turn + 1)
            scans(fs, keepf, ee, 0.0, ALU.mult, ALU.add, False)
            scans(bs_, keepb, ee, 0.0, ALU.mult, ALU.add, True)
            c.hold()
            v.sem_inc(S("sm_sum"), 1)
            c.link(v.tensor_tensor(flat(tot), flat(fs), flat(ee), ALU.subtract))
            c.link(v.tensor_tensor(flat(tot), flat(tot), flat(bs_), ALU.add))
            v.wait_ge(S("sm_sumcarry"), turn + 1)
            c.link(v.tensor_copy(carry[Q, 2, 0:nh], bank[6][Q, 0:nh]))
            c.link(v.tensor_copy(carry[Q, 3, 0:nh], bank[6][Q, nh:2 * nh]))
            for n, edge in ((2, head), (3, tail)):
                for h in range(nh):
                    c.do(v.scalar_tensor_tensor(tot[Q, h, :], edge[Q, :], carry[Q, n, h:h + 1], tot[Q, h, :],
                                                ALU.mult, ALU.add))
                c.hold()
            if guard:
                c.link(v.tensor_scalar(flat(tot), flat(tot), guard, None, ALU.add))
            c.link(v.reciprocal(flat(fs), flat(tot)))
            c.link(v.tensor_tensor(flat(ee), flat(ee), flat(fs), ALU.mult))
            v.sem_inc(S("sm_alpha"), 1)
            v.wait_ge(S("sm_back"), turn + 1)
            for r in range(2):
                c.do(v.tensor_copy(to.rearrange("p (q r) h -> p r h q", r=2)[:, r, :, :],
                                   bank[r][:, 0:nh * NQ].rearrange("p (h q) -> p h q", h=nh)))
            c.hold()

        def softmax_scalar(a, turn, nh, work):
            a.wait_ge(S("sm_centred"), turn + 1)
            nc.scalar.activation(work[3][Q].rearrange("p h c -> p (h c)"), work[0][Q].rearrange("p h c -> p (h c)"),
                                 ACT.Exp).then_inc(S("sm_exp"), 1)

        xmain = x[0:NJ * P, :].rearrange("(p j) f -> p j f", p=P)
        mains = [t[0:NJ * P, :].rearrange("(p j) f -> p j f", p=P) for t in (x1_t, x3_t, out)]

        def is_last(i):
            return isinstance(i, int) and i == BODIES

        def dense_k(i):
            return DLAST + 1 if is_last(i) else DK

        def before_of(i, j):
            return (i, j - 1) if j else (i - 1, RING - 1)

        def a_pool(pool):
            def step(i, j):
                count(pool, "a_tr", i, j, RING)
                slot_done(pool, "a_out", i, j, 16, 1)
                indices(pool, "a_ix", 2, i, j)
                pause(pool)
                gather(pool, lambda c: ring[:, j, 0, c, :], x, j, 0, S(f"a_in{j}"))
                gather(pool, lambda c: ring[:, j, 1, c, :], x, j, 1, S(f"a_in{j}"))
            groups(pool, step)

        def a_sync(sp):
            def load(i, j):
                s = j % 2
                count(sp, "n_u1", i, j, 2)
                count(sp, "n_tr", i, j, 2)
                if not is_last(i):
                    sp.dma_start(xin[s][:, :, :], xmain[:, bass.ds((RING * i + j) * DK, DK), :]) \
                        .then_inc(S(f"n_in{s}"), 32)
                else:
                    sp.dma_start(xin[s][:, 0:DLAST, :], xmain[:, NJ - DLAST:NJ, :]).then_inc(S(f"n_in{s}"), 16)
                    sp.dma_start(xin[s][0:NTAIL, DLAST, :], x[NJ * P:N, :]).then_inc(S(f"n_in{s}"), 16)

            def stores(i, j):
                wait(sp, f"a_in{j}", (i + 1) * 2 * GT * 16)
                sp.dma_start(xd_e[bass.ds(RING * i + j, 1)].rearrange("a p f -> (a p) f"), ringf[:, j, 1, :]) \
                    .then_inc(S(f"a_out{j}"), 16)
                for n in range(3):
                    count(sp, f"n_y{n}", i, j)
                    if not is_last(i):
                        sp.dma_start(mains[n][:, bass.ds((RING * i + j) * DK, DK), :], y[n][:, :, :]) \
                            .then_inc(S(f"n_out{n}"), 32)
                    else:
                        t = (x1_t, x3_t, out)[n]
                        sp.dma_start(mains[n][:, NJ - DLAST:NJ, :], y[n][:, 0:DLAST, :]).then_inc(S(f"n_out{n}"), 16)
                        sp.dma_start(t[NJ * P:N, :], y[n][0:NTAIL, DLAST, :]).then_inc(S(f"n_out{n}"), 16)

            load(0, 0)

            def step(i, j):
                if not is_last(i):
                    load(i, j + 1) if j + 1 < RING else load(i + 1, 0)
                stores(i, j)

            def whole():
                for j in range(RING):
                    step(0, j)
                with sp.Fori(1, BODIES - 1) as i:
                    for j in range(RING):
                        step(i, j)
                for j in range(RING):
                    step(BODIES - 1, j)
                step(BODIES, 0)
            whole()
            for j in range(RING):
                wait(sp, f"a_out{j}", 16 * (BODIES + (j == 0)))
            for n in range(3):
                wait(sp, f"n_out{n}", 32 * NG)

        def a_tensor(pe):
            def step(i, j):
                s = j % 2
                K = dense_k(i)
                wait(pe, f"n_in{s}", 32 * (2 * i + j // 2 + 1))
                count(pe, "n_xT", i, j, 1)
                for k in range(K):
                    ins = nc.tensor.transpose(bank[k // 4][:, (k % 4) * P:(k % 4 + 1) * P], xin[s][:, k, :], ident[:])
                ins.then_inc(S("n_tr"), 1)
                wait(pe, f"a_in{j}", (i + 1) * 2 * GT * 16)
                count(pe, "a_xT", i, j, 1)
                for n in range(2):
                    for c in range(GT):
                        ins = nc.tensor.transpose(bank[2 + n][:, c * P:(c + 1) * P], ring[:, j, n, c, :], ident[:])
                ins.then_inc(S("a_tr"), 1)
                count(pe, "n_xT", i, j)
                count(pe, "n_dots", i, j, 2)
                for k in range(K):
                    ins = nc.tensor.matmul(bank[4 + s][:, 4 * k:4 * k + 4], dxT[:, k * P:(k + 1) * P], bT[:],
                                           start=True, stop=True)
                ins.then_inc(S("n_mm"), 1)
                count(pe, "a_xT", i, j)
                count(pe, "a_feat", i, j, 2)
                for c in range(GT):
                    o = bank[6 + s][:, c * FW:(c + 1) * FW]
                    nc.tensor.matmul(o[:, 0:HF], xT[:, s, 0, c * P:(c + 1) * P], W1x[:, 0:HF], start=True, stop=True)
                    nc.tensor.matmul(o[:, HF:FW], xT[:, s, 0, c * P:(c + 1) * P], W1x[:, HF:FW],
                                     start=True, stop=False)
                    ins = nc.tensor.matmul(o[:, HF:FW], xT[:, s, 1, c * P:(c + 1) * P], W1r[:], start=False, stop=True)
                ins.then_inc(S("a_mm"), 1)
            groups(pe, step)

        def a_scalar(a):
            def evac(i, j):
                s = j % 2
                K = dense_k(i)
                count(a, "n_tr", i, j)
                count(a, "n_mm", i, j, 1)
                for b in range(2):
                    n = min(K - 4 * b, 4) * P
                    ins = nc.scalar.activation(dxT[:, b * 4 * P:b * 4 * P + n], bank[b][:, 0:n], ACT.Copy)
                ins.then_inc(S("n_xT"), 1)
                count(a, "a_tr", i, j)
                count(a, "a_mm", i, j, 2)
                for n in range(2):
                    ins = nc.scalar.activation(xT[:, s, n, :], bank[2 + n][:], ACT.Copy)
                ins.then_inc(S("a_xT"), 1)

            def apply(i, j):
                s = j % 2
                K = dense_k(i)
                for n, l in ((0, 0), (1, 2), (2, 3)):
                    count(a, f"n_u{l + 1}", i, j)
                    if not (isinstance(i, int) and i == 0 and j == 0):
                        wait(a, f"n_out{n}", 32 * (RING * i + j))
                    for k in range(K):
                        ins = nc.scalar.activation(y[n][:, k, :], u[l][:, k, :], ACT.Copy,
                                                   scale=rho[:, s, l, k:k + 1])
                    ins.then_inc(S(f"n_y{n}"), 1)

            def feats(i, j):
                s = j % 2
                count(a, "a_mm", i, j)
                pause(a)
                nc.scalar.activation(feat[:, four(RING * i + j), :],
                                     bank[6 + s][:, 0:GT * FW].rearrange("p (c f) -> p c f", f=FW), ACT.Copy) \
                    .then_inc(S("a_feat"), 1)

            def step(i, j):
                evac(i, j)
                if not (isinstance(i, int) and i == 0 and j == 0):
                    apply(*before_of(i, j))
                feats(i, j)
                for l in range(4):
                    wait(a, "n_var", (RING * i + j) * 4 + l + 1)
                    nc.scalar.activation(small[:, 9, :], small[:, 2, :], ACT.Sqrt, bias=epsc[:]) \
                        .then_inc(S("n_sd"), 1)
            groups(a, step)
            apply(BODIES, 0)

        def a_vector(v):
            c = Chain(v, "a_dve")
            index_first(v, "a_ix", (SRC, DST))

            def step(i, j):
                s = j % 2
                K = dense_k(i)
                c.at(i, j)
                if not is_last(i):
                    index_columns(v, "a_ix", (SRC, DST), "a_in", 2 * GT * 16, i, j)
                wait(v, f"n_in{s}", 32 * (2 * i + j // 2 + 1))
                xb = xin[s]
                for k in range(DK):
                    c.do(v.bn_stats(stats[:, k, :], xb[:, k, :]))
                c.hold()
                pause(v)
                for k in range(DK):
                    c.do(v.bn_aggr(mv[:, 1, k, :], stats[:, k, :]))
                c.hold()
                m_, var = mv[:, 1, :, 0], mv[:, 1, :, 1]
                count(v, "n_mm", i, j)
                if is_last(i):
                    K4 = K
                else:
                    K4 = DK
                c.link(v.tensor_scalar(small[:, 0, :], m_, -1.0, None, ALU.mult))
                v.tensor_copy(dots[:, 0:K4, :], bank[4 + s][:, 0:4 * K4].rearrange("p (k n) -> p k n", n=4)) \
                    .then_inc(S("n_dots"), 1)
                count(v, "n_dots", i, j)
                count(v, "n_y2", i, j, 2)
                w, rr = var, rho[:, s]
                for l in range(4):
                    B = [BB[:, 4 * l + n:4 * l + n + 1] for n in range(4)]
                    cl = dots[:, :, l]
                    c.link(v.scalar_tensor_tensor(small[:, 1, :], cl, 2.0, w, ALU.mult, ALU.add))
                    v.tensor_scalar(small[:, 2, :], small[:, 1, :], B[l], None, ALU.add).then_inc(S("n_var"), 1)
                    wait(v, "n_sd", (RING * i + j) * 4 + l + 1)
                    c.link(v.reciprocal(small[:, 3, :], small[:, 9, :]))
                    r = small[:, 3, :]
                    if l == 0:
                        c.do(v.tensor_copy(rr[:, 0, :], r))
                    else:
                        c.do(v.tensor_tensor(rr[:, l, :], rr[:, l - 1, :], r, ALU.mult))
                    for n in range(l + 1, 4):
                        c.do(v.scalar_tensor_tensor(dots[:, :, n], dots[:, :, n], B[n], r, ALU.add, ALU.mult))
                    c.do(v.tensor_tensor(small[:, 4, :], r, r, ALU.mult))
                    c.hold()
                    c.link(v.tensor_tensor(small[:, 5, :], small[:, 2, :], small[:, 4, :], ALU.mult))
                    w = small[:, 5, :]
                    if l < 3:
                        c.link(v.reciprocal(small[:, 6 + l, :], rr[:, l, :]))
                if not (isinstance(i, int) and i == 0 and j == 0):
                    count(v, "n_y2", i, j, 1)
                for l in range(4):
                    for k in range(DK):
                        if l == 0:
                            ins = v.scalar_tensor_tensor(u[0][:, k, :], xb[:, k, :], small[:, 0, k:k + 1],
                                                         biasc[:, 0, :], ALU.add, ALU.add)
                        else:
                            ins = v.scalar_tensor_tensor(u[l][:, k, :], biasc[:, l, :], small[:, 5 + l, k:k + 1],
                                                         u[l - 1][:, k, :], ALU.mult, ALU.add)
                    ins.then_inc(S(f"n_u{l + 1}"), 1)
                    if l < 3:
                        count(v, f"n_u{l + 1}", i, j)
            groups(v, step)

        def weigh(v, i, j, frm, width, heads, rev=False):
            s = j % 2
            g = RING * i + j
            if rev:
                g = NG - 1 - g
            if frm is None:
                slot_done(v, "h_xs", i, j, 16)
                pause(v)
                rowsv = ring[:, j, 0, :, 0:width]
            else:
                rowsv = frm[:, four(g), 0:width]
            o = msg[:, s, :, 0:width]
            if heads > 1:
                d = width // heads
                return v.tensor_tensor(o.rearrange("p t (h d) -> p t h d", h=heads),
                                       rowsv.rearrange("p t (h d) -> p t h d", h=heads),
                                       alpha[:, four(g), 0:heads].unsqueeze(3).to_broadcast([P, GT, heads, d]),
                                       ALU.mult)
            return v.tensor_tensor(o, rowsv, alpha[:, four(g), 0:1].to_broadcast([P, GT, width]), ALU.mult)

        def next_of(i, j):
            return (i, j + 1) if j + 1 < RING else (i + 1, 0)

        def scan_sum(v, tag, i, j, width, src_ap, dst_t, rev=False, op=None, c=None):
            s = j % 2
            g = RING * i + j
            m = cont[0:width, bass.ds(g * GE, GE)]
            o = dst_t[0:width, s, :]
            start = isinstance(i, int) and i == 0 and j == 0
            ini = 0.0 if start else (dst_t[0:width, 1 - s, 0:1] if rev else dst_t[0:width, 1 - s, GE - 1:GE])
            if rev:
                o, src_ap = o[:, ::-1], src_ap[:, ::-1]
            return v.tensor_tensor_scan(o, m, src_ap, ini, ALU.mult, ALU.add)

        def b_vector(v):
            c = Chain(v, "b_dve")
            index_first(v, "b_ix", (LAST,))
            weigh(v, 0, 0, feat, HF, HEADS).then_inc(S("b_msg"), 1)

            def step(i, j):
                s = j % 2
                c.at(i, j)
                if not is_last(i):
                    index_columns(v, "b_ix", (LAST,), "b_sc", GT * 16, i, j)
                    ni, nj = next_of(i, j)
                    count(v, "b_tr", ni, nj, 2)
                    pause(v)
                    weigh(v, ni, nj, feat, HF, HEADS).then_inc(S("b_msg"), 1)
                count(v, "b_tr", i, j)
                if not (isinstance(i, int) and i == 0 and j == 0):
                    count(v, "b_scan", i, j, 1)
                scan_sum(v, "b", i, j, HF, bank[s][0:HF, :], G).then_inc(S("b_scan"), 1)
                count(v, "b_scan", i, j)
                count(v, "b_mm", i, j, 2)
                c.do(v.tensor_scalar(hT[0:HF, s, 0, :], G[0:HF, s, :], b1c[:, 0:1], 0.0, ALU.add, ALU.max))
                v.tensor_scalar(hT[0:HF, s, 1, :], G[0:HF, s, :], b1c[:, 0:1], 0.0, ALU.add, ALU.min) \
                    .then_inc(S("b_min"), 1)
                count(v, "b_exp", i, j)
                c.hold()
                v.scalar_tensor_tensor(hT[0:HF, s, 2, :], hT[0:HF, s, 1, :], -1.0, hT[0:HF, s, 0, :],
                                       ALU.add, ALU.add).then_inc(S("b_h"), 1)
            groups(v, step)

        def b_tensor(pe):
            def step(i, j):
                s = j % 2
                count(pe, "b_msg", i, j)
                count(pe, "b_scan", i, j, 2)
                pause(pe)
                for c in range(GT):
                    ins = nc.tensor.transpose(bank[s][0:HF, c * P:(c + 1) * P], msg[:, s, c, 0:HF], ident[:])
                ins.then_inc(S("b_tr"), 1)
                count(pe, "b_h", i, j)
                count(pe, "b_er", i, j, 2)
                for c in range(GT):
                    ins = nc.tensor.matmul(bank[2 + s][:, c * (HF + 2):(c + 1) * (HF + 2)],
                                           hT[0:HF, s, 2, c * P:(c + 1) * P], W2x[:], start=True, stop=True)
                ins.then_inc(S("b_mm"), 1)
            groups(pe, step)

        def b_scalar(a):
            def step(i, j):
                s = j % 2
                count(a, "b_min", i, j)
                nc.scalar.activation(hT[0:HF, s, 1, :], hT[0:HF, s, 1, :], ACT.Exp).then_inc(S("b_exp"), 1)
                count(a, "b_mm", i, j)
                slot_done(a, "b_sc", i, j, GT * 16, 1)
                ps = bank[2 + s][:, 0:GT * (HF + 2)].rearrange("p (c f) -> p c f", f=HF + 2)
                nc.scalar.activation(outr[:, j, :, 0:HW], ps[:, :, 0:HW], ACT.Copy).then_inc(S("b_row"), 1)
                nc.scalar.activation(own[:, four(RING * i + j)], ps[:, :, HW], ACT.Copy).then_inc(S("b_er"), 1)
            groups(a, step)

        def b_pool(pool):
            def step(i, j):
                count(pool, "b_row", i, j)
                indices(pool, "b_ix", 1, i, j)
                pause(pool)
                scatter(pool, lambda c: outr[:, j, c, 0:HW], hidden_t, j, 0, S(f"b_sc{j}"))
            groups(pool, step)
            for j in range(RING):
                wait(pool, f"b_sc{j}", GT * 16 * (BODIES + (j == 0)))

        def c_pool(pool):
            def step(i, j):
                count(pool, "c_copy", i, j, RING)
                indices(pool, "c_ix", 1, i, j)
                pause(pool)
                gather(pool, lambda c: ring[:, j, 0, c, 0:HW], hidden_t, j, 0, S(f"c_in{j}"))
            groups(pool, step)

        def c_vector(v):
            index_first(v, "c_ix", (SRC,))

            def step(i, j):
                if not is_last(i):
                    index_columns(v, "c_ix", (SRC,), "c_in", GT * 16, i, j)
            groups(v, step)

        def c_scalar(a):
            def step(i, j):
                slot_done(a, "c_in", i, j, GT * 16)
                pause(a)
                nc.scalar.activation(feat[:, four(RING * i + j), 0:HF], ring[:, j, 0, :, 0:HF], ACT.Copy)
                nc.scalar.activation(logit[:, four(RING * i + j), 0], ring[:, j, 0, :, HF], ACT.Copy) \
                    .then_inc(S("c_copy"), 1)
            groups(a, step)

        def attend_vector(v, tag, frm, width, kind, rev):
            c = Chain(v, tag + "_dve")
            index_first(v, tag + "_ix", (kind,), rev)
            weigh(v, 0, 0, frm, width, 1, rev).then_inc(S(tag + "_msg"), 1)

            def step(i, j):
                s = j % 2
                c.at(i, j)
                if not is_last(i):
                    index_columns(v, tag + "_ix", (kind,), tag + "_sc", GT * 16, i, j, rev)
                    ni, nj = next_of(i, j)
                    count(v, tag + "_tr", ni, nj, 2)
                    pause(v)
                    weigh(v, ni, nj, frm, width, 1, rev).then_inc(S(tag + "_msg"), 1)
                count(v, tag + "_tr", i, j)
                if not (isinstance(i, int) and i == 0 and j == 0):
                    count(v, tag + "_scan", i, j, 1)
                count(v, tag + "_mm", i, j, 2)
                scan_sum(v, tag, i, j, width, bank[s][0:width, :], G, rev).then_inc(S(tag + "_scan"), 1)
                count(v, tag + "_mm", i, j)
                wait(v, f"{tag}_ld{s}", 16 * (2 * i + j // 2 + 1))
                count(v, tag + "_row", i, j, 2)
                v.tensor_tensor(z[:, s], bank[2 + s][:].rearrange("p (t f) -> p t f", f=F), xload[:, s], ALU.add) \
                    .then_inc(S(tag + "_z"), 1)
                count(v, tag + "_z", i, j)
                norm_stats(v, c, tag, i, j, z[:, s], rn[:, s]).then_inc(S(tag + "_st"), 1)
            groups(v, step)

        def attend_tensor(pe, tag, width, W, b):
            def step(i, j):
                s = j % 2
                count(pe, tag + "_msg", i, j)
                count(pe, tag + "_scan", i, j, 2)
                pause(pe)
                for c in range(GT):
                    ins = nc.tensor.transpose(bank[s][0:width, c * P:(c + 1) * P], msg[:, s, c, 0:width], ident[:])
                ins.then_inc(S(tag + "_tr"), 1)
                count(pe, tag + "_scan", i, j)
                count(pe, tag + "_z", i, j, 2)
                for c in range(GT):
                    o = bank[2 + s][:, c * F:(c + 1) * F]
                    nc.tensor.matmul(o, G[0:width, s, c * P:(c + 1) * P], W[:], start=True, stop=False)
                    ins = nc.tensor.matmul(o, ones[0:1, 0:P], brow[0:1, b, :], start=False, stop=True)
                ins.then_inc(S(tag + "_mm"), 1)
            groups(pe, step)

        def attend_scalar(a, tag, stored):
            def step(i, j):
                s = j % 2
                norm_sqrt(a, tag, i, j)
                count(a, tag + "_st", i, j)
                slot_done(a, tag + "_sc", i, j, GT * 16, 1)
                if stored:
                    slot_done(a, tag + "_out", i, j, 16, 1)
                norm_apply(z[:, s], outr[:, j], rn[:, s]).then_inc(S(tag + "_row"), 1)
            groups(a, step)

        def attend_pool(pool, tag, table):
            def step(i, j):
                count(pool, tag + "_row", i, j)
                indices(pool, tag + "_ix", 1, i, j)
                pause(pool)
                scatter(pool, lambda c: outr[:, j, c, :], table, j, 0, S(f"{tag}_sc{j}"))
            groups(pool, step)
            for j in range(RING):
                wait(pool, f"{tag}_sc{j}", GT * 16 * (BODIES + (j == 0)))

        def edge_row(t, g):
            return t[bass.ds(g, 1)].rearrange("a p f -> (a p) f")

        def linear_sync(sp, tag, table, to, rev, used, more=None):
            def load(i, j):
                s = j % 2
                g = RING * i + j
                count(sp, tag + used, i, j, 2)
                sp.dma_start(xloadf[:, s, :], edge_row(table, NG - 1 - g if rev else g)) \
                    .then_inc(S(f"{tag}_ld{s}"), 16)
                if more is not None:
                    count(sp, tag + "_msg", i, j, RING)
                    sp.dma_start(ringf[:, j, 0, :], edge_row(more, NG - 1 - g if rev else g)) \
                        .then_inc(S(f"{tag}_xs{j}"), 16)

            def store(i, j):
                g = RING * i + j
                count(sp, tag + "_row", i, j)
                sp.dma_start(edge_row(to, NG - 1 - g if rev else g), outf[:, j, :]).then_inc(S(f"{tag}_out{j}"), 16)
            load(0, 0)

            def step(i, j):
                if not is_last(i):
                    load(*next_of(i, j))
                if to is not None:
                    store(i, j)
            groups(sp, step)
            if to is not None:
                for j in range(RING):
                    wait(sp, f"{tag}_out{j}", 16 * (BODIES + (j == 0)))

        def e_pool(pool):
            def step(i, j):
                count(pool, "e_tr", i, j, RING)
                indices(pool, "e_ix", 1, i, j)
                pause(pool)
                gather(pool, lambda c: ring[:, j, 0, c, :], x1_t, j, 0, S(f"e_in{j}"))
            groups(pool, step)

        def e_tensor(pe):
            def step(i, j):
                s = j % 2
                slot_done(pe, "e_in", i, j, GT * 16)
                count(pe, "e_scan", i, j, 2)
                for c in range(GT):
                    ins = nc.tensor.transpose(bank[s][:, c * P:(c + 1) * P], ring[:, j, 0, c, :], ident[:])
                ins.then_inc(S("e_tr"), 1)
                count(pe, "e_scan", i, j)
                count(pe, "e_z", i, j, 2)
                for c in range(GT):
                    ins = nc.tensor.matmul(bank[2 + s][:, c * F:(c + 1) * F], G[:, s, c * P:(c + 1) * P], L1T[:],
                                           start=True, stop=True)
                ins.then_inc(S("e_mm"), 1)
            groups(pe, step)

        def e_vector(v):
            c = Chain(v, "e_dve")
            index_first(v, "e_ix", (SRC,))

            def step(i, j):
                s = j % 2
                g = RING * i + j
                c.at(i, j)
                if not is_last(i):
                    index_columns(v, "e_ix", (SRC,), "e_in", GT * 16, i, j)
                count(v, "e_tr", i, j)
                if not (isinstance(i, int) and i == 0 and j == 0):
                    count(v, "e_scan", i, j, 1)
                count(v, "e_mm", i, j, 2)
                scan_sum(v, "e", i, j, P, bank[s][:, :], G).then_inc(S("e_scan"), 1)
                count(v, "e_mm", i, j)
                wait(v, f"e_ld{s}", 16 * (2 * i + j // 2 + 1))
                count(v, "e_row", i, j, 2)
                for k in range(GT):
                    c.do(v.scalar_tensor_tensor(z[:, s, k, :], bank[2 + s][:, k * F:(k + 1) * F],
                                                invR[:, bass.ds(g * GT + k, 1)], xload[:, s, k, :],
                                                ALU.mult, ALU.add))
                c.hold()
                v.tensor_tensor(z[:, s], z[:, s], bias[:, 1:2, :].to_broadcast([P, GT, F]), ALU.add) \
                    .then_inc(S("e_z"), 1)
                count(v, "e_z", i, j)
                c.link(norm_stats(v, c, "e", i, j, z[:, s], rn[:, s]))
                v.tensor_tensor(rn[:, s], rn[:, s], lastR[:, four(g)].unsqueeze(2).to_broadcast([P, GT, 2]),
                                ALU.mult).then_inc(S("e_st"), 1)
            groups(v, step)

        def e_scalar(a):
            def step(i, j):
                s = j % 2
                norm_sqrt(a, "e", i, j)
                count(a, "e_st", i, j)
                slot_done(a, "e_out", i, j, 16, 1)
                norm_apply(z[:, s], outr[:, j], rn[:, s]).then_inc(S("e_row"), 1)
            groups(a, step)

        eaR = ring[:, 0:2, 1, :, 0:EF]

        def f_sync(sp):
            sp.dma_start(cont[:].rearrange("p (q c) -> p q c", c=CH),
                         cont_d[1, :].rearrange("(q c) -> q c", c=CH)[::-1, :].partition_broadcast(P)) \
                .then_inc(S("cont_in"), 16)
            def load(i, j):
                s = j % 2
                g = NG - 1 - (RING * i + j)
                count(sp, "f_tr", i, j, 2)
                sp.dma_start(ring[:, s, 0].rearrange("p t f -> p (t f)"), edge_row(x2_e, g)) \
                    .then_inc(S(f"f_x{s}"), 16)
                if isinstance(i, int) and i == 0 and j == 0:
                    full = (E - (NG - 1) * GE) // P
                    base = (NG - 1) * GE
                    wait(sp, "f_pad", 1)
                    sp.dma_start(eaR[:, s, 0:full, :], ea[base:base + full * P, :].rearrange("(c p) f -> p c f", p=P)) \
                        .then_inc(S(f"f_ea{s}"), 16)
                    sp.dma_start(eaR[0:E - base - full * P, s, full, :], ea[base + full * P:E, :]) \
                        .then_inc(S(f"f_ea{s}"), 16)
                else:
                    sp.dma_start(eaR[:, s], ea[bass.ds(g * GE, GE), :].rearrange("(c p) f -> p c f", p=P)) \
                        .then_inc(S(f"f_ea{s}"), 32)

            def store(i, j):
                g = NG - 1 - (RING * i + j)
                count(sp, "f_row", i, j)
                sp.dma_start(edge_row(x3_e, g), outf[:, j, :]).then_inc(S(f"f_out{j}"), 16)
            load(0, 0)

            def step(i, j):
                if not is_last(i):
                    load(*next_of(i, j))
                store(i, j)
            groups(sp, step)
            for j in range(RING):
                wait(sp, f"f_out{j}", 16 * (BODIES + (j == 0)))

        def f_tensor(pe):
            def step(i, j):
                s = j % 2
                uses = 2 * i + j // 2 + 1
                wait(pe, f"f_x{s}", 16 * uses)
                wait(pe, f"f_ea{s}", 32 * uses)
                count(pe, "f_spread", i, j, 1)
                for c in range(GT):
                    nc.tensor.transpose(bank[0][:, c * P:(c + 1) * P], ring[:, s, 0, c, :], ident[:])
                count(pe, "f_eaT", i, j, 1)
                pause(pe)
                for c in range(GT):
                    ins = nc.tensor.transpose(bank[1][0:EF, c * P:(c + 1) * P], eaR[:, s, c, :], ident[:])
                ins.then_inc(S("f_tr"), 1)
                count(pe, "f_spread", i, j)
                count(pe, "f_eaT", i, j)
                count(pe, "f_relu", i, j, 1)
                nc.tensor.matmul(bank[2][:], M1a[:], X2T[:, s, :], start=True, stop=False)
                nc.tensor.matmul(bank[2][:], M1b[:], eaT[:, s, :], start=False, stop=True).then_inc(S("f_m1"), 1)
                count(pe, "f_relu", i, j)
                count(pe, "f_msg", i, j, 1)
                nc.tensor.matmul(bank[3][:], M2_s[:], hT[:, s, 0, :], start=True, stop=True).then_inc(S("f_m2"), 1)
                count(pe, "f_sum", i, j)
                count(pe, "f_zA", i, j, 2)
                for c in range(GT):
                    ins = nc.tensor.matmul(bank[4 + s][:, c * F:(c + 1) * F], G[:, s, c * P:(c + 1) * P], Mm_s[:],
                                           start=True, stop=True)
                ins.then_inc(S("f_mA"), 1)
                count(pe, "f_max", i, j)
                count(pe, "f_z", i, j, 2)
                for c in range(GT):
                    o = bank[6 + s][:, c * F:(c + 1) * F]
                    at = slice(c * P, (c + 1) * P)
                    nc.tensor.matmul(o, G[:, s, at], Ms_s[:], start=True, stop=False)
                    nc.tensor.matmul(o, MX[:, s, at], Mx_s[:], start=False, stop=False)
                    nc.tensor.matmul(o, X2T[:, s, at], ident[:], start=False, stop=False)
                    ins = nc.tensor.matmul(o, ones[0:1, 0:P], brow[0:1, 1, :], start=False, stop=True)
                ins.then_inc(S("f_mB"), 1)
            groups(pe, step)

        def f_scalar(a):
            def tail_part(i, j):
                s = j % 2
                g = NG - 1 - (RING * i + j)
                count(a, "f_mA", i, j)
                count(a, "f_z", i, j, 2)
                pause(a)
                for c in range(GT):
                    ins = nc.scalar.activation(zA[:, s, c, :], bank[4 + s][:, c * F:(c + 1) * F], ACT.Copy,
                                               scale=invR[:, bass.ds(g * GT + c, 1)])
                ins.then_inc(S("f_zA"), 1)

            def rows_part(i, j):
                s = j % 2
                norm_sqrt(a, "f", i, j)
                count(a, "f_st", i, j)
                slot_done(a, "f_sc", i, j, GT * 16, 1)
                slot_done(a, "f_out", i, j, 16, 1)
                norm_apply(z[:, s], outr[:, j], rn[:, s]).then_inc(S("f_row"), 1)

            def step(i, j):
                s = j % 2
                count(a, "f_tr", i, j)
                count(a, "f_m1", i, j, 2)
                nc.scalar.activation(eaT[:, s, :], bank[1][0:EF, :], ACT.Copy).then_inc(S("f_eaT"), 1)
                count(a, "f_m1", i, j)
                count(a, "f_m2", i, j, 2)
                nc.scalar.activation(hT[:, s, 0, :], bank[2][:], ACT.Relu, bias=m1c[:]).then_inc(S("f_relu"), 1)
                count(a, "f_m2", i, j)
                count(a, "f_max", i, j, 2)
                nc.scalar.activation(hT[:, s, 1, :], bank[3][:], ACT.Identity, bias=m2c[:]).then_inc(S("f_msg"), 1)
                tail_part(i, j)
                rows_part(i, j)
            groups(a, step)

        def f_vector(v):
            c = Chain(v, "f_dve")
            v.memset(eaR[:, 0], 0.0).then_inc(S("f_pad"), 1)
            index_first(v, "f_ix", (FIRST,), True)

            def step(i, j):
                s = j % 2
                start = isinstance(i, int) and i == 0 and j == 0
                g = NG - 1 - (RING * i + j)
                m = cont[:, bass.ds((RING * i + j) * GE, GE)]
                c.at(i, j)
                if not is_last(i):
                    index_columns(v, "f_ix", (FIRST,), "f_sc", GT * 16, i, j, True)
                if start:
                    v.wait_ge(S("cont_in"), 32)
                count(v, "f_tr", i, j)
                if not start:
                    count(v, "f_spread", i, j, 1)
                count(v, "f_mB", i, j, 2)
                scan_sum(v, "f", i, j, P, bank[0][:, :], X2T, True).then_inc(S("f_spread"), 1)
                c.do(v.tensor_scalar(neg[:, s, :], m, -1.0, -FAR, ALU.add, ALU.mult))
                count(v, "f_msg", i, j)
                if not start:
                    count(v, "f_sum", i, j, 1)
                scan_sum(v, "f", i, j, P, hT[:, s, 1, :], G, True).then_inc(S("f_sum"), 1)
                c.hold()
                if not start:
                    count(v, "f_max", i, j, 1)
                ini = FAR if start else MX[:, 1 - s, 0:1]
                v.tensor_tensor_scan(MX[:, s, ::-1], neg[:, s, :], hT[:, s, 1, ::-1], ini, ALU.add, ALU.max) \
                    .then_inc(S("f_max"), 1)
                count(v, "f_mB", i, j)
                count(v, "f_zA", i, j)
                count(v, "f_row", i, j, 2)
                v.tensor_tensor(z[:, s], bank[6 + s][:].rearrange("p (t f) -> p t f", f=F), zA[:, s], ALU.add) \
                    .then_inc(S("f_z"), 1)
                count(v, "f_z", i, j)
                norm_stats(v, c, "f", i, j, z[:, s], rn[:, s]).then_inc(S("f_st"), 1)
            groups(v, step)

        def g_pool(pool):
            def step(i, j):
                slot_done(pool, "g_out", i, j, 16, 1)
                count(pool, "g_dot", i, j, RING)
                indices(pool, "g_ix", 1, i, j)
                pause(pool)
                gather(pool, lambda c: ring[:, j, 0, c, :], x3_t, j, 0, S(f"g_in{j}"))
            groups(pool, step)

        def g_vector(v):
            c = Chain(v, "g_dve")
            index_first(v, "g_ix", (SRC,))

            def step(i, j):
                s = j % 2
                g = RING * i + j
                c.at(i, j)
                if not is_last(i):
                    index_columns(v, "g_ix", (SRC,), "g_in", GT * 16, i, j)
                wait(v, f"g_ld{s}", 16 * (2 * i + j // 2 + 1))
                slot_done(v, "g_in", i, j, GT * 16)
                for n in range(2):
                    for k in range(GT):
                        frm = ring[:, j, 0, k, :] if n else xload[:, s, k, :]
                        c.do(v.tensor_tensor_reduce(msg[:, n, k, :], frm, attb[:, n, :], 1.0, 0.0, ALU.mult, ALU.add,
                                                    dots[:, k, n:n + 1]))
                c.hold()
                pause(v)
                v.tensor_copy(own[:, four(g)], dots[:, 0:GT, 0])
                v.tensor_copy(logit[:, four(g), 0], dots[:, 0:GT, 1]).then_inc(S("g_dot"), 1)
                count(v, "g_dot", i, j)
            groups(v, step)

        def g_sync(sp):
            def load(i, j):
                s = j % 2
                count(sp, "g_dot", i, j, 2)
                sp.dma_start(xloadf[:, s, :], edge_row(x3_e, RING * i + j)).then_inc(S(f"g_ld{s}"), 16)
            load(0, 0)

            def step(i, j):
                if not is_last(i):
                    load(*next_of(i, j))
                slot_done(sp, "g_in", i, j, GT * 16)
                sp.dma_start(edge_row(xs_e, RING * i + j), ringf[:, j, 0, :]).then_inc(S(f"g_out{j}"), 16)
            groups(sp, step)
            for j in range(RING):
                wait(sp, f"g_out{j}", 16 * (BODIES + (j == 0)))

        block = ctx.enter_context(nc.Block())

        @block.sync
        def _(sp):
            prep_sync(sp)
            assert prep_sync.loads == LOADS
            barrier(sp)
            a_sync(sp)
            barrier(sp)
            barrier(sp)
            barrier(sp)
            barrier(sp)
            linear_sync(sp, "d", xd_e, x1_e, False, "_z")
            barrier(sp)
            linear_sync(sp, "e", x1_e, x2_e, False, "_z")
            barrier(sp)
            f_sync(sp)
            barrier(sp)
            g_sync(sp)
            barrier(sp)
            linear_sync(sp, "h", x3_e, None, True, "_z", xs_e)
            barrier(sp)

        @block.gpsimd
        def _(pool):
            prep_pool(pool)
            barrier(pool)
            a_pool(pool)
            barrier(pool)
            b_pool(pool)
            barrier(pool)
            c_pool(pool)
            barrier(pool)
            barrier(pool)
            attend_pool(pool, "d", x1_t)
            barrier(pool)
            e_pool(pool)
            barrier(pool)
            attend_pool(pool, "f", x3_t)
            barrier(pool)
            g_pool(pool)
            barrier(pool)
            attend_pool(pool, "h", out)
            barrier(pool)

        @block.tensor
        def _(pe):
            prep_tensor(pe)
            barrier(pe)
            a_tensor(pe)
            barrier(pe)
            softmax_tensor(pe, 0, HEADS, feat[:, :, HF:FW], wide, None)
            b_tensor(pe)
            barrier(pe)
            barrier(pe)
            softmax_tensor(pe, 1, 1, logit[:, :, 0:1], slim, (last,))
            barrier(pe)
            attend_tensor(pe, "d", HF, W2_s, 0)
            barrier(pe)
            e_tensor(pe)
            barrier(pe)
            f_tensor(pe)
            barrier(pe)
            barrier(pe)
            softmax_tensor(pe, 2, 1, logit[:, :, 0:1], slim, (first,))
            attend_tensor(pe, "h", P, W3_s, 2)
            barrier(pe)

        @block.scalar
        def _(a):
            prep_scalar(a)
            barrier(a)
            a_scalar(a)
            barrier(a)
            softmax_scalar(a, 0, HEADS, wide)
            b_scalar(a)
            barrier(a)
            c_scalar(a)
            barrier(a)
            softmax_scalar(a, 1, 1, slim)
            barrier(a)
            attend_scalar(a, "d", True)
            barrier(a)
            e_scalar(a)
            barrier(a)
            f_scalar(a)
            barrier(a)
            barrier(a)
            softmax_scalar(a, 2, 1, slim)
            attend_scalar(a, "h", False)
            barrier(a)

        @block.vector
        def _(v):
            prep_vector(v)
            barrier(v)
            a_vector(v)
            barrier(v)
            softmax_vector(v, 0, HEADS, wide, None, None, alpha[:, :, 0:HEADS])
            b_vector(v)
            barrier(v)
            c_vector(v)
            barrier(v)
            softmax_vector(v, 1, 1, slim, (last,), None, alpha[:, :, 0:1])
            barrier(v)
            attend_vector(v, "d", feat, HF, LAST, False)
            barrier(v)
            e_vector(v)
            barrier(v)
            f_vector(v)
            barrier(v)
            g_vector(v)
            barrier(v)
            softmax_vector(v, 2, 1, slim, (first,), 1e-16, alpha[:, :, 0:1])
            attend_vector(v, "h", None, P, FIRST, True)
            barrier(v)


_INS = ['x', 'src', 'dst', 'edge_attr_64', 'L0_gnn_W1', 'L0_gnn_al1', 'L0_gnn_ar1', 'L0_gnn_b1', 'L0_gnn_W2',
        'L0_gnn_al2', 'L0_gnn_ar2', 'L0_gnn_b2', 'L1_gnn_W', 'L1_gnn_b', 'L2_gnn_W1', 'L2_gnn_b1', 'L2_gnn_W2',
        'L2_gnn_b2', 'L2_gnn_Wm', 'L2_gnn_bm', 'L2_gnn_Wx', 'L2_gnn_bx', 'L2_gnn_Ws', 'L2_gnn_bs', 'L3_gnn_W',
        'L3_gnn_att', 'L3_gnn_bias']


def kernel(**inputs):
    import numpy as _np
    import concourse.bacc as _bacc
    from concourse import mybir as _mybir
    from concourse.bass_utils import run_bass_kernel_spmd as _run

    nc = _bacc.Bacc("TRN2", target_bir_lowering=False, num_devices=1)
    arrays, args = {}, []
    for name in _INS:
        a = _np.ascontiguousarray(inputs[name])
        arrays[f"in_{name}_dram"] = a
        args.append(nc.dram_tensor(f"in_{name}_dram", a.shape, _mybir.dt.from_np(a.dtype), kind="ExternalInput").ap())
    args.append(nc.dram_tensor("out_0_dram", (N, F), _mybir.dt.float32, kind="ExternalOutput").ap())
    program(nc, *args)
    r = _run(nc, [arrays], core_ids=[0])
    return r.results[0]["out_0_dram"]
```

```python
from contextlib import ExitStack

import concourse.bass as bass
from concourse import mybir

F32 = mybir.dt.float32
BF16 = mybir.dt.bfloat16
I32 = mybir.dt.int32
U32 = mybir.dt.uint32
U8 = mybir.dt.uint8
ALU = mybir.AluOpType
ACT = mybir.ActivationFunctionType
X = mybir.AxisListType.X

P = 128
N, E, F = 50000, 25000, 128
HEADS, HID = 4, 16
HF = HEADS * HID
FW = HF + HEADS
HW = HF + 1
EF = 64
GT = 4
GE = GT * P
NG = -(-E // GE)
NT = NG * GT
CH = 2 * P
NQ = NT * P // CH
EP = NT * P
RING = 4
BODIES = NG // RING
NJ = N // P
NTAIL = N - NJ * P
DK = 8
DLAST = NJ - (NG - 1) * DK
SKIP = 1 << 16
BIG = 1.0e38
FAR = -3.0e38
EPS = 1e-5
SLOPE = 0.2
assert NG % RING == 1 and NQ * 2 == NT and 0 < DLAST < DK


def program(nc, x, src, dst, ea, W1, al1, ar1, b1, W2, al2, ar2, b2, L1W, L1b,
            M1, m1, M2, m2, Mm, bm, Mx, bx, Ms, bs, W3, att, b4, out):
    def dram(name, shape, dt=F32):
        return nc.dram_tensor(name, shape, dt, kind="Internal").ap()

    hidden_t = dram("hidden_t", (N, HW))
    x1_t = dram("x1_t", (N, F))
    x3_t = dram("x3_t", (N, F))
    xd_e = dram("xd_e", (NG, P, GT * F))
    x1_e = dram("x1_e", (NG, P, GT * F))
    x2_e = dram("x2_e", (NG, P, GT * F))
    x3_e = dram("x3_e", (NG, P, GT * F))
    xs_e = dram("xs_e", (NG, P, GT * F))
    cont_d = dram("cont_d", (2, EP), U8)

    with ExitStack() as ctx:
        def sb(name, shape, dt=F32):
            return ctx.enter_context(nc.sbuf_tensor(name, shape, dt))

        def sem(name):
            return ctx.enter_context(nc.semaphore(name))

        bank = [ctx.enter_context(nc.psum_tensor(f"bank{n}", [P, 512], F32)) for n in range(8)]

        ident = sb("ident", [P, P])
        before = sb("before", [P, NQ])
        after = sb("after", [P, NQ])
        ones = sb("ones", [P, P])
        W1x = sb("W1x", [P, FW])
        W1r = sb("W1r", [P, HEADS])
        W2_s = sb("W2_s", [HF, F])
        W2x = sb("W2x", [HF, HF + 2])
        L1T = sb("L1T", [P, F])
        raw = sb("raw", [P, F])
        M1a = sb("M1a", [P, F])
        M1b = sb("M1b", [EF, F])
        M2_s = sb("M2_s", [P, F])
        Mm_s = sb("Mm_s", [P, F])
        Mx_s = sb("Mx_s", [P, F])
        Ms_s = sb("Ms_s", [P, F])
        W3_s = sb("W3_s", [P, F])
        W3T = sb("W3T", [P, F])
        bias = sb("bias", [P, 4, F])
        biasc = sb("biasc", [P, 4, F])
        brow4 = sb("brow4", [1, 2, GT * F])
        m3c = sb("m3c", [P, 1])
        bT = sb("bT", [P, 4])
        BB = sb("BB", [P, 16])
        tmpw = sb("tmpw", [P, F])
        b1c = sb("b1c", [HF, 4])
        m1c = sb("m1c", [P, 1])
        m2c = sb("m2c", [P, 1])
        attc = sb("attc", [P, 2])
        attb = sb("attb", [P, 2, F])
        hcol = sb("hcol", [HF, P])
        wmean = sb("wmean", [P, 4])

        cv = sb("cv", [P, 10, CH])
        first = sb("first", [P, CH])
        last = sb("last", [P, CH])
        contb = sb("contb", [P, 2, CH], U8)
        keepf = sb("keepf", [P, CH])
        keepb = sb("keepb", [P, CH])
        penf = sb("penf", [P, CH])
        penb = sb("penb", [P, CH])
        head = sb("head", [P, CH])
        tail = sb("tail", [P, CH])
        headp = sb("headp", [P, CH])
        tailp = sb("tailp", [P, CH])
        linkf = sb("linkf", [P, NQ])
        linkb = sb("linkb", [P, NQ])
        linkfp = sb("linkfp", [P, NQ])
        linkbp = sb("linkbp", [P, NQ])
        endd = sb("endd", [P, 2])
        cont = sb("cont", [P, EP], U8)
        idx = sb("idx", [P, 4, NT + 8], I32)
        SRC, DST, LAST, FIRST = range(4)
        lastR = sb("lastR", [P, NT])
        invR = sb("invR", [P, NT])
        ixr = sb("ixr", [P, RING, 2, GT], I32)

        big = sb("big", [P, NT * FW + DK * F])
        feat = big[:, 0:NT * FW].rearrange("p (t f) -> p t f", f=FW)
        def part(start, n):
            return big[:, start * GE:start * GE + n]

        bload = part(0, 2 * F).rearrange("p (n f) -> p n f", f=F)
        alb = part(1, 2 * F).rearrange("p (n f) -> p n f", f=F)
        e_src, e_dst, e_prev, e_next = (part(2 + n, CH).bitcast(I32) for n in range(4))
        hconst = part(6, 10 * HW).rearrange("p (n f) -> p n f", f=HW)
        X2T = part(9, 4 * GE).rearrange("p (s e) -> p s e", s=4)
        aT = part(13, 2 * GE).rearrange("p (s e) -> p s e", s=2)
        bT2 = part(15, 2 * GE).rearrange("p (s e) -> p s e", s=2)
        MX = part(2, 2 * GE).rearrange("p (s e) -> p s e", s=2)
        xd2 = sb("xd2", [P, DK * F])
        zA = part(4, 2 * GE).rearrange("p (s t f) -> p s t f", s=2, f=F)
        eaT = part(6, 2 * GE)[0:EF].rearrange("p (s e) -> p s e", s=2)
        neg = part(8, GE).bitcast(BF16).rearrange("p (s e) -> p s e", s=2)
        slim = [cv[:, n:n + 1, :] for n in range(9)]
        xload = sb("xload", [P, 2, GT, F])
        xloadf = xload[:, :, :, :].rearrange("p r t f -> p r (t f)")
        ring = sb("ring", [P, RING, 2, GT, F])
        ringf = ring[:, :, :, :, :].rearrange("p r a t f -> p r a (t f)")
        outr = sb("outr", [P, RING, GT, F])
        outf = outr[:, :, :, :].rearrange("p r t f -> p r (t f)")
        xT = sb("xT", [P, 2, 2, GE])
        msg = sb("msg", [P, 2, GT, F])
        G = sb("G", [P, 2, GE])
        z = sb("z", [P, 2, GT, F])
        hT = sb("hT", [P, 2, 3, GE])
        blocks = [t.rearrange("p n -> p n") for t in (
            msg[:, :, :, :].rearrange("p s t f -> p (s t f)"), G[:, :, :].rearrange("p s e -> p (s e)"),
            z[:, :, :, :].rearrange("p s t f -> p (s t f)"), xload[:, :, :, :].rearrange("p s t f -> p (s t f)"),
            outf[:, 0:2, :].rearrange("p s e -> p (s e)"), outf[:, 2:4, :].rearrange("p s e -> p (s e)"),
            hT[:, 0, 0:2, :].rearrange("p s e -> p (s e)"), hT[:, 1, 1:3, :].rearrange("p s e -> p (s e)"),
            big[:, NT * FW:NT * FW + DK * F], xd2[:, :])]
        kf = [t.rearrange("p (k f) -> p k f", f=F) for t in blocks]
        u, y, xin, dxT = kf[0:4], kf[4:7], kf[7:9], blocks[9]
        wide = [t.rearrange("p (h c) -> p h c", h=HEADS) for t in blocks[0:7]]
        sd = sb("sd", [P, DK])
        epsc = sb("epsc", [P, 1])
        stats = sb("stats", [P, DK, 6])
        mv = sb("mv", [P, 2, DK, 2])
        rn = sb("rn", [P, 2, GT, 2])
        rho = sb("rho", [P, 2, 4, DK])
        small = sb("small", [P, 16, DK])
        dots = sb("dots", [P, DK, 4])
        logit = sb("logit", [P, NT, 1])
        alpha = sb("alpha", [P, NT, HEADS])
        own = sb("own", [P, NT])
        carry = sb("carry", [P, 4, HEADS])
        R1 = G

        idle = sem("idle")
        phase = sem("phase")
        sems = {}

        def sem_of(name):
            if name not in sems:
                sems[name] = sem(name)
            return sems[name]

        def S(name):
            return sem_of(shared(name)[0])

        SHARED = {
            "in": (4, {"a": 2 * GT * 16, "c": GT * 16, "e": GT * 16, "g": GT * 16}),
            "out": (4, {"a": 16, "d": 16, "e": 16, "f": 16, "g": 16}),
            "sc": (4, {"b": GT * 16, "d": GT * 16, "f": GT * 16, "h": GT * 16}),
            "ld": (2, {"d": 16, "e": 16, "g": 16, "h": 16}),
            "ix": (1, {"a": 2, "b": 1, "c": 1, "d": 1, "e": 1, "f": 1, "g": 1, "h": 1}),
            "tr": (1, {"a": 1, "b": 1, "d": 1, "e": 1, "f": 1, "h": 1}),
            "scan": (1, {"b": 1, "d": 1, "e": 1, "h": 1}),
            "mm": (1, {"a": 1, "b": 1, "d": 1, "e": 1, "h": 1}),
            "z": (1, {"d": 1, "e": 1, "f": 1, "h": 1}),
            "var": (1, {"d": 1, "e": 1, "f": 1, "h": 1}),
            "sd": (1, {"d": 1, "e": 1, "f": 1, "h": 1}),
            "bn": (1, {"d": 1, "e": 1, "f": 1, "h": 1}),
            "rc": (1, {"d": 1, "e": 1, "f": 1, "h": 1}),
            "st": (1, {"d": 1, "e": 1, "f": 1, "h": 1}),
            "row": (1, {"b": 1, "d": 1, "e": 1, "f": 1, "h": 1}),
            "msg": (1, {"b": 1, "d": 1, "f": 1, "h": 1}),
        }

        def shared(name):
            tag, _, kind = name.partition("_")
            slot = kind[-1] if kind[-1:].isdigit() else ""
            kind = kind[:-1] if slot else kind
            ways, users = SHARED.get(kind, (0, {}))
            if tag not in users or bool(slot) != (ways > 1):
                return name, 0
            uses = len(range(int(slot), NG, ways)) if slot else NG + (kind == "ix")
            start = 0
            for t, per in users.items():
                if t == tag:
                    return "g_" + kind + slot, start
                start += per * uses

        def wait(eng, name, n):
            sem_name, start = shared(name)
            eng.wait_ge(sem_of(sem_name), n + start)
            if eng is nc.sync and not isinstance(n, int):
                pause(eng)

        def pause(eng):
            eng.sem_inc(idle, 1)

        phases = {}

        def barrier(eng):
            phases[eng] = phases.get(eng, 0) + 1
            eng.drain().then_inc(phase, 1)
            eng.wait_ge(phase, 5 * phases[eng])

        def groups(eng, step):
            for j in range(RING):
                step(0, j)
            with eng.Fori(1, BODIES) as i:
                for j in range(RING):
                    step(i, j)
            step(BODIES, 0)

        def pipeline(eng, stages):
            least, most = min(lag for lag, _ in stages), max(lag for lag, _ in stages)

            def fixed(g):
                for lag, stage in stages:
                    if 0 <= g - lag < NG:
                        stage((g - lag) // RING, (g - lag) % RING)
            for g in range(least, RING):
                fixed(g)
            with eng.Fori(1, BODIES) as i:
                for j in range(RING):
                    for lag, stage in stages:
                        stage(i + (j - lag) // RING, (j - lag) % RING)
            for g in range(NG - 1, NG + most):
                fixed(g)

        def count(eng, name, i, j, lag=0, per=1):
            n = RING * i + j + 1 - lag
            if isinstance(n, int) and n <= 0:
                return
            wait(eng, name, n * per)

        def slot_done(eng, name, i, j, per, lag=0):
            n = i + 1 - lag
            if isinstance(n, int) and n <= 0:
                return
            wait(eng, f"{name}{j}", n * per)

        class Chain:

            def __init__(self, eng, name):
                self.eng, self.sem, self.n, self.base, self.per = eng, S(name), 0, 0, None

            def at(self, i, j):
                if self.per is None and not (i == 0 and j == 0 and isinstance(i, int)):
                    self.per = self.n
                if self.per is not None:
                    assert self.n == self.per, (self.n, self.per)
                    self.base = (RING * i + j) * self.per
                self.n = 0

            def do(self, ins):
                ins.then_inc(self.sem, 1)
                self.n += 1
                return ins

            def hold(self):
                self.eng.wait_ge(self.sem, self.base + self.n)

            def link(self, ins):
                self.do(ins)
                self.hold()

        def four(g):
            return bass.ds(g * GT, GT)

        def col(v):
            return v.rearrange("(p a) -> p a", a=1)

        def rowof(v):
            return v.rearrange("(a n) -> a n", a=1)

        FULL = E // CH
        REST = E - FULL * CH

        def prep_sync(sp):
            w = S("weights")
            loads = [
                (W1x[:, 0:HF], W1), (W2_s[:], W2), (raw[:], L1W),
                (M1a[:], M1[0:F, :]), (M1b[:], M1[F:F + EF, :]), (M2_s[:], M2), (Mm_s[:], Mm), (Mx_s[:], Mx),
                (Ms_s[:], Ms), (W3_s[:], W3),
                (bias[:, 0, :], b2.partition_broadcast(P)), (bias[:, 1, :], L1b.partition_broadcast(P)),
                (bias[:, 2, :], bm.partition_broadcast(P)), (bias[:, 3, :], b4.partition_broadcast(P)),
                (bload[:, 0, :], bx.partition_broadcast(P)), (bload[:, 1, :], bs.partition_broadcast(P)),
                (alb[:, 0, 0:HF], al1.rearrange("h d -> (h d)").partition_broadcast(P)),
                (alb[:, 0, HF:], ar1.rearrange("h d -> (h d)").partition_broadcast(P)),
                (hT[0:HF, 0, 0, 0:F], al2.rearrange("h d -> (h d)").partition_broadcast(HF)),
                (hT[0:HF, 0, 1, 0:F], ar2.rearrange("h d -> (h d)").partition_broadcast(HF)),
                (b1c[:, 0:1], col(b1)), (m1c[:], col(m1)), (m2c[:], col(m2)),
                (attc[:, 0:1], col(att[0, 0:F])), (attc[:, 1:2], col(att[0, F:])),
            ]
            for to, frm in loads:
                sp.dma_start(to, frm).then_inc(w, 16)
            prep_sync.loads = len(loads)
            sp.wait_ge(S("pads"), 1)
            edges = [
                (e_src[0:FULL, :], src[0:FULL * CH].rearrange("(q c) -> q c", c=CH)),
                (e_src[FULL:FULL + 1, 0:REST], rowof(src[FULL * CH:E])),
                (e_dst[0:FULL, :], dst[0:FULL * CH].rearrange("(q c) -> q c", c=CH)),
                (e_dst[FULL:FULL + 1, 0:REST], rowof(dst[FULL * CH:E])),
                (e_prev[0:1, 1:CH], rowof(dst[0:CH - 1])),
                (e_prev[1:FULL, :], dst[CH - 1:FULL * CH - 1].rearrange("(q c) -> q c", c=CH)),
                (e_prev[FULL:FULL + 1, 0:REST + 1], rowof(dst[FULL * CH - 1:E])),
                (e_next[0:FULL, :], dst[1:FULL * CH + 1].rearrange("(q c) -> q c", c=CH)),
                (e_next[FULL:FULL + 1, 0:REST - 1], rowof(dst[FULL * CH + 1:E])),
            ]
            for to, frm in edges:
                sp.dma_start(to, frm).then_inc(S("edges"), 16)
            sp.wait_ge(S("cont_made"), 2)
            sp.dma_start(cont_d[0, :].rearrange("(q c) -> q c", c=CH), contb[0:NQ, 0, :]).then_inc(S("cont_out"), 16)
            sp.dma_start(cont_d[1, :].rearrange("(q c) -> q c", c=CH), contb[0:NQ, 1, :]) \
                .then_inc(S("cont_out"), 16)
            sp.wait_ge(S("cont_out"), 32)
            sp.dma_start(cont[:], cont_d[0, :].partition_broadcast(P)).then_inc(S("cont_in"), 16)
            sp.wait_ge(S("hconst"), 1)
            main = hidden_t[0:NJ * P, :].rearrange("(p j) f -> p j f", p=P)
            with sp.Fori(0, NJ // 10) as i:
                sp.dma_start(main[:, bass.ds(i * 10, 10), :], hconst[:]).then_inc(S("hfill"), 16)
            sp.dma_start(hidden_t[NJ * P:N, :], hconst[0:NTAIL, 0, :]).then_inc(S("hfill"), 16)
            sp.wait_ge(S("cont_in"), 16)
            sp.wait_ge(S("hfill"), 16 * (NJ // 10 + 1))

        def prep_pool(pool):
            made = S("shapes")
            nc.gpsimd.memset(ident[:], 0.0).then_inc(made, 1)
            nc.gpsimd.memset(before[:], 1.0).then_inc(made, 1)
            nc.gpsimd.memset(after[:], 1.0).then_inc(made, 1)
            pool.wait_ge(made, 3)
            nc.gpsimd.affine_select(out=ident[:], in_=ident[:], compare_op=ALU.not_equal, fill=1.0, base=0,
                                    pattern=[[-1, P]], channel_multiplier=1).then_inc(made, 1)
            nc.gpsimd.affine_select(out=before[:], in_=before[:], compare_op=ALU.is_gt, fill=0.0, base=0,
                                    pattern=[[1, NQ]], channel_multiplier=-1).then_inc(made, 1)
            nc.gpsimd.affine_select(out=after[:], in_=after[:], compare_op=ALU.is_gt, fill=0.0, base=0,
                                    pattern=[[-1, NQ]], channel_multiplier=1).then_inc(made, 1)

        def prep_tensor(pe):
            pe.wait_ge(S("shapes"), 6)
            pe.wait_ge(S("weights"), 16 * LOADS)
            nc.tensor.transpose(bank[0][:, 0:P], raw[:], ident[:])
            nc.tensor.transpose(bank[0][:, P:2 * P], W3_s[:], ident[:]).then_inc(S("wt"), 1)
            pe.wait_ge(S("biasc"), 1)
            for n in range(4):
                ins = nc.tensor.transpose(bank[1][:, n * P:(n + 1) * P], biasc[:, n, :], ident[:])
            ins.then_inc(S("bt"), 1)
            nc.tensor.transpose(bank[7][:, 0:P], bias[:, 2, :], ident[:]).then_inc(S("m3"), 1)
            pe.wait_ge(S("attb"), 1)
            for n in range(2):
                ins = nc.tensor.matmul(bank[2][:, n * P:(n + 1) * P], attb[:, n, :], W3T[:], start=True, stop=True)
            ins.then_inc(S("wa"), 1)
            pe.wait_ge(S("bcols"), 1)
            for n in range(4):
                ins = nc.tensor.matmul(bank[3][:, 4 * n:4 * n + 4], raw4[n], bT[:], start=True, stop=True)
            ins.then_inc(S("bb"), 1)
            pe.wait_ge(S("hcol"), 1)
            nc.tensor.matmul(bank[4][:, 0:HW], hcol[:], W2x[:, 0:HW], start=True, stop=True).then_inc(S("hrow0"), 1)
            pe.wait_ge(S("ends"), 1)
            nc.tensor.transpose(bank[5][0:NQ, 0:NQ], cv[0:NQ, 1, 0:1].to_broadcast([NQ, NQ]), ident[0:NQ, 0:NQ])
            nc.tensor.transpose(bank[5][0:NQ, P:P + NQ], cv[0:NQ, 1, CH - 1:CH].to_broadcast([NQ, NQ]),
                                ident[0:NQ, 0:NQ]).then_inc(S("endrows"), 1)
            pe.wait_ge(S("links"), 1)
            nc.tensor.matmul(bank[6][0:NQ, 0:1], linkf[0:NQ, :], cv[0:NQ, 6, CH - 1:CH], start=True, stop=True)
            nc.tensor.matmul(bank[6][0:NQ, 1:2], linkb[0:NQ, :], cv[0:NQ, 7, 0:1],
                             start=True, stop=True).then_inc(S("degc"), 1)
            pe.wait_ge(S("tomake"), 1)
            for m in range(6):
                if m % 2 == 0 and m:
                    pe.wait_ge(S("torow"), m)
                for r in range(2):
                    ins = nc.tensor.transpose(bank[m % 2][:, r * P:r * P + NQ],
                                              rowsrc[m][0:NQ, r * P:(r + 1) * P], ident[0:NQ, 0:NQ])
                ins.then_inc(S("rowps"), 1)

        rowsrc = [cv[:, 0, :], cv[:, 2, :], cv[:, 3, :], cv[:, 4, :], last, cv[:, 5, :]]
        raw4 = [msg[:, 0, n, :] for n in range(4)]

        def prep_vector(v):
            c = Chain(v, "prep_dve")
            for t in (e_src, e_dst, e_prev, e_next):
                c.do(v.memset(t[:], 0 if t is e_src else N))
            c.hold()
            v.memset(e_prev[0:1, 0:1], -1).then_inc(S("pads"), 1)
            v.memset(ones[:], 1.0)
            v.memset(epsc[:], EPS)
            c.do(v.memset(idx[:], 0))
            v.wait_ge(S("weights"), 16 * LOADS)
            v.wait_ge(S("shapes"), 6)
            for n, to in ((0, W1x[:, HF:FW]), (1, W1r[:])):
                c.link(v.tensor_tensor(tmpw[:, 0:HF], W1x[:, 0:HF], alb[:, 0, n * HF:(n + 1) * HF], ALU.mult))
                c.link(v.tensor_reduce(to, tmpw[:, 0:HF].rearrange("p (h d) -> p h d", h=HEADS), X, ALU.add))
            c.do(v.tensor_copy(W2x[:, 0:HF], ident[0:HF, 0:HF]))
            for n in range(2):
                c.link(v.tensor_tensor(tmpw[0:HF, :], W2_s[:], hT[0:HF, 0, n, 0:F], ALU.mult))
                c.link(v.tensor_reduce(W2x[:, HF + n:HF + n + 1], tmpw[0:HF, :], X, ALU.add))
            c.link(v.tensor_tensor(bias[:, 2, :], bias[:, 2, :], bload[:, 0, :], ALU.add))
            c.link(v.tensor_tensor(bias[:, 2, :], bias[:, 2, :], bload[:, 1, :], ALU.add))
            for n, k in ((0, 0), (1, 3)):
                c.do(v.tensor_copy(brow4[0:1, n, :].rearrange("p (t f) -> p t f", f=F),
                                   bias[0:1, k:k + 1, :].to_broadcast([1, GT, F])))
            c.link(v.tensor_reduce(wmean[:], bias[:], X, ALU.add))
            c.link(v.tensor_scalar(wmean[:], wmean[:], -1.0 / F, None, ALU.mult))
            for n in range(4):
                c.do(v.tensor_scalar(biasc[:, n, :], bias[:, n, :], wmean[:, n:n + 1], None, ALU.add))
            c.hold()
            v.sem_inc(S("biasc"), 1)
            v.wait_ge(S("wt"), 1)
            c.do(v.tensor_copy(L1T[:], bank[0][:, 0:P]))
            c.do(v.tensor_copy(W3T[:], bank[0][:, P:2 * P]))
            for n in range(2):
                c.do(v.tensor_scalar(attb[:, n, :], ones[:], attc[:, n:n + 1], None, ALU.mult))
            c.hold()
            v.sem_inc(S("attb"), 1)
            v.wait_ge(S("bt"), 1)
            c.link(v.tensor_scalar(bT[:], bank[1][:, :].rearrange("p (n m) -> p n m", n=4)[:, :, 0], 1.0 / F, None,
                                   ALU.mult))
            for n in range(4):
                c.do(v.tensor_scalar(raw4[n], ones[:], bank[1][:, n * P:n * P + 1], None, ALU.mult))
            c.hold()
            v.sem_inc(S("bcols"), 1)
            v.wait_ge(S("m3"), 1)
            c.do(v.tensor_copy(m3c[:], bank[7][:, 0:1]))
            v.wait_ge(S("wa"), 1)
            c.do(v.tensor_copy(attb[:], bank[2][:, 0:2 * P].rearrange("p (n f) -> p n f", n=2)))
            v.wait_ge(S("bb"), 1)
            c.do(v.tensor_copy(BB[:], bank[3][:, 0:16]))
            v.tensor_scalar(b1c[:, 1:2], b1c[:, 0:1], 0.0, None, ALU.min).then_inc(S("b1min"), 1)
            c.do(v.tensor_scalar(b1c[:, 2:3], b1c[:, 0:1], 0.0, None, ALU.max))
            v.wait_ge(S("b1exp"), 1)
            c.hold()
            c.link(v.scalar_tensor_tensor(b1c[:, 3:4], b1c[:, 3:4], -1.0, b1c[:, 2:3], ALU.add, ALU.add))
            v.tensor_scalar(hcol[:], ones[0:HF, :], b1c[:, 3:4], None, ALU.mult).then_inc(S("hcol"), 1)
            v.wait_ge(S("hrow0"), 1)
            for n in range(10):
                c.do(v.tensor_copy(hconst[:, n, :], bank[4][:, 0:HW]))
            c.hold()
            v.sem_inc(S("hconst"), 1)

            v.wait_ge(S("edges"), 16 * 9)
            for n, t in ((0, e_src), (1, e_dst), (8, e_prev), (9, e_next)):
                c.do(v.tensor_copy(cv[:, n, :], t[:]))
            c.hold()
            q = slice(0, NQ)
            v.sem_inc(S("ends"), 1)
            c.do(v.tensor_tensor(first[:], cv[:, 1, :], cv[:, 8, :], ALU.not_equal))
            c.do(v.tensor_tensor(last[:], cv[:, 1, :], cv[:, 9, :], ALU.not_equal))
            v.tensor_tensor(contb[:, 0, :], cv[:, 1, :], cv[:, 8, :], ALU.is_equal).then_inc(S("cont_made"), 1)
            v.tensor_tensor(contb[:, 1, :], cv[:, 1, ::-1], cv[:, 9, ::-1], ALU.is_equal).then_inc(S("cont_made"), 1)
            c.hold()
            c.do(v.tensor_scalar(keepf[:], first[:], -1.0, 1.0, ALU.mult, ALU.add))
            c.do(v.tensor_scalar(keepb[:], last[:], -1.0, 1.0, ALU.mult, ALU.add))
            c.hold()
            c.do(v.memset(keepf[:, 0:1], 0.0))
            c.do(v.memset(keepb[:, CH - 1:CH], 0.0))
            c.do(v.tensor_scalar(head[:], cv[:, 1, :], cv[:, 1, 0:1], None, ALU.is_equal))
            c.do(v.tensor_scalar(tail[:], cv[:, 1, :], cv[:, 1, CH - 1:CH], None, ALU.is_equal))
            c.hold()
            for to, frm in ((penf, keepf), (penb, keepb), (headp, head), (tailp, tail)):
                c.do(v.tensor_scalar(to[:], frm[:], -1.0, BIG, ALU.add, ALU.mult))
            v.wait_ge(S("endrows"), 1)
            c.do(v.scalar_tensor_tensor(linkf[q, :], bank[5][q, 0:NQ], cv[q, 1, CH - 1:CH], before[q, :],
                                        ALU.is_equal, ALU.mult))
            c.do(v.scalar_tensor_tensor(linkb[q, :], bank[5][q, P:P + NQ], cv[q, 1, 0:1], after[q, :],
                                        ALU.is_equal, ALU.mult))
            c.hold()
            c.do(v.tensor_scalar(linkfp[q, :], linkf[q, :], -1.0, BIG, ALU.add, ALU.mult))
            c.do(v.tensor_scalar(linkbp[q, :], linkb[q, :], -1.0, BIG, ALU.add, ALU.mult))
            c.link(v.memset(cv[:, 5, :], 1.0))
            c.do(v.tensor_tensor_scan(cv[q, 6, :], keepf[q, :], cv[q, 5, :], 0.0, ALU.mult, ALU.add))
            c.do(v.tensor_tensor_scan(cv[q, 7, ::-1], keepb[q, ::-1], cv[q, 5, :], 0.0, ALU.mult, ALU.add))
            c.hold()
            v.sem_inc(S("links"), 1)
            v.wait_ge(S("degc"), 1)
            c.link(v.tensor_copy(carry[q, 0, 0:2], bank[6][q, 0:2]))
            c.link(v.scalar_tensor_tensor(cv[q, 6, :], cv[q, 6, :], -1.0, cv[q, 7, :], ALU.add, ALU.add))
            c.link(v.scalar_tensor_tensor(cv[q, 6, :], head[q, :], carry[q, 0, 0:1], cv[q, 6, :], ALU.mult, ALU.add))
            c.link(v.scalar_tensor_tensor(cv[q, 6, :], tail[q, :], carry[q, 0, 1:2], cv[q, 6, :], ALU.mult, ALU.add))
            c.link(v.reciprocal(cv[q, 5, :], cv[q, 6, :]))
            c.do(v.tensor_scalar(cv[:, 2, :], cv[:, 1, :], float(N - 1), None, ALU.min))
            for n, m in ((3, last), (4, first)):
                c.link(v.scalar_tensor_tensor(cv[:, n, :], cv[:, 1, :], -float(SKIP), m[:], ALU.add, ALU.mult))
                c.link(v.tensor_scalar(cv[:, n, :], cv[:, n, :], float(SKIP), None, ALU.add))
            v.sem_inc(S("tomake"), 1)
            for m in range(6):
                v.wait_ge(S("rowps"), m + 1)
                to = idx[:, m, GT:GT + NT] if m < 4 else (lastR if m == 4 else invR)[:, :]
                to = to.rearrange("p (q r) -> p r q", r=2)
                v.tensor_copy(to, bank[m % 2][:, 0:2 * P].rearrange("p (r q) -> p r q", r=2)[:, :, 0:NQ]) \
                    .then_inc(S("torow"), 1)
            v.wait_ge(S("torow"), 6)

        def prep_scalar(a):
            a.wait_ge(S("b1min"), 1)
            nc.scalar.activation(b1c[:, 3:4], b1c[:, 1:2], ACT.Exp).then_inc(S("b1exp"), 1)

        LOADS = 25

        def index_columns(v, name, kinds, gathered, per, i, j, rev=False):
            s = (j + 2) % RING
            uses = i if j < 2 else i + 1
            if not (isinstance(uses, int) and uses == 0):
                wait(v, f"{gathered}{s}", uses * per)
                pause(v)
            g = RING * i + j + 2
            if rev:
                g = NG - 1 - g
            for n, kind in enumerate(kinds):
                v.tensor_copy(ixr[:, s, n, :], idx[:, kind, four(g + 1)]).then_inc(S(name), 1)

        def index_first(v, name, kinds, rev=False):
            for s in range(2):
                g = NG - 1 - s if rev else s
                for n, kind in enumerate(kinds):
                    v.tensor_copy(ixr[:, s, n, :], idx[:, kind, four(g + 1)]).then_inc(S(name), 1)

        def indices(eng, name, kinds, i, j):
            wait(eng, name, (RING * i + j + 1) * kinds)

        def gather(pool, to, table, s, n, done):
            for c in range(GT):
                nc.gpsimd.indirect_dma_start(
                    to(c), None, table, bass.IndirectOffsetOnAxis(ap=ixr[:, s, n, c:c + 1].bitcast(U32), axis=0)
                ).then_inc(done, 16)

        def scatter(pool, frm, table, s, n, done):
            for c in range(GT):
                nc.gpsimd.indirect_dma_start(
                    table, bass.IndirectOffsetOnAxis(ap=ixr[:, s, n, c:c + 1].bitcast(U32), axis=0), frm(c), None,
                    bounds_check=N - 1, oob_is_err=False).then_inc(done, 16)

        def norm_stats(v, tag):
            def stage(i, j):
                s = j % 2
                count(v, tag + "_z", i, j)
                for k in range(GT):
                    ins = v.bn_stats(stats[:, k, :], z[:, s, k, :])
                ins.then_inc(S(tag + "_bn"), 1)
            return stage

        def norm_var(v, tag):
            def stage(i, j):
                count(v, tag + "_bn", i, j)
                pause(v)
                for k in range(GT):
                    ins = v.bn_aggr(mv[:, 0, k, :], stats[:, k, :])
                ins.then_inc(S(tag + "_var"), 1)
            return stage

        def norm_scale(v, tag, masked=False):
            def stage(i, j):
                s = j % 2
                count(v, tag + "_sd", i, j)
                count(v, tag + "_row", i, j, 2)
                v.reciprocal(rn[:, s, :, 0], sd[:, 0:GT]).then_inc(S(tag + "_rc"), 1)
                count(v, tag + "_rc", i, j)
                v.scalar_tensor_tensor(rn[:, s, :, 1], mv[:, 0, 0:GT, 0], -1.0, rn[:, s, :, 0], ALU.mult, ALU.mult) \
                    .then_inc(S("e_rm" if masked else tag + "_st"), 1)
                if masked:
                    count(v, "e_rm", i, j)
                    v.tensor_tensor(rn[:, s], rn[:, s],
                                    lastR[:, four(RING * i + j)].unsqueeze(2).to_broadcast([P, GT, 2]),
                                    ALU.mult).then_inc(S("e_st"), 1)
            return stage

        def norm_sqrt(a, tag, i, j):
            count(a, tag + "_var", i, j)
            nc.scalar.activation(sd[:, 0:GT], mv[:, 0, 0:GT, 1], ACT.Sqrt, bias=epsc[:]).then_inc(S(tag + "_sd"), 1)

        def norm_apply(frm, to, sc):
            for k in range(GT):
                ins = nc.scalar.activation(to[:, k, :], frm[:, k, :], ACT.Identity,
                                           bias=sc[:, k, 1:2], scale=sc[:, k, 0:1])
            return ins

        Q = slice(0, NQ)

        def softmax_tensor(pe, turn, nh, lg, work, spread):
            ee, fs, bs_ = work[3], work[4], work[5]
            fm, bm_ = work[1], work[2]
            if spread is not None:
                kind = spread[0]
                link = linkf if kind is first else linkb
                at = slice(CH - 1, CH) if kind is first else slice(0, 1)
                for r in range(2):
                    ins = nc.tensor.transpose(bank[2][Q, r * P:(r + 1) * P],
                                              own[:, :].rearrange("p (q r) -> p r q", r=2)[:, r, :], ident[:])
                ins.then_inc(S("sm_own"), 1)
                pe.wait_ge(S("sm_ownscan"), turn)
                nc.tensor.matmul(bank[3][Q, 0:1], link[Q, :], work[6][Q, 0, at],
                                 start=True, stop=True).then_inc(S("sm_owncarry"), 1)
            for r in range(2):
                for h in range(nh):
                    ins = nc.tensor.transpose(bank[r][Q, h * P:(h + 1) * P],
                                              lg.rearrange("p (q r) h -> p r h q", r=2)[:, r, h, :], ident[:])
            ins.then_inc(S("sm_lg"), 1)
            pe.wait_ge(S("sm_max"), turn + 1)
            for h in range(nh):
                nc.tensor.transpose(bank[4][Q, h * NQ:(h + 1) * NQ], fm[Q, h, CH - 1:CH].to_broadcast([NQ, NQ]),
                                    ident[Q, 0:NQ])
                ins = nc.tensor.transpose(bank[5][Q, h * NQ:(h + 1) * NQ], bm_[Q, h, 0:1].to_broadcast([NQ, NQ]),
                                          ident[Q, 0:NQ])
            ins.then_inc(S("sm_maxrow"), 1)
            pe.wait_ge(S("sm_sum"), turn + 1)
            nc.tensor.matmul(bank[6][Q, 0:nh], linkf[Q, :], fs[Q, :, CH - 1], start=True, stop=True)
            nc.tensor.matmul(bank[6][Q, nh:2 * nh], linkb[Q, :], bs_[Q, :, 0], start=True, stop=True) \
                .then_inc(S("sm_sumcarry"), 1)
            pe.wait_ge(S("sm_alpha"), turn + 1)
            for r in range(2):
                for h in range(nh):
                    ins = nc.tensor.transpose(bank[r][:, h * NQ:(h + 1) * NQ], ee[Q, h, r * P:(r + 1) * P],
                                              ident[Q, 0:NQ])
            ins.then_inc(S("sm_back"), 1)

        def softmax_vector(v, turn, nh, work, spread, guard, to):
            c = Chain(v, f"sm{turn}_dve")
            lg, fm, bm_, ee, fs, bs_, tot = (work[n] for n in range(7))

            def flat(t):
                return t[Q].rearrange("p h c -> p (h c)")

            def scans(to, keep, frm, ini, op0, op1, rev):
                for h in range(nh):
                    o, d0, d1 = to[Q, h, :], keep[Q, :], frm[Q, h, :]
                    if rev:
                        o, d0, d1 = back(o), back(d0), back(d1)
                    c.do(v.tensor_tensor_scan(o, d0, d1, ini, op0, op1))

            def back(ap):
                return ap[:, ::-1]

            if spread is not None:
                kind = spread[0]
                keep, edge = (keepf, head) if kind is first else (keepb, tail)
                v.wait_ge(S("sm_own"), turn)
                c.link(v.tensor_tensor(work[7][Q, 0, :], bank[2][Q, 0:CH], kind[Q, :], ALU.mult))
                d0, d1, o = keep[Q, :], work[7][Q, 0, :], work[6][Q, 0, :]
                if kind is last:
                    d0, d1, o = back(d0), back(d1), back(o)
                c.link(v.tensor_tensor_scan(o, d0, d1, 0.0, ALU.mult, ALU.add))
                v.sem_inc(S("sm_ownscan"), 1)
                v.wait_ge(S("sm_owncarry"), turn)
                c.link(v.tensor_copy(carry[Q, 3, 0:1], bank[3][Q, 0:1]))
                c.link(v.scalar_tensor_tensor(work[7][Q, 0, :], edge[Q, :], carry[Q, 3, 0:1], work[6][Q, 0, :],
                                              ALU.mult, ALU.add))
            v.wait_ge(S("sm_lg"), turn + 1)
            for r in range(2):
                o = lg[Q, :, r * P:(r + 1) * P]
                i_ = bank[r][Q, 0:nh * P].rearrange("p (h c) -> p h c", h=nh)
                if spread is not None:
                    c.do(v.tensor_tensor(o, i_, work[7][Q, :, r * P:(r + 1) * P], ALU.add))
                else:
                    c.do(v.tensor_copy(o, i_))
            c.hold()
            c.link(v.scalar_tensor_tensor(flat(lg), flat(lg), SLOPE, flat(lg), ALU.mult, ALU.max))
            scans(fm, penf, lg, -BIG, ALU.add, ALU.max, False)
            scans(bm_, penb, lg, -BIG, ALU.add, ALU.max, True)
            c.hold()
            v.sem_inc(S("sm_max"), 1)
            v.wait_ge(S("sm_maxrow"), turn + 1)
            for n, pen, b in ((0, linkbp, 4), (1, linkfp, 5)):
                for h in range(nh):
                    c.do(v.tensor_tensor(tot[Q, h, 0:NQ] if n == 0 else tot[Q, h, P:P + NQ],
                                         bank[b][Q, h * NQ:(h + 1) * NQ], pen[Q, :], ALU.add))
            c.hold()
            for n in range(2):
                c.do(v.tensor_reduce(carry[Q, n, 0:nh], tot[Q, :, n * P:n * P + NQ], X, ALU.max))
            c.link(v.tensor_tensor(flat(fm), flat(fm), flat(bm_), ALU.max))
            for n, edge in ((0, headp), (1, tailp)):
                for h in range(nh):
                    c.do(v.scalar_tensor_tensor(fm[Q, h, :], edge[Q, :], carry[Q, n, h:h + 1], fm[Q, h, :],
                                                ALU.add, ALU.max))
                c.hold()
            c.link(v.tensor_tensor(flat(lg), flat(lg), flat(fm), ALU.subtract))
            v.sem_inc(S("sm_centred"), 1)
            v.wait_ge(S("sm_exp"), turn + 1)
            scans(fs, keepf, ee, 0.0, ALU.mult, ALU.add, False)
            scans(bs_, keepb, ee, 0.0, ALU.mult, ALU.add, True)
            c.hold()
            v.sem_inc(S("sm_sum"), 1)
            c.link(v.tensor_tensor(flat(tot), flat(fs), flat(ee), ALU.subtract))
            c.link(v.tensor_tensor(flat(tot), flat(tot), flat(bs_), ALU.add))
            v.wait_ge(S("sm_sumcarry"), turn + 1)
            c.link(v.tensor_copy(carry[Q, 2, 0:nh], bank[6][Q, 0:nh]))
            c.link(v.tensor_copy(carry[Q, 3, 0:nh], bank[6][Q, nh:2 * nh]))
            for n, edge in ((2, head), (3, tail)):
                for h in range(nh):
                    c.do(v.scalar_tensor_tensor(tot[Q, h, :], edge[Q, :], carry[Q, n, h:h + 1], tot[Q, h, :],
                                                ALU.mult, ALU.add))
                c.hold()
            if guard:
                c.link(v.tensor_scalar(flat(tot), flat(tot), guard, None, ALU.add))
            c.link(v.reciprocal(flat(fs), flat(tot)))
            c.link(v.tensor_tensor(flat(ee), flat(ee), flat(fs), ALU.mult))
            v.sem_inc(S("sm_alpha"), 1)
            v.wait_ge(S("sm_back"), turn + 1)
            for r in range(2):
                c.do(v.tensor_copy(to.rearrange("p (q r) h -> p r h q", r=2)[:, r, :, :],
                                   bank[r][:, 0:nh * NQ].rearrange("p (h q) -> p h q", h=nh)))
            c.hold()

        def softmax_scalar(a, turn, nh, work):
            a.wait_ge(S("sm_centred"), turn + 1)
            nc.scalar.activation(work[3][Q].rearrange("p h c -> p (h c)"), work[0][Q].rearrange("p h c -> p (h c)"),
                                 ACT.Exp).then_inc(S("sm_exp"), 1)

        xmain = x[0:NJ * P, :].rearrange("(p j) f -> p j f", p=P)
        mains = [t[0:NJ * P, :].rearrange("(p j) f -> p j f", p=P) for t in (x1_t, x3_t, out)]

        def is_last(i):
            return isinstance(i, int) and i == BODIES

        def dense_k(i):
            return DLAST + 1 if is_last(i) else DK

        def before_of(i, j):
            return (i, j - 1) if j else (i - 1, RING - 1)

        def a_pool(pool):
            def step(i, j):
                count(pool, "a_tr", i, j, RING)
                slot_done(pool, "a_out", i, j, 16, 1)
                indices(pool, "a_ix", 2, i, j)
                pause(pool)
                gather(pool, lambda c: ring[:, j, 0, c, :], x, j, 0, S(f"a_in{j}"))
                gather(pool, lambda c: ring[:, j, 1, c, :], x, j, 1, S(f"a_in{j}"))
            groups(pool, step)

        def a_sync(sp):
            def load(i, j):
                s = j % 2
                count(sp, "n_u1", i, j, 2)
                count(sp, "n_tr", i, j, 2)
                if not is_last(i):
                    sp.dma_start(xin[s][:, :, :], xmain[:, bass.ds((RING * i + j) * DK, DK), :]) \
                        .then_inc(S(f"n_in{s}"), 32)
                else:
                    sp.dma_start(xin[s][:, 0:DLAST, :], xmain[:, NJ - DLAST:NJ, :]).then_inc(S(f"n_in{s}"), 16)
                    sp.dma_start(xin[s][0:NTAIL, DLAST, :], x[NJ * P:N, :]).then_inc(S(f"n_in{s}"), 16)

            def stores(i, j):
                wait(sp, f"a_in{j}", (i + 1) * 2 * GT * 16)
                sp.dma_start(xd_e[bass.ds(RING * i + j, 1)].rearrange("a p f -> (a p) f"), ringf[:, j, 1, :]) \
                    .then_inc(S(f"a_out{j}"), 16)
                for n in range(3):
                    count(sp, f"n_y{n}", i, j)
                    if not is_last(i):
                        sp.dma_start(mains[n][:, bass.ds((RING * i + j) * DK, DK), :], y[n][:, :, :]) \
                            .then_inc(S(f"n_out{n}"), 32)
                    else:
                        t = (x1_t, x3_t, out)[n]
                        sp.dma_start(mains[n][:, NJ - DLAST:NJ, :], y[n][:, 0:DLAST, :]).then_inc(S(f"n_out{n}"), 16)
                        sp.dma_start(t[NJ * P:N, :], y[n][0:NTAIL, DLAST, :]).then_inc(S(f"n_out{n}"), 16)

            load(0, 0)

            def step(i, j):
                if not is_last(i):
                    load(i, j + 1) if j + 1 < RING else load(i + 1, 0)
                stores(i, j)

            def whole():
                for j in range(RING):
                    step(0, j)
                with sp.Fori(1, BODIES - 1) as i:
                    for j in range(RING):
                        step(i, j)
                for j in range(RING):
                    step(BODIES - 1, j)
                step(BODIES, 0)
            whole()
            for j in range(RING):
                wait(sp, f"a_out{j}", 16 * (BODIES + (j == 0)))
            for n in range(3):
                wait(sp, f"n_out{n}", 32 * NG)

        def a_tensor(pe):
            def step(i, j):
                s = j % 2
                K = dense_k(i)
                wait(pe, f"n_in{s}", 32 * (2 * i + j // 2 + 1))
                count(pe, "n_xT", i, j, 1)
                for k in range(K):
                    ins = nc.tensor.transpose(bank[k // 4][:, (k % 4) * P:(k % 4 + 1) * P], xin[s][:, k, :], ident[:])
                ins.then_inc(S("n_tr"), 1)
                wait(pe, f"a_in{j}", (i + 1) * 2 * GT * 16)
                count(pe, "a_xT", i, j, 1)
                for n in range(2):
                    for c in range(GT):
                        ins = nc.tensor.transpose(bank[2 + n][:, c * P:(c + 1) * P], ring[:, j, n, c, :], ident[:])
                ins.then_inc(S("a_tr"), 1)
                count(pe, "n_xT", i, j)
                count(pe, "n_dots", i, j, 2)
                for k in range(K):
                    ins = nc.tensor.matmul(bank[4 + s][:, 4 * k:4 * k + 4], dxT[:, k * P:(k + 1) * P], bT[:],
                                           start=True, stop=True)
                ins.then_inc(S("n_mm"), 1)
                count(pe, "a_xT", i, j)
                count(pe, "a_feat", i, j, 2)
                for c in range(GT):
                    o = bank[6 + s][:, c * FW:(c + 1) * FW]
                    nc.tensor.matmul(o[:, 0:HF], xT[:, s, 0, c * P:(c + 1) * P], W1x[:, 0:HF], start=True, stop=True)
                    nc.tensor.matmul(o[:, HF:FW], xT[:, s, 0, c * P:(c + 1) * P], W1x[:, HF:FW],
                                     start=True, stop=False)
                    ins = nc.tensor.matmul(o[:, HF:FW], xT[:, s, 1, c * P:(c + 1) * P], W1r[:], start=False, stop=True)
                ins.then_inc(S("a_mm"), 1)
            groups(pe, step)

        def a_scalar(a):
            def evac(i, j):
                s = j % 2
                K = dense_k(i)
                count(a, "n_tr", i, j)
                count(a, "n_mm", i, j, 1)
                for b in range(2):
                    n = min(K - 4 * b, 4) * P
                    ins = nc.scalar.activation(dxT[:, b * 4 * P:b * 4 * P + n], bank[b][:, 0:n], ACT.Copy)
                ins.then_inc(S("n_xT"), 1)
                count(a, "a_tr", i, j)
                count(a, "a_mm", i, j, 2)
                for n in range(2):
                    ins = nc.scalar.activation(xT[:, s, n, :], bank[2 + n][:], ACT.Copy)
                ins.then_inc(S("a_xT"), 1)

            def apply(i, j):
                s = j % 2
                K = dense_k(i)
                for n, l in ((0, 0), (1, 2), (2, 3)):
                    count(a, f"n_u{l + 1}", i, j)
                    if not (isinstance(i, int) and i == 0 and j == 0):
                        wait(a, f"n_out{n}", 32 * (RING * i + j))
                    for k in range(K):
                        ins = nc.scalar.activation(y[n][:, k, :], u[l][:, k, :], ACT.Copy,
                                                   scale=rho[:, s, l, k:k + 1])
                    ins.then_inc(S(f"n_y{n}"), 1)

            def feats(i, j):
                s = j % 2
                count(a, "a_mm", i, j)
                pause(a)
                nc.scalar.activation(feat[:, four(RING * i + j), :],
                                     bank[6 + s][:, 0:GT * FW].rearrange("p (c f) -> p c f", f=FW), ACT.Copy) \
                    .then_inc(S("a_feat"), 1)

            def step(i, j):
                evac(i, j)
                if not (isinstance(i, int) and i == 0 and j == 0):
                    apply(*before_of(i, j))
                feats(i, j)
                for l in range(4):
                    wait(a, "n_var", (RING * i + j) * 4 + l + 1)
                    nc.scalar.activation(small[:, 9, :], small[:, 2, :], ACT.Sqrt, bias=epsc[:]) \
                        .then_inc(S("n_sd"), 1)
            groups(a, step)
            apply(BODIES, 0)

        def a_vector(v):
            c = Chain(v, "a_dve")
            index_first(v, "a_ix", (SRC, DST))

            def step(i, j):
                s = j % 2
                K = dense_k(i)
                c.at(i, j)
                if not is_last(i):
                    index_columns(v, "a_ix", (SRC, DST), "a_in", 2 * GT * 16, i, j)
                wait(v, f"n_in{s}", 32 * (2 * i + j // 2 + 1))
                xb = xin[s]
                for k in range(DK):
                    c.do(v.bn_stats(stats[:, k, :], xb[:, k, :]))
                c.hold()
                pause(v)
                for k in range(DK):
                    c.do(v.bn_aggr(mv[:, 1, k, :], stats[:, k, :]))
                c.hold()
                m_, var = mv[:, 1, :, 0], mv[:, 1, :, 1]
                count(v, "n_mm", i, j)
                if is_last(i):
                    K4 = K
                else:
                    K4 = DK
                c.link(v.tensor_scalar(small[:, 0, :], m_, -1.0, None, ALU.mult))
                v.tensor_copy(dots[:, 0:K4, :], bank[4 + s][:, 0:4 * K4].rearrange("p (k n) -> p k n", n=4)) \
                    .then_inc(S("n_dots"), 1)
                count(v, "n_dots", i, j)
                count(v, "n_y2", i, j, 2)
                w, rr = var, rho[:, s]
                for l in range(4):
                    B = [BB[:, 4 * l + n:4 * l + n + 1] for n in range(4)]
                    cl = dots[:, :, l]
                    c.link(v.scalar_tensor_tensor(small[:, 1, :], cl, 2.0, w, ALU.mult, ALU.add))
                    v.tensor_scalar(small[:, 2, :], small[:, 1, :], B[l], None, ALU.add).then_inc(S("n_var"), 1)
                    wait(v, "n_sd", (RING * i + j) * 4 + l + 1)
                    c.link(v.reciprocal(small[:, 3, :], small[:, 9, :]))
                    r = small[:, 3, :]
                    if l == 0:
                        c.do(v.tensor_copy(rr[:, 0, :], r))
                    else:
                        c.do(v.tensor_tensor(rr[:, l, :], rr[:, l - 1, :], r, ALU.mult))
                    for n in range(l + 1, 4):
                        c.do(v.scalar_tensor_tensor(dots[:, :, n], dots[:, :, n], B[n], r, ALU.add, ALU.mult))
                    c.do(v.tensor_tensor(small[:, 4, :], r, r, ALU.mult))
                    c.hold()
                    c.link(v.tensor_tensor(small[:, 5, :], small[:, 2, :], small[:, 4, :], ALU.mult))
                    w = small[:, 5, :]
                    if l < 3:
                        c.link(v.reciprocal(small[:, 6 + l, :], rr[:, l, :]))
                if not (isinstance(i, int) and i == 0 and j == 0):
                    count(v, "n_y2", i, j, 1)
                for l in range(4):
                    for k in range(DK):
                        if l == 0:
                            ins = v.scalar_tensor_tensor(u[0][:, k, :], xb[:, k, :], small[:, 0, k:k + 1],
                                                         biasc[:, 0, :], ALU.add, ALU.add)
                        else:
                            ins = v.scalar_tensor_tensor(u[l][:, k, :], biasc[:, l, :], small[:, 5 + l, k:k + 1],
                                                         u[l - 1][:, k, :], ALU.mult, ALU.add)
                    ins.then_inc(S(f"n_u{l + 1}"), 1)
                    if l < 3:
                        count(v, f"n_u{l + 1}", i, j)
            groups(v, step)

        def weigh(v, i, j, frm, width, heads, rev=False):
            s = j % 2
            g = RING * i + j
            if rev:
                g = NG - 1 - g
            if frm is None:
                slot_done(v, "h_xs", i, j, 16)
                pause(v)
                rowsv = ring[:, j, 0, :, 0:width]
            else:
                rowsv = frm[:, four(g), 0:width]
            o = msg[:, s, :, 0:width]
            if heads > 1:
                d = width // heads
                return v.tensor_tensor(o.rearrange("p t (h d) -> p t h d", h=heads),
                                       rowsv.rearrange("p t (h d) -> p t h d", h=heads),
                                       alpha[:, four(g), 0:heads].unsqueeze(3).to_broadcast([P, GT, heads, d]),
                                       ALU.mult)
            return v.tensor_tensor(o, rowsv, alpha[:, four(g), 0:1].to_broadcast([P, GT, width]), ALU.mult)

        def next_of(i, j):
            return (i, j + 1) if j + 1 < RING else (i + 1, 0)

        def scan_sum(v, tag, i, j, width, src_ap, dst_t, rev=False, op=None, c=None):
            s = j % 2
            g = RING * i + j
            m = cont[0:width, bass.ds(g * GE, GE)]
            o = dst_t[0:width, s, :]
            start = isinstance(i, int) and i == 0 and j == 0
            ini = 0.0 if start else (dst_t[0:width, 1 - s, 0:1] if rev else dst_t[0:width, 1 - s, GE - 1:GE])
            if rev:
                o, src_ap = o[:, ::-1], src_ap[:, ::-1]
            return v.tensor_tensor_scan(o, m, src_ap, ini, ALU.mult, ALU.add)

        def weighing(v, tag, frm, width, heads, rev=False):
            def stage(i, j):
                count(v, tag + "_tr", i, j, 2)
                pause(v)
                weigh(v, i, j, frm, width, heads, rev).then_inc(S(tag + "_msg"), 1)
            return stage

        def scanning(v, tag, width, rev=False):
            def stage(i, j):
                s = j % 2
                count(v, tag + "_tr", i, j)
                if not (isinstance(i, int) and i == 0 and j == 0):
                    count(v, tag + "_scan", i, j, 1)
                count(v, tag + "_mm", i, j, 2)
                scan_sum(v, tag, i, j, width, bank[s][0:width, :], G, rev).then_inc(S(tag + "_scan"), 1)
            return stage

        def b_vector(v):
            index_first(v, "b_ix", (LAST,))

            def split(i, j):
                s = j % 2
                count(v, "b_scan", i, j)
                v.tensor_scalar(hT[0:HF, s, 0, :], G[0:HF, s, :], b1c[:, 0:1], 0.0, ALU.add, ALU.max)
                v.tensor_scalar(hT[0:HF, s, 1, :], G[0:HF, s, :], b1c[:, 0:1], 0.0, ALU.add, ALU.min) \
                    .then_inc(S("b_min"), 1)

            def join(i, j):
                s = j % 2
                if not is_last(i):
                    index_columns(v, "b_ix", (LAST,), "b_sc", GT * 16, i, j)
                count(v, "b_mm", i, j, 2)
                count(v, "b_exp", i, j)
                v.scalar_tensor_tensor(hT[0:HF, s, 2, :], hT[0:HF, s, 1, :], -1.0, hT[0:HF, s, 0, :],
                                       ALU.add, ALU.add).then_inc(S("b_h"), 1)
            pipeline(v, [(-1, weighing(v, "b", feat, HF, HEADS)), (1, join), (0, scanning(v, "b", HF)), (0, split)])

        def turning(pe, tag, width):
            def stage(i, j):
                s = j % 2
                count(pe, tag + "_msg", i, j)
                count(pe, tag + "_scan", i, j, 2)
                pause(pe)
                for c in range(GT):
                    ins = nc.tensor.transpose(bank[s][0:width, c * P:(c + 1) * P], msg[:, s, c, 0:width], ident[:])
                ins.then_inc(S(tag + "_tr"), 1)
            return stage

        def b_tensor(pe):
            def project(i, j):
                s = j % 2
                count(pe, "b_h", i, j)
                count(pe, "b_er", i, j, 2)
                for c in range(GT):
                    ins = nc.tensor.matmul(bank[2 + s][:, c * (HF + 2):(c + 1) * (HF + 2)],
                                           hT[0:HF, s, 2, c * P:(c + 1) * P], W2x[:], start=True, stop=True)
                ins.then_inc(S("b_mm"), 1)
            pipeline(pe, [(0, turning(pe, "b", HF)), (1, project)])

        def b_scalar(a):
            def expo(i, j):
                s = j % 2
                count(a, "b_min", i, j)
                nc.scalar.activation(hT[0:HF, s, 1, :], hT[0:HF, s, 1, :], ACT.Exp).then_inc(S("b_exp"), 1)

            def rows(i, j):
                s = j % 2
                count(a, "b_mm", i, j)
                slot_done(a, "b_sc", i, j, GT * 16, 1)
                ps = bank[2 + s][:, 0:GT * (HF + 2)].rearrange("p (c f) -> p c f", f=HF + 2)
                nc.scalar.activation(outr[:, j, :, 0:HW], ps[:, :, 0:HW], ACT.Copy).then_inc(S("b_row"), 1)
                nc.scalar.activation(own[:, four(RING * i + j)], ps[:, :, HW], ACT.Copy).then_inc(S("b_er"), 1)
            pipeline(a, [(0, expo), (1, rows)])

        def b_pool(pool):
            def step(i, j):
                count(pool, "b_row", i, j)
                indices(pool, "b_ix", 1, i, j)
                pause(pool)
                scatter(pool, lambda c: outr[:, j, c, 0:HW], hidden_t, j, 0, S(f"b_sc{j}"))
            groups(pool, step)
            for j in range(RING):
                wait(pool, f"b_sc{j}", GT * 16 * (BODIES + (j == 0)))

        def c_pool(pool):
            def step(i, j):
                count(pool, "c_copy", i, j, RING)
                indices(pool, "c_ix", 1, i, j)
                pause(pool)
                gather(pool, lambda c: ring[:, j, 0, c, 0:HW], hidden_t, j, 0, S(f"c_in{j}"))
            groups(pool, step)

        def c_vector(v):
            index_first(v, "c_ix", (SRC,))

            def step(i, j):
                if not is_last(i):
                    index_columns(v, "c_ix", (SRC,), "c_in", GT * 16, i, j)
            groups(v, step)

        def c_scalar(a):
            def step(i, j):
                slot_done(a, "c_in", i, j, GT * 16)
                pause(a)
                nc.scalar.activation(feat[:, four(RING * i + j), 0:HF], ring[:, j, 0, :, 0:HF], ACT.Copy)
                nc.scalar.activation(logit[:, four(RING * i + j), 0], ring[:, j, 0, :, HF], ACT.Copy) \
                    .then_inc(S("c_copy"), 1)
            groups(a, step)

        def attend_vector(v, tag, frm, width, kind, rev):
            index_first(v, tag + "_ix", (kind,), rev)

            def scale(i, j):
                if not is_last(i):
                    index_columns(v, tag + "_ix", (kind,), tag + "_sc", GT * 16, i, j, rev)
                norm_scale(v, tag)(i, j)

            def residual(i, j):
                s = j % 2
                count(v, tag + "_mm", i, j)
                wait(v, f"{tag}_ld{s}", 16 * (2 * i + j // 2 + 1))
                count(v, tag + "_row", i, j, 2)
                v.tensor_tensor(z[:, s], bank[2 + s][:].rearrange("p (t f) -> p t f", f=F), xload[:, s], ALU.add) \
                    .then_inc(S(tag + "_z"), 1)
            pipeline(v, [(-1, weighing(v, tag, frm, width, 1, rev)), (2, scale), (0, scanning(v, tag, width, rev)),
                         (1, residual), (1, norm_stats(v, tag)), (1, norm_var(v, tag))])

        def attend_tensor(pe, tag, width, W, b):
            def project(i, j):
                s = j % 2
                count(pe, tag + "_scan", i, j)
                count(pe, tag + "_z", i, j, 2)
                nc.tensor.matmul(bank[2 + s][:], ones[0:1, 0:P], brow4[0:1, b, :], start=True, stop=False)
                for c in range(GT):
                    ins = nc.tensor.matmul(bank[2 + s][:, c * F:(c + 1) * F], G[0:width, s, c * P:(c + 1) * P], W[:],
                                           start=False, stop=(c == GT - 1))
                ins.then_inc(S(tag + "_mm"), 1)
            pipeline(pe, [(0, turning(pe, tag, width)), (1, project)])

        def attend_scalar(a, tag, stored):
            def step(i, j):
                s = j % 2
                norm_sqrt(a, tag, i, j)
                count(a, tag + "_st", i, j)
                slot_done(a, tag + "_sc", i, j, GT * 16, 1)
                if stored:
                    slot_done(a, tag + "_out", i, j, 16, 1)
                norm_apply(z[:, s], outr[:, j], rn[:, s]).then_inc(S(tag + "_row"), 1)
            groups(a, step)

        def attend_pool(pool, tag, table):
            def step(i, j):
                count(pool, tag + "_row", i, j)
                indices(pool, tag + "_ix", 1, i, j)
                pause(pool)
                scatter(pool, lambda c: outr[:, j, c, :], table, j, 0, S(f"{tag}_sc{j}"))
            groups(pool, step)
            for j in range(RING):
                wait(pool, f"{tag}_sc{j}", GT * 16 * (BODIES + (j == 0)))

        def edge_row(t, g):
            return t[bass.ds(g, 1)].rearrange("a p f -> (a p) f")

        def linear_sync(sp, tag, table, to, rev, used, more=None):
            def load(i, j):
                s = j % 2
                g = RING * i + j
                count(sp, tag + used, i, j, 2)
                sp.dma_start(xloadf[:, s, :], edge_row(table, NG - 1 - g if rev else g)) \
                    .then_inc(S(f"{tag}_ld{s}"), 16)

            def rows(i, j):
                g = RING * i + j
                count(sp, tag + "_msg", i, j, RING)
                sp.dma_start(ringf[:, j, 0, :], edge_row(more, NG - 1 - g if rev else g)) \
                    .then_inc(S(f"{tag}_xs{j}"), 16)

            def store(i, j):
                g = RING * i + j
                count(sp, tag + "_row", i, j)
                sp.dma_start(edge_row(to, NG - 1 - g if rev else g), outf[:, j, :]).then_inc(S(f"{tag}_out{j}"), 16)
            pipeline(sp, [(0, load), (3, store)] if more is None else [(-1, rows), (1, load)])
            if to is not None:
                for j in range(RING):
                    wait(sp, f"{tag}_out{j}", 16 * (BODIES + (j == 0)))

        def e_pool(pool):
            def step(i, j):
                count(pool, "e_tr", i, j, RING)
                indices(pool, "e_ix", 1, i, j)
                pause(pool)
                gather(pool, lambda c: ring[:, j, 0, c, :], x1_t, j, 0, S(f"e_in{j}"))
            groups(pool, step)

        def e_tensor(pe):
            def turn(i, j):
                s = j % 2
                slot_done(pe, "e_in", i, j, GT * 16)
                count(pe, "e_scan", i, j, 2)
                for c in range(GT):
                    ins = nc.tensor.transpose(bank[s][:, c * P:(c + 1) * P], ring[:, j, 0, c, :], ident[:])
                ins.then_inc(S("e_tr"), 1)

            def project(i, j):
                s = j % 2
                count(pe, "e_scan", i, j)
                count(pe, "e_zp", i, j, 2)
                for c in range(GT):
                    ins = nc.tensor.matmul(bank[2 + s][:, c * F:(c + 1) * F], G[:, s, c * P:(c + 1) * P], L1T[:],
                                           start=True, stop=True)
                ins.then_inc(S("e_mm"), 1)
            pipeline(pe, [(0, turn), (1, project)])

        def e_vector(v):
            index_first(v, "e_ix", (SRC,))

            def columns(i, j):
                if not is_last(i):
                    index_columns(v, "e_ix", (SRC,), "e_in", GT * 16, i, j)

            def residual(i, j):
                s = j % 2
                g = RING * i + j
                count(v, "e_mm", i, j)
                wait(v, f"e_ld{s}", 16 * (2 * i + j // 2 + 1))
                count(v, "e_row", i, j, 2)
                for k in range(GT):
                    ins = v.scalar_tensor_tensor(z[:, s, k, :], bank[2 + s][:, k * F:(k + 1) * F],
                                                 invR[:, bass.ds(g * GT + k, 1)], xload[:, s, k, :],
                                                 ALU.mult, ALU.add)
                ins.then_inc(S("e_zp"), 1)
                count(v, "e_zp", i, j)
                v.tensor_tensor(z[:, s], z[:, s], bias[:, 1:2, :].to_broadcast([P, GT, F]), ALU.add) \
                    .then_inc(S("e_z"), 1)
            pipeline(v, [(0, columns), (2, norm_scale(v, "e", True)), (0, scanning(v, "e", P)), (1, residual),
                         (1, norm_stats(v, "e")), (1, norm_var(v, "e"))])

        def e_scalar(a):
            def step(i, j):
                s = j % 2
                norm_sqrt(a, "e", i, j)
                count(a, "e_st", i, j)
                slot_done(a, "e_out", i, j, 16, 1)
                norm_apply(z[:, s], outr[:, j], rn[:, s]).then_inc(S("e_row"), 1)
            groups(a, step)

        eaR = ring[:, 0:2, 1, :, 0:EF]

        def f_sync(sp):
            sp.dma_start(cont[:].rearrange("p (q c) -> p q c", c=CH),
                         cont_d[1, :].rearrange("(q c) -> q c", c=CH)[::-1, :].partition_broadcast(P)) \
                .then_inc(S("cont_in"), 16)
            def load(i, j):
                s = j % 2
                g = NG - 1 - (RING * i + j)
                count(sp, "f_tr", i, j, 2)
                sp.dma_start(ring[:, s, 0].rearrange("p t f -> p (t f)"), edge_row(x2_e, g)) \
                    .then_inc(S(f"f_x{s}"), 16)
                if isinstance(i, int) and i == 0 and j == 0:
                    full = (E - (NG - 1) * GE) // P
                    base = (NG - 1) * GE
                    wait(sp, "f_pad", 1)
                    sp.dma_start(eaR[:, s, 0:full, :], ea[base:base + full * P, :].rearrange("(c p) f -> p c f", p=P)) \
                        .then_inc(S(f"f_ea{s}"), 16)
                    sp.dma_start(eaR[0:E - base - full * P, s, full, :], ea[base + full * P:E, :]) \
                        .then_inc(S(f"f_ea{s}"), 16)
                else:
                    sp.dma_start(eaR[:, s], ea[bass.ds(g * GE, GE), :].rearrange("(c p) f -> p c f", p=P)) \
                        .then_inc(S(f"f_ea{s}"), 32)

            def store(i, j):
                g = NG - 1 - (RING * i + j)
                count(sp, "f_row", i, j)
                sp.dma_start(edge_row(x3_e, g), outf[:, j, :]).then_inc(S(f"f_out{j}"), 16)
            pipeline(sp, [(0, load), (4, store)])
            for j in range(RING):
                wait(sp, f"f_out{j}", 16 * (BODIES + (j == 0)))

        def f_tensor(pe):
            def turn(i, j):
                s = j % 2
                uses = 2 * i + j // 2 + 1
                wait(pe, f"f_x{s}", 16 * uses)
                wait(pe, f"f_ea{s}", 32 * uses)
                count(pe, "f_spread", i, j, 1)
                for c in range(GT):
                    nc.tensor.transpose(bank[0][:, c * P:(c + 1) * P], ring[:, s, 0, c, :], ident[:])
                count(pe, "f_eaT", i, j, 1)
                pause(pe)
                for c in range(GT):
                    ins = nc.tensor.transpose(bank[1][0:EF, c * P:(c + 1) * P], eaR[:, s, c, :], ident[:])
                ins.then_inc(S("f_tr"), 1)

            def hidden(i, j):
                s = j % 2
                count(pe, "f_spread", i, j)
                count(pe, "f_eaT", i, j)
                count(pe, "f_relu", i, j, 1)
                nc.tensor.matmul(bank[2][:], M1a[:], X2T[:, j, :], start=True, stop=False)
                nc.tensor.matmul(bank[2][:], M1b[:], eaT[:, s, :], start=False, stop=True).then_inc(S("f_m1"), 1)

            def message(i, j):
                s = j % 2
                count(pe, "f_relu", i, j)
                count(pe, "f_msg", i, j, 1)
                nc.tensor.matmul(bank[3][:], M2_s[:], hT[:, s, 0, :], start=True, stop=True).then_inc(S("f_m2"), 1)

            def combine(i, j):
                s = j % 2
                count(pe, "f_max", i, j)
                count(pe, "f_aT", i, j, 1)
                count(pe, "f_bT", i, j, 1)
                nc.tensor.matmul(bank[4][:], Mm_s[:], G[:, s, :], start=True, stop=True)
                nc.tensor.matmul(bank[5][:], Ms_s[:], G[:, s, :], start=True, stop=False)
                nc.tensor.matmul(bank[5][:], Mx_s[:], MX[:, s, :], start=False, stop=True).then_inc(S("f_mm2"), 1)

            def rows(i, j):
                s = j % 2
                count(pe, "f_aT", i, j)
                count(pe, "f_bT", i, j)
                count(pe, "f_zA", i, j, 1)
                count(pe, "f_z", i, j, 1)
                for n, t in ((6, aT), (7, bT2)):
                    for c in range(GT):
                        ins = nc.tensor.transpose(bank[n][:, c * P:(c + 1) * P], t[:, s, c * P:(c + 1) * P], ident[:])
                ins.then_inc(S("f_back"), 1)
            pipeline(pe, [(0, hidden), (-1, turn), (0, message), (2, rows), (1, combine)])

        def f_scalar(a):
            def relu(i, j):
                s = j % 2
                count(a, "f_m1", i, j)
                count(a, "f_m2", i, j, 2)
                nc.scalar.activation(hT[:, s, 0, :], bank[2][:], ACT.Relu, bias=m1c[:]).then_inc(S("f_relu"), 1)

            def edges(i, j):
                s = j % 2
                count(a, "f_tr", i, j)
                count(a, "f_m1", i, j, 2)
                nc.scalar.activation(eaT[:, s, :], bank[1][0:EF, :], ACT.Copy).then_inc(S("f_eaT"), 1)

            def message(i, j):
                s = j % 2
                count(a, "f_m2", i, j)
                count(a, "f_max", i, j, 2)
                nc.scalar.activation(hT[:, s, 1, :], bank[3][:], ACT.Identity, bias=m2c[:]).then_inc(S("f_msg"), 1)

            def means(i, j):
                s = j % 2
                g = NG - 1 - (RING * i + j)
                count(a, "f_back", i, j)
                count(a, "f_z", i, j, 2)
                pause(a)
                for c in range(GT):
                    ins = nc.scalar.activation(zA[:, s, c, :], bank[6][:, c * F:(c + 1) * F], ACT.Copy,
                                               scale=invR[:, bass.ds(g * GT + c, 1)])
                ins.then_inc(S("f_zA"), 1)

            def columns(i, j):
                s = j % 2
                count(a, "f_mm2", i, j)
                count(a, "f_back", i, j, 2)
                nc.scalar.activation(aT[:, s, :], bank[4][:], ACT.Copy).then_inc(S("f_aT"), 1)

            def root(i, j):
                norm_sqrt(a, "f", i, j)

            def apply(i, j):
                s = j % 2
                count(a, "f_st", i, j)
                slot_done(a, "f_sc", i, j, GT * 16, 1)
                slot_done(a, "f_out", i, j, 16, 1)
                norm_apply(z[:, s], outr[:, j], rn[:, s]).then_inc(S("f_row"), 1)
            pipeline(a, [(0, relu), (-1, edges), (0, message), (3, apply), (2, means), (1, columns), (2, root)])

        def f_vector(v):
            v.memset(eaR[:, 0], 0.0).then_inc(S("f_pad"), 1)
            index_first(v, "f_ix", (FIRST,), True)

            def scale(i, j):
                if not is_last(i):
                    index_columns(v, "f_ix", (FIRST,), "f_sc", GT * 16, i, j, True)
                norm_scale(v, "f")(i, j)

            def spread(i, j):
                start = isinstance(i, int) and i == 0 and j == 0
                if start:
                    v.wait_ge(S("cont_in"), 32)
                else:
                    count(v, "f_spread", i, j, 1)
                count(v, "f_tr", i, j)
                count(v, "f_m1", i, j, RING)
                m = cont[:, bass.ds((RING * i + j) * GE, GE)]
                ini = 0.0 if start else X2T[:, (j - 1) % RING, 0:1]
                v.tensor_tensor_scan(X2T[:, j, ::-1], m, bank[0][:, ::-1], ini, ALU.mult, ALU.add) \
                    .then_inc(S("f_spread"), 1)

            def penalty(i, j):
                m = cont[:, bass.ds((RING * i + j) * GE, GE)]
                count(v, "f_max", i, j, 2)
                pause(v)
                v.tensor_scalar(neg[:, j % 2, :], m, -1.0, -FAR, ALU.add, ALU.mult).then_inc(S("f_neg"), 1)

            def totals(i, j):
                s = j % 2
                start = isinstance(i, int) and i == 0 and j == 0
                count(v, "f_msg", i, j)
                count(v, "f_mm2", i, j, 2)
                if not start:
                    count(v, "f_sum", i, j, 1)
                scan_sum(v, "f", i, j, P, hT[:, s, 1, :], G, True).then_inc(S("f_sum"), 1)
                count(v, "f_neg", i, j)
                if not start:
                    count(v, "f_max", i, j, 1)
                ini = FAR if start else MX[:, 1 - s, 0:1]
                v.tensor_tensor_scan(MX[:, s, ::-1], neg[:, s, :], hT[:, s, 1, ::-1], ini, ALU.add, ALU.max) \
                    .then_inc(S("f_max"), 1)

            def columns(i, j):
                s = j % 2
                count(v, "f_mm2", i, j)
                count(v, "f_back", i, j, 2)
                v.scalar_tensor_tensor(bT2[:, s, :], bank[5][:], m3c[:], X2T[:, j, :], ALU.add, ALU.add) \
                    .then_inc(S("f_bT"), 1)

            def residual(i, j):
                s = j % 2
                count(v, "f_back", i, j)
                count(v, "f_zA", i, j)
                count(v, "f_row", i, j, 2)
                v.tensor_tensor(z[:, s], bank[7][:].rearrange("p (t f) -> p t f", f=F), zA[:, s], ALU.add) \
                    .then_inc(S("f_z"), 1)
            pipeline(v, [(3, scale), (-1, spread), (0, penalty), (2, residual), (2, norm_stats(v, "f")), (0, totals),
                         (2, norm_var(v, "f")), (1, columns)])

        def g_pool(pool):
            def step(i, j):
                slot_done(pool, "g_out", i, j, 16, 1)
                count(pool, "g_dot", i, j, RING)
                indices(pool, "g_ix", 1, i, j)
                pause(pool)
                gather(pool, lambda c: ring[:, j, 0, c, :], x3_t, j, 0, S(f"g_in{j}"))
            groups(pool, step)

        def g_vector(v):
            c = Chain(v, "g_dve")
            index_first(v, "g_ix", (SRC,))

            def step(i, j):
                s = j % 2
                g = RING * i + j
                c.at(i, j)
                if not is_last(i):
                    index_columns(v, "g_ix", (SRC,), "g_in", GT * 16, i, j)
                wait(v, f"g_ld{s}", 16 * (2 * i + j // 2 + 1))
                slot_done(v, "g_in", i, j, GT * 16)
                for n in range(2):
                    for k in range(GT):
                        frm = ring[:, j, 0, k, :] if n else xload[:, s, k, :]
                        c.do(v.tensor_tensor_reduce(msg[:, n, k, :], frm, attb[:, n, :], 1.0, 0.0, ALU.mult, ALU.add,
                                                    dots[:, k, n:n + 1]))
                c.hold()
                pause(v)
                v.tensor_copy(own[:, four(g)], dots[:, 0:GT, 0])
                v.tensor_copy(logit[:, four(g), 0], dots[:, 0:GT, 1]).then_inc(S("g_dot"), 1)
                count(v, "g_dot", i, j)
            groups(v, step)

        def g_sync(sp):
            def load(i, j):
                s = j % 2
                count(sp, "g_dot", i, j, 2)
                sp.dma_start(xloadf[:, s, :], edge_row(x3_e, RING * i + j)).then_inc(S(f"g_ld{s}"), 16)
            load(0, 0)

            def step(i, j):
                if not is_last(i):
                    load(*next_of(i, j))
                slot_done(sp, "g_in", i, j, GT * 16)
                sp.dma_start(edge_row(xs_e, RING * i + j), ringf[:, j, 0, :]).then_inc(S(f"g_out{j}"), 16)
            groups(sp, step)
            for j in range(RING):
                wait(sp, f"g_out{j}", 16 * (BODIES + (j == 0)))

        block = ctx.enter_context(nc.Block())

        @block.sync
        def _(sp):
            prep_sync(sp)
            assert prep_sync.loads == LOADS
            barrier(sp)
            a_sync(sp)
            barrier(sp)
            barrier(sp)
            barrier(sp)
            barrier(sp)
            linear_sync(sp, "d", xd_e, x1_e, False, "_z")
            barrier(sp)
            linear_sync(sp, "e", x1_e, x2_e, False, "_z")
            barrier(sp)
            f_sync(sp)
            barrier(sp)
            g_sync(sp)
            barrier(sp)
            linear_sync(sp, "h", x3_e, None, True, "_z", xs_e)
            barrier(sp)

        @block.gpsimd
        def _(pool):
            prep_pool(pool)
            barrier(pool)
            a_pool(pool)
            barrier(pool)
            b_pool(pool)
            barrier(pool)
            c_pool(pool)
            barrier(pool)
            barrier(pool)
            attend_pool(pool, "d", x1_t)
            barrier(pool)
            e_pool(pool)
            barrier(pool)
            attend_pool(pool, "f", x3_t)
            barrier(pool)
            g_pool(pool)
            barrier(pool)
            attend_pool(pool, "h", out)
            barrier(pool)

        @block.tensor
        def _(pe):
            prep_tensor(pe)
            barrier(pe)
            a_tensor(pe)
            barrier(pe)
            softmax_tensor(pe, 0, HEADS, feat[:, :, HF:FW], wide, None)
            b_tensor(pe)
            barrier(pe)
            barrier(pe)
            softmax_tensor(pe, 1, 1, logit[:, :, 0:1], slim, (last,))
            barrier(pe)
            attend_tensor(pe, "d", HF, W2_s, 0)
            barrier(pe)
            e_tensor(pe)
            barrier(pe)
            f_tensor(pe)
            barrier(pe)
            barrier(pe)
            softmax_tensor(pe, 2, 1, logit[:, :, 0:1], slim, (first,))
            attend_tensor(pe, "h", P, W3_s, 1)
            barrier(pe)

        @block.scalar
        def _(a):
            prep_scalar(a)
            barrier(a)
            a_scalar(a)
            barrier(a)
            softmax_scalar(a, 0, HEADS, wide)
            b_scalar(a)
            barrier(a)
            c_scalar(a)
            barrier(a)
            softmax_scalar(a, 1, 1, slim)
            barrier(a)
            attend_scalar(a, "d", True)
            barrier(a)
            e_scalar(a)
            barrier(a)
            f_scalar(a)
            barrier(a)
            barrier(a)
            softmax_scalar(a, 2, 1, slim)
            attend_scalar(a, "h", False)
            barrier(a)

        @block.vector
        def _(v):
            prep_vector(v)
            barrier(v)
            a_vector(v)
            barrier(v)
            softmax_vector(v, 0, HEADS, wide, None, None, alpha[:, :, 0:HEADS])
            b_vector(v)
            barrier(v)
            c_vector(v)
            barrier(v)
            softmax_vector(v, 1, 1, slim, (last,), None, alpha[:, :, 0:1])
            barrier(v)
            attend_vector(v, "d", feat, HF, LAST, False)
            barrier(v)
            e_vector(v)
            barrier(v)
            f_vector(v)
            barrier(v)
            g_vector(v)
            barrier(v)
            softmax_vector(v, 2, 1, slim, (first,), 1e-16, alpha[:, :, 0:1])
            attend_vector(v, "h", None, P, FIRST, True)
            barrier(v)


_INS = ['x', 'src', 'dst', 'edge_attr_64', 'L0_gnn_W1', 'L0_gnn_al1', 'L0_gnn_ar1', 'L0_gnn_b1', 'L0_gnn_W2',
        'L0_gnn_al2', 'L0_gnn_ar2', 'L0_gnn_b2', 'L1_gnn_W', 'L1_gnn_b', 'L2_gnn_W1', 'L2_gnn_b1', 'L2_gnn_W2',
        'L2_gnn_b2', 'L2_gnn_Wm', 'L2_gnn_bm', 'L2_gnn_Wx', 'L2_gnn_bx', 'L2_gnn_Ws', 'L2_gnn_bs', 'L3_gnn_W',
        'L3_gnn_att', 'L3_gnn_bias']


def kernel(**inputs):
    import numpy as _np
    import concourse.bacc as _bacc
    from concourse import mybir as _mybir
    from concourse.bass_utils import run_bass_kernel_spmd as _run

    nc = _bacc.Bacc("TRN2", target_bir_lowering=False, num_devices=1)
    arrays, args = {}, []
    for name in _INS:
        a = _np.ascontiguousarray(inputs[name])
        arrays[f"in_{name}_dram"] = a
        args.append(nc.dram_tensor(f"in_{name}_dram", a.shape, _mybir.dt.from_np(a.dtype), kind="ExternalInput").ap())
    args.append(nc.dram_tensor("out_0_dram", (N, F), _mybir.dt.float32, kind="ExternalOutput").ap())
    program(nc, *args)
    r = _run(nc, [arrays], core_ids=[0])
    return r.results[0]["out_0_dram"]
```

```python
from contextlib import ExitStack

import concourse.bass as bass
from concourse import mybir

F32 = mybir.dt.float32
BF16 = mybir.dt.bfloat16
I32 = mybir.dt.int32
U32 = mybir.dt.uint32
U8 = mybir.dt.uint8
ALU = mybir.AluOpType
ACT = mybir.ActivationFunctionType
X = mybir.AxisListType.X

P = 128
N, E, F = 50000, 25000, 128
HEADS, HID = 4, 16
HF = HEADS * HID
FW = HF + HEADS
PW = FW + HEADS
HW = HF + 1
EF = 64
GT = 4
GE = GT * P
NG = -(-E // GE)
NT = NG * GT
CH = 2 * P
NQ = NT * P // CH
EP = NT * P
RING = 4
BODIES = NG // RING
NJ = N // P
NTAIL = N - NJ * P
DK = 8
DH = DK // 2
DP = 4
DC = NG * DK
DTAIL = NJ - (2 * NG - 1) * DH
DLAST = NJ - (NG - 1) * DK
SKIP = 1 << 16
BIG = 1.0e38
FAR = -3.0e38
EPS = 1e-5
SLOPE = 0.2
assert NG % RING == 1 and NQ * 2 == NT and 0 < DLAST < DK and DK * F == 2 * GE


def program(nc, x, src, dst, ea, W1, al1, ar1, b1, W2, al2, ar2, b2, L1W, L1b,
            M1, m1, M2, m2, Mm, bm, Mx, bx, Ms, bs, W3, att, b4, out):
    def dram(name, shape, dt=F32):
        return nc.dram_tensor(name, shape, dt, kind="Internal").ap()

    hidden_t = dram("hidden_t", (N, HW))
    x1_t = dram("x1_t", (N, F))
    x3_t = dram("x3_t", (N, F))
    xd_e = dram("xd_e", (NG, P, GT * F))
    x1_e = dram("x1_e", (NG, P, GT * F))
    x2_e = dram("x2_e", (NG, P, GT * F))
    x3_e = dram("x3_e", (NG, P, GT * F))
    xs_e = dram("xs_e", (NG, P, GT * F))
    cont_d = dram("cont_d", (2, EP), U8)

    with ExitStack() as ctx:
        def sb(name, shape, dt=F32):
            return ctx.enter_context(nc.sbuf_tensor(name, shape, dt))

        def sem(name):
            return ctx.enter_context(nc.semaphore(name))

        bank = [ctx.enter_context(nc.psum_tensor(f"bank{n}", [P, 512], F32)) for n in range(8)]

        ident = sb("ident", [P, P])
        before = sb("before", [P, NQ])
        after = sb("after", [P, NQ])
        ones = sb("ones", [P, P])
        W1x = sb("W1x", [P, FW])
        W1r = sb("W1r", [P, HEADS])
        W2_s = sb("W2_s", [HF + 1, F])
        W2x = sb("W2x", [HF, HF + 2])
        L1T = sb("L1T", [P, F])
        raw = sb("raw", [P, F])
        M1a = sb("M1a", [P, F])
        M1b = sb("M1b", [EF, F])
        M2_s = sb("M2_s", [P, F])
        Mm_s = sb("Mm_s", [P, F])
        Mx_s = sb("Mx_s", [P, F])
        Ms_s = sb("Ms_s", [P, F])
        W3_s = sb("W3_s", [P, F])
        W3T = sb("W3T", [P, F])
        bias = sb("bias", [P, 4, F])
        biasc = sb("biasc", [P, 4, F])
        brow = sb("brow", [1, GT * F])
        m3c = sb("m3c", [P, 1])
        bT = sb("bT", [P, 4])
        BB = sb("BB", [P, 16])
        tmpw = sb("tmpw", [P, F])
        b1c = sb("b1c", [HF, 4])
        m1c = sb("m1c", [P, 1])
        m2c = sb("m2c", [P, 1])
        attc = sb("attc", [P, 2])
        attb = sb("attb", [P, 2, F])
        hcol = sb("hcol", [HF, P])
        hconst = sb("hconst", [P, DK, HW])
        wmean = sb("wmean", [P, 4])

        cv = sb("cv", [P, 10, CH])
        first = sb("first", [P, CH])
        last = sb("last", [P, CH])
        contb = sb("contb", [P, 2, CH], U8)
        keepf = sb("keepf", [P, CH])
        keepb = sb("keepb", [P, CH])
        penf = sb("penf", [P, CH])
        penb = sb("penb", [P, CH])
        head = sb("head", [P, CH])
        tail = sb("tail", [P, CH])
        headp = sb("headp", [P, CH])
        tailp = sb("tailp", [P, CH])
        linkf = sb("linkf", [P, NQ])
        linkb = sb("linkb", [P, NQ])
        linkfp = sb("linkfp", [P, NQ])
        linkbp = sb("linkbp", [P, NQ])
        endd = sb("endd", [P, 2])
        cont = sb("cont", [P, EP], U8)
        idx = sb("idx", [P, 4, NT + 8], I32)
        SRC, DST, LAST, FIRST = range(4)
        lastR = sb("lastR", [P, NT])
        invR = sb("invR", [P, NT])
        ixr = sb("ixr", [P, RING, 2, GT], I32)

        big = sb("big", [P, NT * FW + 2 * GE])
        feat = big[:, 0:NT * FW].rearrange("p (t f) -> p t f", f=FW)
        def part(start, n):
            return big[:, start * GE:start * GE + n]

        bload = part(0, 2 * F).rearrange("p (n f) -> p n f", f=F)
        alb = part(1, 2 * F).rearrange("p (n f) -> p n f", f=F)
        e_src, e_dst, e_prev, e_next = (part(2 + n, CH).bitcast(I32) for n in range(4))
        X2T = part(9, 4 * GE).rearrange("p (s e) -> p s e", s=4)
        aT = part(13, 2 * GE).rearrange("p (s e) -> p s e", s=2)
        bT2 = part(15, 2 * GE).rearrange("p (s e) -> p s e", s=2)
        MX = part(2, 2 * GE).rearrange("p (s e) -> p s e", s=2)
        zA = part(4, 2 * GE).rearrange("p (s t f) -> p s t f", s=2, f=F)
        eaT = part(6, 2 * GE)[0:EF].rearrange("p (s e) -> p s e", s=2)
        neg = part(8, GE).bitcast(BF16).rearrange("p (s e) -> p s e", s=2)
        slim = [cv[:, n:n + 1, :] for n in range(9)]
        xload = sb("xload", [P, 2, GT, F])
        xloadf = xload[:, :, :, :].rearrange("p r t f -> p r (t f)")
        ring = sb("ring", [P, RING, 2, GT, F])
        ringf = ring[:, :, :, :, :].rearrange("p r a t f -> p r a (t f)")
        outr = sb("outr", [P, RING, GT, F])
        outf = outr[:, :, :, :].rearrange("p r t f -> p r (t f)")
        xT = sb("xT", [P, 2, 2, GE])
        xlast = sb("xlast", [P, DK, F])
        msg = sb("msg", [P, 2, GT, F])
        G = sb("G", [P, 2, GE])
        z = sb("z", [P, 2, GT, F])
        hT = sb("hT", [P, 2, 3, GE])
        blocks = [t.rearrange("p n -> p n") for t in (
            msg[:, :, :, :].rearrange("p s t f -> p (s t f)"), G[:, :, :].rearrange("p s e -> p (s e)"),
            z[:, :, :, :].rearrange("p s t f -> p (s t f)"), xload[:, :, :, :].rearrange("p s t f -> p (s t f)"),
            outf[:, 0:2, :].rearrange("p s e -> p (s e)"), outf[:, 2:4, :].rearrange("p s e -> p (s e)"),
            big[:, NT * FW:NT * FW + 2 * GE],
            xT[:, 0, :, :].rearrange("p n e -> p (n e)"), xT[:, 1, :, :].rearrange("p n e -> p (n e)"),
            hT[:, 0, 0:2, :].rearrange("p n e -> p (n e)"), hT[:, 1, 0:2, :].rearrange("p n e -> p (n e)"))]
        wide = [blocks[n].rearrange("p (h c) -> p h c", h=HEADS) for n in (0, 1, 2, 9, 4, 5, 6)]
        kf = [t.rearrange("p (k f) -> p k f", f=F) for t in blocks]
        y = (kf[0:2], kf[2:4])
        y4 = [xT[:, n // 2, n % 2, :].rearrange("p (k f) -> p k f", f=F) for n in range(RING)]
        s23 = kf[7]
        xin = (kf[6], kf[9], kf[10], xlast[:])
        dxT = blocks[0][:, 0:DP * F]
        waste = (kf[1], kf[2])
        stat = blocks[3][:, 0:2 * DC].rearrange("p (c n) -> p c n", n=2)
        cross = sb("cross", [P, DC, 4])
        temps = [blocks[n][:, h * GE:h * GE + DC] for n in (7, 8) for h in range(2)]
        rates = cv[:, :, :].rearrange("p n c -> p (n c)")[:, 0:4 * DC].rearrange("p (n c) -> p n c", n=4)
        rate4 = cross[:, :, 0]
        rate = sb("rate", [P, RING, 4, DK])
        sd = sb("sd", [P, DK])
        epsc = sb("epsc", [P, 1])
        stats = sb("stats", [P, DK, 6])
        mv = sb("mv", [P, 2, DK, 2])
        rn = sb("rn", [P, 2, GT, 2])
        dots = sb("dots", [P, GT, 2])
        dotv = sb("dotv", [P, 2, DK - DP, 4])
        logit = sb("logit", [P, NT, 1])
        alpha = sb("alpha", [P, NT, HEADS])
        own = sb("own", [P, NT])
        carry = sb("carry", [P, 4, HEADS])
        R1 = G

        idle = sem("idle")
        phase = sem("phase")
        sems = {}

        def sem_of(name):
            if name not in sems:
                sems[name] = sem(name)
            return sems[name]

        def S(name):
            return sem_of(shared(name)[0])

        SHARED = {
            "in": (4, {"a": 2 * GT * 16, "c": GT * 16, "e": GT * 16, "g": GT * 16}),
            "out": (4, {"a": 16, "d": 16, "e": 16, "f": 16, "g": 16}),
            "sc": (4, {"b": GT * 16, "d": GT * 16, "f": GT * 16, "h": GT * 16}),
            "ld": (2, {"d": 16, "e": 16, "g": 16, "h": 16}),
            "ix": (1, {"a": 2, "b": 1, "c": 1, "d": 1, "e": 1, "f": 1, "g": 1, "h": 1}),
            "tr": (1, {"a": 1, "b": 1, "d": 1, "e": 1, "f": 1, "h": 1}),
            "scan": (1, {"b": 1, "d": 1, "e": 1, "h": 1}),
            "mm": (1, {"a": 1, "b": 1, "d": 1, "e": 1, "h": 1}),
            "z": (1, {"d": 1, "e": 1, "f": 1, "h": 1}),
            "din": (4, {"n": 32, "m": 32}),
            "var": (1, {"d": 1, "e": 1, "f": 1, "h": 1}),
            "sd": (1, {"d": 1, "e": 1, "f": 1, "h": 1}),
            "bn": (1, {"d": 1, "e": 1, "f": 1, "h": 1}),
            "rc": (1, {"d": 1, "e": 1, "f": 1, "h": 1}),
            "st": (1, {"d": 1, "e": 1, "f": 1, "h": 1}),
            "row": (1, {"b": 1, "d": 1, "e": 1, "f": 1, "h": 1}),
            "msg": (1, {"b": 1, "d": 1, "f": 1, "h": 1}),
        }

        def shared(name):
            tag, _, kind = name.partition("_")
            slot = kind[-1] if kind[-1:].isdigit() else ""
            kind = kind[:-1] if slot else kind
            ways, users = SHARED.get(kind, (0, {}))
            if tag not in users or bool(slot) != (ways > 1):
                return name, 0
            uses = len(range(int(slot), NG, ways)) if slot else NG + (kind == "ix")
            start = 0
            for t, per in users.items():
                if t == tag:
                    return "g_" + kind + slot, start
                start += per * uses

        def wait(eng, name, n):
            sem_name, start = shared(name)
            eng.wait_ge(sem_of(sem_name), n + start)
            if eng is nc.sync and not isinstance(n, int):
                pause(eng)

        def pause(eng):
            eng.sem_inc(idle, 1)

        phases = {}

        def arrive(eng):
            phases[eng] = phases.get(eng, 0) + 1
            eng.drain().then_inc(phase, 1)

        def barrier(eng):
            arrive(eng)
            eng.wait_ge(phase, 5 * phases[eng])

        def groups(eng, step):
            for j in range(RING):
                step(0, j)
            with eng.Fori(1, BODIES) as i:
                for j in range(RING):
                    step(i, j)
            step(BODIES, 0)

        def pipeline(eng, stages, between=()):
            least, most = min(lag for lag, _ in stages), max(lag for lag, _ in stages)

            def fixed(g):
                for lag, stage in stages:
                    if 0 <= g - lag < NG:
                        stage((g - lag) // RING, (g - lag) % RING)
            for g in range(least, RING):
                fixed(g)
            parts = max(len(between), 1)
            for n in range(parts):
                with eng.Fori(1 + (BODIES - 1) * n // parts, 1 + (BODIES - 1) * (n + 1) // parts) as i:
                    for j in range(RING):
                        for lag, stage in stages:
                            stage(i + (j - lag) // RING, (j - lag) % RING)
                if between:
                    between[n]()
            for g in range(NG - 1, NG + most):
                fixed(g)

        def count(eng, name, i, j, lag=0, per=1):
            n = RING * i + j + 1 - lag
            if isinstance(n, int) and n <= 0:
                return
            wait(eng, name, n * per)

        def slot_done(eng, name, i, j, per, lag=0):
            n = i + 1 - lag
            if isinstance(n, int) and n <= 0:
                return
            wait(eng, f"{name}{j}", n * per)

        class Chain:

            def __init__(self, eng, name):
                self.eng, self.sem, self.n, self.base, self.per = eng, S(name), 0, 0, None

            def at(self, i, j):
                if self.per is None and not (i == 0 and j == 0 and isinstance(i, int)):
                    self.per = self.n
                if self.per is not None:
                    assert self.n == self.per, (self.n, self.per)
                    self.base = (RING * i + j) * self.per
                self.n = 0

            def do(self, ins):
                ins.then_inc(self.sem, 1)
                self.n += 1
                return ins

            def hold(self):
                self.eng.wait_ge(self.sem, self.base + self.n)

            def link(self, ins):
                self.do(ins)
                self.hold()

        def four(g):
            return bass.ds(g * GT, GT)

        def col(v):
            return v.rearrange("(p a) -> p a", a=1)

        def rowof(v):
            return v.rearrange("(a n) -> a n", a=1)

        FULL = E // CH
        REST = E - FULL * CH

        def prep_sync(sp):
            w = S("weights")
            loads = [
                (W1x[:, 0:HF], W1), (W2_s[0:HF, :], W2), (W2_s[HF:HF + 1, :], rowof(b2)), (raw[:], L1W),
                (M1a[:], M1[0:F, :]), (M1b[:], M1[F:F + EF, :]), (M2_s[:], M2), (Mm_s[:], Mm), (Mx_s[:], Mx),
                (Ms_s[:], Ms), (W3_s[:], W3),
                (bias[:, 0, :], b2.partition_broadcast(P)), (bias[:, 1, :], L1b.partition_broadcast(P)),
                (bias[:, 2, :], bm.partition_broadcast(P)), (bias[:, 3, :], b4.partition_broadcast(P)),
                (bload[:, 0, :], bx.partition_broadcast(P)), (bload[:, 1, :], bs.partition_broadcast(P)),
                (alb[:, 0, 0:HF], al1.rearrange("h d -> (h d)").partition_broadcast(P)),
                (alb[:, 0, HF:], ar1.rearrange("h d -> (h d)").partition_broadcast(P)),
                (hT[0:HF, 0, 0, 0:F], al2.rearrange("h d -> (h d)").partition_broadcast(HF)),
                (hT[0:HF, 0, 1, 0:F], ar2.rearrange("h d -> (h d)").partition_broadcast(HF)),
                (b1c[:, 0:1], col(b1)), (m1c[:], col(m1)), (m2c[:], col(m2)),
                (attc[:, 0:1], col(att[0, 0:F])), (attc[:, 1:2], col(att[0, F:])),
            ]
            sp.wait_ge(S("pads"), 1)
            edges = [
                (e_src[0:FULL, :], src[0:FULL * CH].rearrange("(q c) -> q c", c=CH)),
                (e_src[FULL:FULL + 1, 0:REST], rowof(src[FULL * CH:E])),
                (e_dst[0:FULL, :], dst[0:FULL * CH].rearrange("(q c) -> q c", c=CH)),
                (e_dst[FULL:FULL + 1, 0:REST], rowof(dst[FULL * CH:E])),
                (e_prev[0:1, 1:CH], rowof(dst[0:CH - 1])),
                (e_prev[1:FULL, :], dst[CH - 1:FULL * CH - 1].rearrange("(q c) -> q c", c=CH)),
                (e_prev[FULL:FULL + 1, 0:REST + 1], rowof(dst[FULL * CH - 1:E])),
                (e_next[0:FULL, :], dst[1:FULL * CH + 1].rearrange("(q c) -> q c", c=CH)),
                (e_next[FULL:FULL + 1, 0:REST - 1], rowof(dst[FULL * CH + 1:E])),
            ]
            for to, frm in edges:
                sp.dma_start(to, frm).then_inc(S("edges"), 16)
            for to, frm in loads:
                sp.dma_start(to, frm).then_inc(w, 16)
            prep_sync.loads = len(loads)
            sp.wait_ge(S("cont_made"), 2)
            sp.dma_start(cont_d[0, :].rearrange("(q c) -> q c", c=CH), contb[0:NQ, 0, :]).then_inc(S("cont_out"), 16)
            sp.dma_start(cont_d[1, :].rearrange("(q c) -> q c", c=CH), contb[0:NQ, 1, :]) \
                .then_inc(S("cont_out"), 16)
            sp.wait_ge(S("cont_out"), 32)
            sp.dma_start(cont[:], cont_d[0, :].partition_broadcast(P)).then_inc(S("cont_in"), 16)

        def prep_pool(pool):
            made = S("shapes")
            nc.gpsimd.memset(ident[:], 0.0).then_inc(made, 1)
            nc.gpsimd.memset(before[:], 1.0).then_inc(made, 1)
            nc.gpsimd.memset(after[:], 1.0).then_inc(made, 1)
            pool.wait_ge(made, 3)
            nc.gpsimd.affine_select(out=ident[:], in_=ident[:], compare_op=ALU.not_equal, fill=1.0, base=0,
                                    pattern=[[-1, P]], channel_multiplier=1).then_inc(made, 1)
            nc.gpsimd.affine_select(out=before[:], in_=before[:], compare_op=ALU.is_gt, fill=0.0, base=0,
                                    pattern=[[1, NQ]], channel_multiplier=-1).then_inc(made, 1)
            nc.gpsimd.affine_select(out=after[:], in_=after[:], compare_op=ALU.is_gt, fill=0.0, base=0,
                                    pattern=[[-1, NQ]], channel_multiplier=1).then_inc(made, 1)

        def prep_tensor(pe):
            pe.wait_ge(S("shapes"), 6)
            pe.wait_ge(S("ends"), 1)
            nc.tensor.transpose(bank[5][0:NQ, 0:NQ], cv[0:NQ, 1, 0:1].to_broadcast([NQ, NQ]), ident[0:NQ, 0:NQ])
            nc.tensor.transpose(bank[5][0:NQ, P:P + NQ], cv[0:NQ, 1, CH - 1:CH].to_broadcast([NQ, NQ]),
                                ident[0:NQ, 0:NQ]).then_inc(S("endrows"), 1)
            pe.wait_ge(S("links"), 1)
            nc.tensor.matmul(bank[6][0:NQ, 0:1], linkf[0:NQ, :], cv[0:NQ, 6, CH - 1:CH], start=True, stop=True)
            nc.tensor.matmul(bank[6][0:NQ, 1:2], linkb[0:NQ, :], cv[0:NQ, 7, 0:1],
                             start=True, stop=True).then_inc(S("degc"), 1)
            pe.wait_ge(S("tomake"), 1)
            for m in range(6):
                if m % 2 == 0 and m:
                    pe.wait_ge(S("torow"), m)
                for r in range(2):
                    ins = nc.tensor.transpose(bank[m % 2][:, r * P:r * P + NQ],
                                              rowsrc[m][0:NQ, r * P:(r + 1) * P], ident[0:NQ, 0:NQ])
                ins.then_inc(S("rowps"), 1)
            pe.wait_ge(S("torow"), 6)
            pe.wait_ge(S("weights"), 16 * LOADS)
            nc.tensor.transpose(bank[0][:, 0:P], raw[:], ident[:])
            nc.tensor.transpose(bank[0][:, P:2 * P], W3_s[:], ident[:]).then_inc(S("wt"), 1)
            pe.wait_ge(S("biasc"), 1)
            for n in range(4):
                ins = nc.tensor.transpose(bank[1][:, n * P:(n + 1) * P], biasc[:, n, :], ident[:])
            ins.then_inc(S("bt"), 1)
            nc.tensor.transpose(bank[7][:, 0:P], bias[:, 2, :], ident[:]).then_inc(S("m3"), 1)
            pe.wait_ge(S("attb"), 1)
            for n in range(2):
                ins = nc.tensor.matmul(bank[2][:, n * P:(n + 1) * P], attb[:, n, :], W3T[:], start=True, stop=True)
            ins.then_inc(S("wa"), 1)
            pe.wait_ge(S("bcols"), 1)
            for n in range(4):
                ins = nc.tensor.matmul(bank[3][:, 4 * n:4 * n + 4], raw4[n], bT[:], start=True, stop=True)
            ins.then_inc(S("bb"), 1)
            pe.wait_ge(S("hcol"), 1)
            nc.tensor.matmul(bank[4][:, 0:HW], hcol[:], W2x[:, 0:HW], start=True, stop=True).then_inc(S("hrow0"), 1)

        rowsrc = [cv[:, 0, :], cv[:, 2, :], cv[:, 3, :], cv[:, 4, :], last, cv[:, 5, :]]
        raw4 = [msg[:, 0, n, :] for n in range(4)]

        def prep_vector(v):
            c = Chain(v, "prep_dve")
            for t in (e_src, e_dst, e_prev, e_next):
                c.do(v.memset(t[:], 0 if t is e_src else N))
            c.hold()
            v.memset(e_prev[0:1, 0:1], -1).then_inc(S("pads"), 1)
            c.do(v.memset(idx[:], 0))
            v.wait_ge(S("shapes"), 6)
            v.wait_ge(S("edges"), 16 * 9)
            for n, t in ((0, e_src), (1, e_dst), (8, e_prev), (9, e_next)):
                c.do(v.tensor_copy(cv[:, n, :], t[:]))
            c.hold()
            q = slice(0, NQ)
            v.sem_inc(S("ends"), 1)
            c.do(v.tensor_tensor(first[:], cv[:, 1, :], cv[:, 8, :], ALU.not_equal))
            c.do(v.tensor_tensor(last[:], cv[:, 1, :], cv[:, 9, :], ALU.not_equal))
            v.tensor_tensor(contb[:, 0, :], cv[:, 1, :], cv[:, 8, :], ALU.is_equal).then_inc(S("cont_made"), 1)
            v.tensor_tensor(contb[:, 1, :], cv[:, 1, ::-1], cv[:, 9, ::-1], ALU.is_equal).then_inc(S("cont_made"), 1)
            c.hold()
            c.do(v.tensor_scalar(keepf[:], first[:], -1.0, 1.0, ALU.mult, ALU.add))
            c.do(v.tensor_scalar(keepb[:], last[:], -1.0, 1.0, ALU.mult, ALU.add))
            c.hold()
            c.do(v.memset(keepf[:, 0:1], 0.0))
            c.do(v.memset(keepb[:, CH - 1:CH], 0.0))
            c.do(v.tensor_scalar(head[:], cv[:, 1, :], cv[:, 1, 0:1], None, ALU.is_equal))
            c.do(v.tensor_scalar(tail[:], cv[:, 1, :], cv[:, 1, CH - 1:CH], None, ALU.is_equal))
            c.hold()
            for to, frm in ((penf, keepf), (penb, keepb), (headp, head), (tailp, tail)):
                c.do(v.tensor_scalar(to[:], frm[:], -1.0, BIG, ALU.add, ALU.mult))
            v.wait_ge(S("endrows"), 1)
            c.do(v.scalar_tensor_tensor(linkf[q, :], bank[5][q, 0:NQ], cv[q, 1, CH - 1:CH], before[q, :],
                                        ALU.is_equal, ALU.mult))
            c.do(v.scalar_tensor_tensor(linkb[q, :], bank[5][q, P:P + NQ], cv[q, 1, 0:1], after[q, :],
                                        ALU.is_equal, ALU.mult))
            c.hold()
            c.do(v.tensor_scalar(linkfp[q, :], linkf[q, :], -1.0, BIG, ALU.add, ALU.mult))
            c.do(v.tensor_scalar(linkbp[q, :], linkb[q, :], -1.0, BIG, ALU.add, ALU.mult))
            c.link(v.memset(cv[:, 5, :], 1.0))
            c.do(v.tensor_tensor_scan(cv[q, 6, :], keepf[q, :], cv[q, 5, :], 0.0, ALU.mult, ALU.add))
            c.do(v.tensor_tensor_scan(cv[q, 7, ::-1], keepb[q, ::-1], cv[q, 5, :], 0.0, ALU.mult, ALU.add))
            c.hold()
            v.sem_inc(S("links"), 1)
            v.wait_ge(S("degc"), 1)
            c.link(v.tensor_copy(carry[q, 0, 0:2], bank[6][q, 0:2]))
            c.link(v.scalar_tensor_tensor(cv[q, 6, :], cv[q, 6, :], -1.0, cv[q, 7, :], ALU.add, ALU.add))
            c.link(v.scalar_tensor_tensor(cv[q, 6, :], head[q, :], carry[q, 0, 0:1], cv[q, 6, :], ALU.mult, ALU.add))
            c.link(v.scalar_tensor_tensor(cv[q, 6, :], tail[q, :], carry[q, 0, 1:2], cv[q, 6, :], ALU.mult, ALU.add))
            c.link(v.reciprocal(cv[q, 5, :], cv[q, 6, :]))
            c.do(v.tensor_scalar(cv[:, 2, :], cv[:, 1, :], float(N - 1), None, ALU.min))
            for n, m in ((3, last), (4, first)):
                c.link(v.scalar_tensor_tensor(cv[:, n, :], cv[:, 1, :], -float(SKIP), m[:], ALU.add, ALU.mult))
                c.link(v.tensor_scalar(cv[:, n, :], cv[:, n, :], float(SKIP), None, ALU.add))
            v.sem_inc(S("tomake"), 1)
            for m in range(6):
                v.wait_ge(S("rowps"), m + 1)
                to = idx[:, m, GT:GT + NT] if m < 4 else (lastR if m == 4 else invR)[:, :]
                to = to.rearrange("p (q r) -> p r q", r=2)
                v.tensor_copy(to, bank[m % 2][:, 0:2 * P].rearrange("p (r q) -> p r q", r=2)[:, :, 0:NQ]) \
                    .then_inc(S("torow"), 1)
            v.wait_ge(S("torow"), 6)
            index_first(v, "a_ix", (SRC, DST))
            v.memset(ones[:], 1.0)
            v.memset(epsc[:], EPS)
            v.wait_ge(S("weights"), 16 * LOADS)
            for n, to in ((0, W1x[:, HF:FW]), (1, W1r[:])):
                c.link(v.tensor_tensor(tmpw[:, 0:HF], W1x[:, 0:HF], alb[:, 0, n * HF:(n + 1) * HF], ALU.mult))
                c.link(v.tensor_reduce(to, tmpw[:, 0:HF].rearrange("p (h d) -> p h d", h=HEADS), X, ALU.add))
            c.do(v.tensor_copy(W2x[:, 0:HF], ident[0:HF, 0:HF]))
            for n in range(2):
                c.link(v.tensor_tensor(tmpw[0:HF, :], W2_s[0:HF, :], hT[0:HF, 0, n, 0:F], ALU.mult))
                c.link(v.tensor_reduce(W2x[:, HF + n:HF + n + 1], tmpw[0:HF, :], X, ALU.add))
            c.link(v.tensor_tensor(bias[:, 2, :], bias[:, 2, :], bload[:, 0, :], ALU.add))
            c.link(v.tensor_tensor(bias[:, 2, :], bias[:, 2, :], bload[:, 1, :], ALU.add))
            c.do(v.tensor_copy(brow[0:1, :].rearrange("p (t f) -> p t f", f=F), bias[0:1, 3:4, :].to_broadcast([1, GT, F])))
            c.link(v.tensor_reduce(wmean[:], bias[:], X, ALU.add))
            c.link(v.tensor_scalar(wmean[:], wmean[:], -1.0 / F, None, ALU.mult))
            for n in range(4):
                c.do(v.tensor_scalar(biasc[:, n, :], bias[:, n, :], wmean[:, n:n + 1], None, ALU.add))
            c.hold()
            v.sem_inc(S("biasc"), 1)
            v.wait_ge(S("wt"), 1)
            c.do(v.tensor_copy(L1T[:], bank[0][:, 0:P]))
            c.do(v.tensor_copy(W3T[:], bank[0][:, P:2 * P]))
            for n in range(2):
                c.do(v.tensor_scalar(attb[:, n, :], ones[:], attc[:, n:n + 1], None, ALU.mult))
            c.hold()
            v.sem_inc(S("attb"), 1)
            v.wait_ge(S("bt"), 1)
            c.link(v.tensor_scalar(bT[:], bank[1][:, :].rearrange("p (n m) -> p n m", n=4)[:, :, 0], 1.0 / F, None,
                                   ALU.mult))
            for n in range(4):
                c.do(v.tensor_scalar(raw4[n], ones[:], bank[1][:, n * P:n * P + 1], None, ALU.mult))
            c.hold()
            v.sem_inc(S("bcols"), 1)
            v.wait_ge(S("m3"), 1)
            c.do(v.tensor_copy(m3c[:], bank[7][:, 0:1]))
            v.wait_ge(S("wa"), 1)
            c.do(v.tensor_copy(attb[:], bank[2][:, 0:2 * P].rearrange("p (n f) -> p n f", n=2)))
            v.wait_ge(S("bb"), 1)
            c.do(v.tensor_copy(BB[:], bank[3][:, 0:16]))
            v.tensor_scalar(b1c[:, 1:2], b1c[:, 0:1], 0.0, None, ALU.min).then_inc(S("b1min"), 1)
            c.do(v.tensor_scalar(b1c[:, 2:3], b1c[:, 0:1], 0.0, None, ALU.max))
            v.wait_ge(S("b1exp"), 1)
            c.hold()
            c.link(v.scalar_tensor_tensor(b1c[:, 3:4], b1c[:, 3:4], -1.0, b1c[:, 2:3], ALU.add, ALU.add))
            v.tensor_scalar(hcol[:], ones[0:HF, :], b1c[:, 3:4], None, ALU.mult).then_inc(S("hcol"), 1)
            v.wait_ge(S("hrow0"), 1)
            for n in range(DK):
                c.do(v.tensor_copy(hconst[:, n, :], bank[4][:, 0:HW]))
            c.hold()


        def prep_scalar(a):
            a.wait_ge(S("b1min"), 1)
            nc.scalar.activation(b1c[:, 3:4], b1c[:, 1:2], ACT.Exp).then_inc(S("b1exp"), 1)

        LOADS = 26

        def index_columns(v, name, kinds, gathered, per, i, j, rev=False):
            s = (j + 2) % RING
            uses = i if j < 2 else i + 1
            if not (isinstance(uses, int) and uses == 0):
                wait(v, f"{gathered}{s}", uses * per)
                pause(v)
            g = RING * i + j + 2
            if rev:
                g = NG - 1 - g
            for n, kind in enumerate(kinds):
                v.tensor_copy(ixr[:, s, n, :], idx[:, kind, four(g + 1)]).then_inc(S(name), 1)

        def index_first(v, name, kinds, rev=False):
            for s in range(2):
                g = NG - 1 - s if rev else s
                for n, kind in enumerate(kinds):
                    v.tensor_copy(ixr[:, s, n, :], idx[:, kind, four(g + 1)]).then_inc(S(name), 1)

        def indices(eng, name, kinds, i, j):
            wait(eng, name, (RING * i + j + 1) * kinds)

        def gather(pool, to, table, s, n, done):
            for c in range(GT):
                nc.gpsimd.indirect_dma_start(
                    to(c), None, table, bass.IndirectOffsetOnAxis(ap=ixr[:, s, n, c:c + 1].bitcast(U32), axis=0)
                ).then_inc(done, 16)

        def scatter(pool, frm, table, s, n, done):
            for c in range(GT):
                nc.gpsimd.indirect_dma_start(
                    table, bass.IndirectOffsetOnAxis(ap=ixr[:, s, n, c:c + 1].bitcast(U32), axis=0), frm(c), None,
                    bounds_check=N - 1, oob_is_err=False).then_inc(done, 16)

        def norm_stats(v, tag):
            def stage(i, j):
                s = j % 2
                count(v, tag + "_z", i, j)
                for k in range(GT):
                    ins = v.bn_stats(stats[:, k, :], z[:, s, k, :])
                ins.then_inc(S(tag + "_bn"), 1)
            return stage

        def norm_var(v, tag):
            def stage(i, j):
                count(v, tag + "_bn", i, j)
                pause(v)
                for k in range(GT):
                    ins = v.bn_aggr(mv[:, 0, k, :], stats[:, k, :])
                ins.then_inc(S(tag + "_var"), 1)
            return stage

        def norm_rate(v, tag):
            def stage(i, j):
                count(v, tag + "_sd", i, j)
                count(v, tag + "_row", i, j, 2)
                v.reciprocal(rn[:, j % 2, :, 0], sd[:, 0:GT]).then_inc(S(tag + "_rc"), 1)
            return stage

        def norm_shift(v, tag, masked=False):
            def stage(i, j):
                s = j % 2
                count(v, tag + "_rc", i, j)
                v.scalar_tensor_tensor(rn[:, s, :, 1], mv[:, 0, 0:GT, 0], -1.0, rn[:, s, :, 0], ALU.mult, ALU.mult) \
                    .then_inc(S("e_rm" if masked else tag + "_st"), 1)
            return stage

        def norm_mask(v):
            def stage(i, j):
                s = j % 2
                count(v, "e_rm", i, j)
                v.tensor_tensor(rn[:, s], rn[:, s], lastR[:, four(RING * i + j)].unsqueeze(2).to_broadcast([P, GT, 2]),
                                ALU.mult).then_inc(S("e_st"), 1)
            return stage

        def norm_sqrt(a, tag, i, j):
            count(a, tag + "_var", i, j)
            nc.scalar.activation(sd[:, 0:GT], mv[:, 0, 0:GT, 1], ACT.Sqrt, bias=epsc[:]).then_inc(S(tag + "_sd"), 1)

        def norm_apply(frm, to, sc):
            for k in range(GT):
                ins = nc.scalar.activation(to[:, k, :], frm[:, k, :], ACT.Identity,
                                           bias=sc[:, k, 1:2], scale=sc[:, k, 0:1])
            return ins

        Q = slice(0, NQ)

        def softmax_tensor(pe, turn, nh, lg, work, spread):
            ee, fs, bs_ = work[3], work[4], work[5]
            fm, bm_ = work[1], work[2]
            if spread is not None:
                kind = spread[0]
                link = linkf if kind is first else linkb
                at = slice(CH - 1, CH) if kind is first else slice(0, 1)
                for r in range(2):
                    ins = nc.tensor.transpose(bank[2][Q, r * P:(r + 1) * P],
                                              own[:, :].rearrange("p (q r) -> p r q", r=2)[:, r, :], ident[:])
                ins.then_inc(S("sm_own"), 1)
                pe.wait_ge(S("sm_ownscan"), turn)
                nc.tensor.matmul(bank[3][Q, 0:1], link[Q, :], work[6][Q, 0, at],
                                 start=True, stop=True).then_inc(S("sm_owncarry"), 1)
            for r in range(2):
                for h in range(nh):
                    ins = nc.tensor.transpose(bank[r][Q, h * P:(h + 1) * P],
                                              lg.rearrange("p (q r) h -> p r h q", r=2)[:, r, h, :], ident[:])
            ins.then_inc(S("sm_lg"), 1)
            pe.wait_ge(S("sm_max"), turn + 1)
            for h in range(nh):
                nc.tensor.transpose(bank[4][Q, h * NQ:(h + 1) * NQ], fm[Q, h, CH - 1:CH].to_broadcast([NQ, NQ]),
                                    ident[Q, 0:NQ])
                ins = nc.tensor.transpose(bank[5][Q, h * NQ:(h + 1) * NQ], bm_[Q, h, 0:1].to_broadcast([NQ, NQ]),
                                          ident[Q, 0:NQ])
            ins.then_inc(S("sm_maxrow"), 1)
            pe.wait_ge(S("sm_sum"), turn + 1)
            nc.tensor.matmul(bank[6][Q, 0:nh], linkf[Q, :], fs[Q, :, CH - 1], start=True, stop=True)
            nc.tensor.matmul(bank[6][Q, nh:2 * nh], linkb[Q, :], bs_[Q, :, 0], start=True, stop=True) \
                .then_inc(S("sm_sumcarry"), 1)
            pe.wait_ge(S("sm_alpha"), turn + 1)
            for r in range(2):
                for h in range(nh):
                    ins = nc.tensor.transpose(bank[r][:, h * NQ:(h + 1) * NQ], ee[Q, h, r * P:(r + 1) * P],
                                              ident[Q, 0:NQ])
            ins.then_inc(S("sm_back"), 1)

        def softmax_vector(v, turn, nh, work, spread, guard, to):
            c = Chain(v, f"sm{turn}_dve")
            lg, fm, bm_, ee, fs, bs_, tot = (work[n] for n in range(7))

            def flat(t):
                return t[Q].rearrange("p h c -> p (h c)")

            def scans(to, keep, frm, ini, op0, op1, rev):
                for h in range(nh):
                    o, d0, d1 = to[Q, h, :], keep[Q, :], frm[Q, h, :]
                    if rev:
                        o, d0, d1 = back(o), back(d0), back(d1)
                    c.do(v.tensor_tensor_scan(o, d0, d1, ini, op0, op1))

            def back(ap):
                return ap[:, ::-1]

            if spread is not None:
                kind = spread[0]
                keep, edge = (keepf, head) if kind is first else (keepb, tail)
                v.wait_ge(S("sm_own"), turn)
                c.link(v.tensor_tensor(work[7][Q, 0, :], bank[2][Q, 0:CH], kind[Q, :], ALU.mult))
                d0, d1, o = keep[Q, :], work[7][Q, 0, :], work[6][Q, 0, :]
                if kind is last:
                    d0, d1, o = back(d0), back(d1), back(o)
                c.link(v.tensor_tensor_scan(o, d0, d1, 0.0, ALU.mult, ALU.add))
                v.sem_inc(S("sm_ownscan"), 1)
                v.wait_ge(S("sm_owncarry"), turn)
                c.link(v.tensor_copy(carry[Q, 3, 0:1], bank[3][Q, 0:1]))
                c.link(v.scalar_tensor_tensor(work[7][Q, 0, :], edge[Q, :], carry[Q, 3, 0:1], work[6][Q, 0, :],
                                              ALU.mult, ALU.add))
            v.wait_ge(S("sm_lg"), turn + 1)
            for r in range(2):
                o = lg[Q, :, r * P:(r + 1) * P]
                i_ = bank[r][Q, 0:nh * P].rearrange("p (h c) -> p h c", h=nh)
                if spread is not None:
                    c.do(v.tensor_tensor(o, i_, work[7][Q, :, r * P:(r + 1) * P], ALU.add))
                else:
                    c.do(v.tensor_copy(o, i_))
            c.hold()
            c.link(v.scalar_tensor_tensor(flat(lg), flat(lg), SLOPE, flat(lg), ALU.mult, ALU.max))
            scans(fm, penf, lg, -BIG, ALU.add, ALU.max, False)
            scans(bm_, penb, lg, -BIG, ALU.add, ALU.max, True)
            c.hold()
            v.sem_inc(S("sm_max"), 1)
            v.wait_ge(S("sm_maxrow"), turn + 1)
            for n, pen, b in ((0, linkbp, 4), (1, linkfp, 5)):
                for h in range(nh):
                    c.do(v.tensor_tensor(tot[Q, h, 0:NQ] if n == 0 else tot[Q, h, P:P + NQ],
                                         bank[b][Q, h * NQ:(h + 1) * NQ], pen[Q, :], ALU.add))
            c.hold()
            for n in range(2):
                c.do(v.tensor_reduce(carry[Q, n, 0:nh], tot[Q, :, n * P:n * P + NQ], X, ALU.max))
            c.link(v.tensor_tensor(flat(fm), flat(fm), flat(bm_), ALU.max))
            for n, edge in ((0, headp), (1, tailp)):
                for h in range(nh):
                    c.do(v.scalar_tensor_tensor(fm[Q, h, :], edge[Q, :], carry[Q, n, h:h + 1], fm[Q, h, :],
                                                ALU.add, ALU.max))
                c.hold()
            c.link(v.tensor_tensor(flat(lg), flat(lg), flat(fm), ALU.subtract))
            v.sem_inc(S("sm_centred"), 1)
            v.wait_ge(S("sm_exp"), turn + 1)
            scans(fs, keepf, ee, 0.0, ALU.mult, ALU.add, False)
            scans(bs_, keepb, ee, 0.0, ALU.mult, ALU.add, True)
            c.hold()
            v.sem_inc(S("sm_sum"), 1)
            c.link(v.tensor_tensor(flat(tot), flat(fs), flat(ee), ALU.subtract))
            c.link(v.tensor_tensor(flat(tot), flat(tot), flat(bs_), ALU.add))
            v.wait_ge(S("sm_sumcarry"), turn + 1)
            c.link(v.tensor_copy(carry[Q, 2, 0:nh], bank[6][Q, 0:nh]))
            c.link(v.tensor_copy(carry[Q, 3, 0:nh], bank[6][Q, nh:2 * nh]))
            for n, edge in ((2, head), (3, tail)):
                for h in range(nh):
                    c.do(v.scalar_tensor_tensor(tot[Q, h, :], edge[Q, :], carry[Q, n, h:h + 1], tot[Q, h, :],
                                                ALU.mult, ALU.add))
                c.hold()
            if guard:
                c.link(v.tensor_scalar(flat(tot), flat(tot), guard, None, ALU.add))
            c.link(v.reciprocal(flat(fs), flat(tot)))
            c.link(v.tensor_tensor(flat(ee), flat(ee), flat(fs), ALU.mult))
            v.sem_inc(S("sm_alpha"), 1)
            v.wait_ge(S("sm_back"), turn + 1)
            for r in range(2):
                c.do(v.tensor_copy(to.rearrange("p (q r) h -> p r h q", r=2)[:, r, :, :],
                                   bank[r][:, 0:nh * NQ].rearrange("p (h q) -> p h q", h=nh)))
            c.hold()

        def softmax_scalar(a, turn, nh, work):
            a.wait_ge(S("sm_centred"), turn + 1)
            nc.scalar.activation(work[3][Q].rearrange("p h c -> p (h c)"), work[0][Q].rearrange("p h c -> p (h c)"),
                                 ACT.Exp).then_inc(S("sm_exp"), 1)

        xmain = x[0:NJ * P, :].rearrange("(p j) f -> p j f", p=P)
        tables = (x1_t, x3_t, out)
        mains = [t[0:NJ * P, :].rearrange("(p j) f -> p j f", p=P) for t in tables]

        def is_last(i):
            return isinstance(i, int) and i == BODIES

        def dense_load(sp, tag, i, j):
            if not is_last(i):
                sp.dma_start(xin[j], xmain[:, bass.ds((RING * i + j) * DK, DK), :]).then_inc(S(f"{tag}_din{j}"), 32)
            else:
                sp.dma_start(xin[j][:, 0:DLAST, :], xmain[:, NJ - DLAST:NJ, :]).then_inc(S(f"{tag}_din{j}"), 16)
                sp.dma_start(xin[j][0:NTAIL, DLAST, :], x[NJ * P:N, :]).then_inc(S(f"{tag}_din{j}"), 16)

        def stat_load(sp):
            def stage(i, j):
                count(sp, "n_dotv", i, j, RING)
                count(sp, "n_dtr", i, j, RING)
                dense_load(sp, "n", i, j)
            return stage

        def stat_turn(i, j):
            wait(nc.tensor, f"n_din{j}", 32 * (i + 1))
            count(nc.tensor, "n_dxT", i, j, 1)
            for k in range(DP):
                ins = nc.tensor.transpose(bank[0][:, k * P:(k + 1) * P], xin[j][:, k, :], ident[:])
            ins.then_inc(S("n_dtr"), 1)

        def stat_products(i, j):
            s = j % 2
            count(nc.tensor, "n_dxT", i, j)
            count(nc.tensor, "n_dots", i, j, 2)
            for k in range(DP):
                ins = nc.tensor.matmul(bank[4 + s][:, 4 * k:4 * k + 4], dxT[:, k * P:(k + 1) * P], bT[:],
                                       start=True, stop=True)
            ins.then_inc(S("n_dmm"), 1)

        def stat_columns(i, j):
            count(nc.scalar, "n_dtr", i, j)
            count(nc.scalar, "n_dmm", i, j, 1)
            nc.scalar.activation(dxT, bank[0][:, 0:DP * F], ACT.Copy).then_inc(S("n_dxT"), 1)

        def statistics(v):
            def stage(i, j):
                s = j % 2
                cols = bass.ds((RING * i + j) * DK, DK)
                wait(v, f"n_din{j}", 32 * (i + 1))
                count(v, "n_moments", i, j, 1)
                for k in range(DK):
                    ins = v.bn_stats(stats[:, k, :], xin[j][:, k, :])
                ins.then_inc(S("n_seen"), 1)
                count(v, "n_cross", i, j, 2)
                for k in range(DP, DK):
                    for n in range(4):
                        at = (k - DP) * 4 + n
                        ins = v.tensor_tensor_reduce(waste[at // DK][:, at % DK, :], xin[j][:, k, :], biasc[:, n, :],
                                                     1.0 / F, 0.0, ALU.mult, ALU.add, dotv[:, s, k - DP, n:n + 1])
                ins.then_inc(S("n_dotv"), 1)
                count(v, "n_dmm", i, j)
                pause(v)
                v.tensor_copy(cross[:, bass.ds((RING * i + j) * DK, DP), :],
                              bank[4 + s][:, 0:4 * DP].rearrange("p (k n) -> p k n", n=4)).then_inc(S("n_dots"), 1)
                count(v, "n_dotv", i, j)
                pause(v)
                v.tensor_copy(cross[:, bass.ds((RING * i + j) * DK + DP, DK - DP), :], dotv[:, s]) \
                    .then_inc(S("n_cross"), 1)
                count(v, "n_seen", i, j)
                count(v, "n_stat", i, j, 2)
                pause(v)
                for k in range(DK):
                    ins = v.bn_aggr(mv[:, s, k, :], stats[:, k, :])
                ins.then_inc(S("n_moments"), 1)
                count(v, "n_moments", i, j)
                pause(v)
                v.tensor_copy(stat[:, cols, :], mv[:, s]).then_inc(S("n_stat"), 1)
            return stage

        def rates_vector(v):
            c = Chain(v, "rates_dve")
            var, w, r, root = temps

            def layer(n):
                def step():
                    c.hold()
                    c.link(v.scalar_tensor_tensor(var, cross[:, :, n], 2.0, w if n else stat[:, :, 1],
                                                  ALU.mult, ALU.add))
                    v.tensor_scalar(var, var, BB[:, 5 * n:5 * n + 1], None, ALU.add).then_inc(S("rates_var"), 1)
                    v.wait_ge(S("rates_root"), n + 1)
                    here = (rates[:, 0, :], r, rates[:, 3, :], rate4)[n]
                    c.link(v.reciprocal(here, rates[:, 2, :] if n == 1 else root))
                    for m in range(n + 1, 4):
                        c.do(v.scalar_tensor_tensor(cross[:, :, m], cross[:, :, m], BB[:, 4 * n + m:4 * n + m + 1],
                                                    here, ALU.add, ALU.mult))
                    if n < 3:
                        c.link(v.tensor_tensor(w, here, here, ALU.mult))
                        c.do(v.tensor_tensor(w, w, var, ALU.mult))
                    if n == 0:
                        c.do(v.scalar_tensor_tensor(rates[:, 1, :], stat[:, :, 0], -1.0, here, ALU.mult, ALU.mult))
                    if n == 2:
                        c.do(v.tensor_tensor(here, here, r, ALU.mult))
                    c.hold()
                return step
            return [layer(n) for n in range(4)]

        def rates_scalar(a):
            var, root = temps[0], temps[3]

            def layer(n):
                def step():
                    a.wait_ge(S("rates_var"), n + 1)
                    if n == 2:
                        a.wait_ge(S("rates_root"), 2)
                    nc.scalar.activation(rates[:, 2, :] if n == 1 else root, var, ACT.Sqrt, bias=epsc[:]) \
                        .then_inc(S("rates_root"), 1)
                return step
            return [layer(n) for n in range(4)]

        def last_columns(t, i, j, tag):
            if tag == "q" and is_last(i):
                return t[0:NJ * P, :].rearrange("(p j) f -> p j f", p=P)[:, NJ - DTAIL:NJ, :], True
            start = (RING * i + j) * DH + (NG * DH if tag == "q" else 0)
            return t[0:NJ * P, :].rearrange("(p j) f -> p j f", p=P)[:, bass.ds(start, DH), :], False

        def last_sync(sp, tag):
            def load(i, j):
                count(sp, tag + "_y", i, j, RING)
                main, tail_too = last_columns(x3_t, i, j, tag)
                done = S(f"{tag}_in{j}")
                if tail_too:
                    sp.dma_start(ring[:, j, 1, 0:DTAIL, :], main).then_inc(done, 16)
                    sp.dma_start(ring[0:NTAIL, j, 1, DTAIL, :], x3_t[NJ * P:N, :]).then_inc(done, 16)
                else:
                    sp.dma_start(ring[:, j, 1, :, :], main).then_inc(done, 32)

            def store(i, j):
                count(sp, tag + "_y", i, j)
                main, tail_too = last_columns(out, i, j, tag)
                done = S(f"{tag}_out{j}")
                if tail_too:
                    sp.dma_start(main, y4[j][:, 0:DTAIL, :]).then_inc(done, 16)
                    sp.dma_start(out[NJ * P:N, :], y4[j][0:NTAIL, DTAIL, :]).then_inc(done, 16)
                else:
                    sp.dma_start(main, y4[j]).then_inc(done, 32)
            return load, store

        def last_ended(sp, tag):
            for j in range(RING):
                wait(sp, f"{tag}_out{j}", 32 * (BODIES + (j == 0)))

        def last_sum(v, tag):
            def stage(i, j):
                count(v, tag + "_y", i, j, RING)
                pause(v)
                start = (RING * i + j) * DH + (NG * DH if tag == "q" else 0)
                v.tensor_copy(rate[:, j, 0, 0:DH], rate4[:, bass.ds(start, DH)]).then_inc(S(tag + "_rate"), 1)
                wait(v, f"{tag}_in{j}", 32 * (i + 1))
                v.tensor_tensor(ring[:, j, 1], ring[:, j, 1], biasc[:, 3:4, :].to_broadcast([P, DH, F]), ALU.add) \
                    .then_inc(S(tag + "_s"), 1)
            return stage

        def last_rows(a, tag):
            def stage(i, j):
                slot_done(a, tag + "_out", i, j, 32, 1)
                count(a, tag + "_rate", i, j)
                count(a, tag + "_s", i, j)
                for k in range(DH):
                    ins = nc.scalar.activation(y4[j][:, k, :], ring[:, j, 1, k, :], ACT.Copy,
                                               scale=rate[:, j, 0, k:k + 1])
                ins.then_inc(S(tag + "_y"), 1)
            return stage

        def a_pool(pool):
            def step(i, j):
                count(pool, "a_tr", i, j, RING)
                slot_done(pool, "a_out", i, j, 16, 1)
                indices(pool, "a_ix", 2, i, j)
                pause(pool)
                gather(pool, lambda c: ring[:, j, 0, c, :], x, j, 0, S(f"a_in{j}"))
                gather(pool, lambda c: ring[:, j, 1, c, :], x, j, 1, S(f"a_in{j}"))
            groups(pool, step)

        def a_sync(sp):
            main = hidden_t[0:NJ * P, :].rearrange("(p j) f -> p j f", p=P)

            def fill(i, j):
                if not is_last(i):
                    sp.dma_start(main[:, bass.ds((RING * i + j) * DK, DK), :], hconst[:]).then_inc(S("hfill"), 16)
                else:
                    sp.dma_start(main[:, NJ - DLAST:NJ, :], hconst[:, 0:DLAST, :]).then_inc(S("hfill"), 16)
                    sp.dma_start(hidden_t[NJ * P:N, :], hconst[0:NTAIL, 0, :]).then_inc(S("hfill"), 16)
            pipeline(sp, [(0, stat_load(sp)), (1, fill)])
            sp.wait_ge(S("cont_in"), 16)
            sp.wait_ge(S("hfill"), 16 * (NG + 1))

        def a_tensor(pe):
            def turn(i, j):
                wait(pe, f"a_in{j}", (i + 1) * 2 * GT * 16)
                count(pe, "a_xT", i, j, 1)
                for n in range(2):
                    for c in range(GT):
                        ins = nc.tensor.transpose(bank[2 + n][:, c * P:(c + 1) * P], ring[:, j, n, c, :], ident[:])
                ins.then_inc(S("a_tr"), 1)

            def project(i, j):
                s = j % 2
                count(pe, "a_xT", i, j)
                count(pe, "a_feat", i, j, 2)
                for c in range(GT):
                    o = bank[6 + s][:, c * PW:(c + 1) * PW]
                    nc.tensor.matmul(o[:, 0:FW], xT[:, s, 0, c * P:(c + 1) * P], W1x[:], start=True, stop=True)
                    ins = nc.tensor.matmul(o[:, FW:PW], xT[:, s, 1, c * P:(c + 1) * P], W1r[:], start=True, stop=True)
                ins.then_inc(S("a_mm"), 1)
            pipeline(pe, [(-1, stat_turn), (0, turn), (-1, stat_products), (0, project)])

        def a_scalar(a):
            def columns(i, j):
                s = j % 2
                slot_done(a, "a_in", i, j, 2 * GT * 16)
                a.dma_start(edge_row(xd_e, RING * i + j), ringf[:, j, 1, :]).then_inc(S(f"a_out{j}"), 16)
                count(a, "a_tr", i, j)
                count(a, "a_mm", i, j, 2)
                for n in range(2):
                    ins = nc.scalar.activation(xT[:, s, n, :], bank[2 + n][:], ACT.Copy)
                ins.then_inc(S("a_xT"), 1)

            def feats(i, j):
                s = j % 2
                count(a, "a_mm", i, j)
                pause(a)
                o = bank[6 + s][:, 0:GT * PW].rearrange("p (c f) -> p c f", f=PW)
                nc.scalar.activation(feat[:, four(RING * i + j), :], o[:, :, 0:FW], ACT.Copy)
                nc.scalar.activation(alpha[:, four(RING * i + j), :], o[:, :, FW:PW], ACT.Copy) \
                    .then_inc(S("a_feat"), 1)
            pipeline(a, [(-1, stat_columns), (0, columns), (0, feats)])
            for j in range(RING):
                wait(a, f"a_out{j}", 16 * (BODIES + (j == 0)))

        def a_vector(v):
            def columns(i, j):
                if not is_last(i):
                    index_columns(v, "a_ix", (SRC, DST), "a_in", 2 * GT * 16, i, j)
            pipeline(v, [(0, columns), (0, statistics(v))])
            wait(v, "a_feat", NG)
            v.tensor_tensor(feat[:, :, HF:FW], feat[:, :, HF:FW], alpha[:], ALU.add)

        def edge_row(t, g):
            return t[bass.ds(g, 1)].rearrange("a p f -> (a p) f")

        def weigh(v, i, j, frm, width, heads, rev=False):
            s = j % 2
            g = RING * i + j
            if rev:
                g = NG - 1 - g
            if frm is None:
                slot_done(v, "h_xs", i, j, 16)
                pause(v)
                rowsv = ring[:, j, 0, :, 0:width]
            else:
                rowsv = frm[:, four(g), 0:width]
            o = msg[:, s, :, 0:width]
            if heads > 1:
                d = width // heads
                return v.tensor_tensor(o.rearrange("p t (h d) -> p t h d", h=heads),
                                       rowsv.rearrange("p t (h d) -> p t h d", h=heads),
                                       alpha[:, four(g), 0:heads].unsqueeze(3).to_broadcast([P, GT, heads, d]),
                                       ALU.mult)
            return v.tensor_tensor(o, rowsv, alpha[:, four(g), 0:1].to_broadcast([P, GT, width]), ALU.mult)

        def next_of(i, j):
            return (i, j + 1) if j + 1 < RING else (i + 1, 0)

        def scan_sum(v, tag, i, j, width, src_ap, dst_t, rev=False, op=None, c=None):
            s = j % 2
            g = RING * i + j
            m = cont[0:width, bass.ds(g * GE, GE)]
            o = dst_t[0:width, s, :]
            start = isinstance(i, int) and i == 0 and j == 0
            ini = 0.0 if start else (dst_t[0:width, 1 - s, 0:1] if rev else dst_t[0:width, 1 - s, GE - 1:GE])
            if rev:
                o, src_ap = o[:, ::-1], src_ap[:, ::-1]
            return v.tensor_tensor_scan(o, m, src_ap, ini, ALU.mult, ALU.add)

        def weighing(v, tag, frm, width, heads, rev=False):
            def stage(i, j):
                count(v, tag + "_tr", i, j, 2)
                pause(v)
                weigh(v, i, j, frm, width, heads, rev).then_inc(S(tag + "_msg"), 1)
            return stage

        def scanning(v, tag, width, rev=False):
            def stage(i, j):
                s = j % 2
                count(v, tag + "_tr", i, j)
                if not (isinstance(i, int) and i == 0 and j == 0):
                    count(v, tag + "_scan", i, j, 1)
                count(v, tag + "_mm", i, j, 2)
                scan_sum(v, tag, i, j, width, bank[s][0:width, :], G, rev).then_inc(S(tag + "_scan"), 1)
            return stage

        def b_vector(v):
            index_first(v, "b_ix", (LAST,))

            def split(i, j):
                s = j % 2
                count(v, "b_scan", i, j)
                v.tensor_scalar(hT[0:HF, s, 0, :], G[0:HF, s, :], b1c[:, 0:1], 0.0, ALU.add, ALU.max)
                v.tensor_scalar(hT[0:HF, s, 1, :], G[0:HF, s, :], b1c[:, 0:1], 0.0, ALU.add, ALU.min) \
                    .then_inc(S("b_min"), 1)

            def columns(i, j):
                if not is_last(i):
                    index_columns(v, "b_ix", (LAST,), "b_sc", GT * 16, i, j)

            def join(i, j):
                s = j % 2
                count(v, "b_mm", i, j, 2)
                count(v, "b_exp", i, j)
                v.scalar_tensor_tensor(hT[0:HF, s, 2, :], hT[0:HF, s, 1, :], -1.0, hT[0:HF, s, 0, :],
                                       ALU.add, ALU.add).then_inc(S("b_h"), 1)
            pipeline(v, [(-1, weighing(v, "b", feat, HF, HEADS)), (1, join), (0, scanning(v, "b", HF)), (0, split),
                         (2, columns)],
                     rates_vector(v))

        def turning(pe, tag, width):
            def stage(i, j):
                s = j % 2
                count(pe, tag + "_msg", i, j)
                count(pe, tag + "_scan", i, j, 2)
                pause(pe)
                for c in range(GT):
                    ins = nc.tensor.transpose(bank[s][0:width, c * P:(c + 1) * P], msg[:, s, c, 0:width], ident[:])
                ins.then_inc(S(tag + "_tr"), 1)
            return stage

        def b_tensor(pe):
            def project(i, j):
                s = j % 2
                count(pe, "b_h", i, j)
                count(pe, "b_er", i, j, 2)
                for c in range(GT):
                    ins = nc.tensor.matmul(bank[2 + s][:, c * (HF + 2):(c + 1) * (HF + 2)],
                                           hT[0:HF, s, 2, c * P:(c + 1) * P], W2x[:], start=True, stop=True)
                ins.then_inc(S("b_mm"), 1)
            pipeline(pe, [(0, turning(pe, "b", HF)), (1, project)])

        def b_scalar(a):
            def expo(i, j):
                s = j % 2
                count(a, "b_min", i, j)
                nc.scalar.activation(hT[0:HF, s, 1, :], hT[0:HF, s, 1, :], ACT.Exp).then_inc(S("b_exp"), 1)

            def rows(i, j):
                s = j % 2
                count(a, "b_mm", i, j)
                slot_done(a, "b_sc", i, j, GT * 16, 1)
                ps = bank[2 + s][:, 0:GT * (HF + 2)].rearrange("p (c f) -> p c f", f=HF + 2)
                nc.scalar.activation(outr[:, j, :, 0:HW], ps[:, :, 0:HW], ACT.Copy).then_inc(S("b_row"), 1)
                nc.scalar.activation(own[:, four(RING * i + j)], ps[:, :, HW], ACT.Copy).then_inc(S("b_er"), 1)
            pipeline(a, [(0, expo), (1, rows)], rates_scalar(a))

        def b_pool(pool):
            def step(i, j):
                count(pool, "b_row", i, j)
                indices(pool, "b_ix", 1, i, j)
                pause(pool)
                scatter(pool, lambda c: outr[:, j, c, 0:HW], hidden_t, j, 0, S(f"b_sc{j}"))
            groups(pool, step)
            for j in range(RING):
                wait(pool, f"b_sc{j}", GT * 16 * (BODIES + (j == 0)))

        def c_pool(pool):
            def step(i, j):
                count(pool, "c_copy", i, j, RING)
                indices(pool, "c_ix", 1, i, j)
                pause(pool)
                gather(pool, lambda c: ring[:, j, 0, c, 0:HW], hidden_t, j, 0, S(f"c_in{j}"))
            groups(pool, step)

        def c_vector(v):
            index_first(v, "c_ix", (SRC,))

            def columns(i, j):
                if not is_last(i):
                    index_columns(v, "c_ix", (SRC,), "c_in", GT * 16, i, j)

            def first_sum(i, j):
                count(v, "m_y3", i, j, RING)
                pause(v)
                v.tensor_copy(rate[:, j], rates[:, :, bass.ds((RING * i + j) * DK, DK)]).then_inc(S("m_rate"), 1)
                wait(v, f"m_din{j}", 32 * (i + 1))
                v.tensor_tensor(xin[j], xin[j], spread_bias(0), ALU.add).then_inc(S("m_s1"), 1)

            def middle_sum(i, j):
                count(v, "m_y1", i, j)
                count(v, "m_y3", i, j, 1)
                count(v, "m_y3b", i, j, 1)
                v.tensor_tensor(s23, y[0][j % 2], spread_bias(1), ALU.add).then_inc(S("m_s2"), 1)
                count(v, "m_s2", i, j)
                count(v, "m_rate", i, j)
                for k in range(DK):
                    ins = v.scalar_tensor_tensor(s23[:, k, :], biasc[:, 2, :], rate[:, j, 2, k:k + 1], s23[:, k, :],
                                                 ALU.mult, ALU.add)
                ins.then_inc(S("m_s3"), 1)

            def middle_rows(i, j):
                s = j % 2
                uses = 2 * i + j // 2
                if not (isinstance(uses, int) and uses == 0):
                    wait(v, f"m_y3_out{s}", 32 * uses)
                count(v, "m_s3", i, j)
                v.tensor_tensor(y[1][s][:, DH:DK, :], s23[:, DH:DK, :],
                                rate[:, j, 3, DH:DK].unsqueeze(2).to_broadcast([P, DK - DH, F]), ALU.mult) \
                    .then_inc(S("m_y3b"), 1)
            pipeline(v, [(0, columns), (1, middle_sum), (-1, first_sum), (1, middle_rows)])

        def spread_bias(n):
            return biasc[:, n:n + 1, :].to_broadcast([P, DK, F])

        def c_sync(sp):
            def load(i, j):
                count(sp, "m_y1", i, j, RING)
                dense_load(sp, "m", i, j)

            def store(n, name):
                def stage(i, j):
                    s = j % 2
                    count(sp, f"m_{name}", i, j)
                    if name == "y3":
                        count(sp, "m_y3b", i, j)
                    done = S(f"m_{name}_out{s}")
                    if not is_last(i):
                        sp.dma_start(mains[n][:, bass.ds((RING * i + j) * DK, DK), :], y[n][s]).then_inc(done, 32)
                    else:
                        sp.dma_start(mains[n][:, NJ - DLAST:NJ, :], y[n][s][:, 0:DLAST, :]).then_inc(done, 16)
                        sp.dma_start(tables[n][NJ * P:N, :], y[n][s][0:NTAIL, DLAST, :]).then_inc(done, 16)
                return stage
            pipeline(sp, [(0, load), (3, store(0, "y1")), (4, store(1, "y3"))])
            for name in ("y1", "y3"):
                for s in range(2):
                    wait(sp, f"m_{name}_out{s}", 32 * len(range(s, NG, 2)))

        def c_scalar(a):
            def copy(i, j):
                slot_done(a, "c_in", i, j, GT * 16)
                pause(a)
                nc.scalar.activation(feat[:, four(RING * i + j), 0:HF], ring[:, j, 0, :, 0:HF], ACT.Copy)
                nc.scalar.activation(logit[:, four(RING * i + j), 0], ring[:, j, 0, :, HF], ACT.Copy) \
                    .then_inc(S("c_copy"), 1)

            def stored(name, i, j):
                uses = 2 * i + j // 2
                if not (isinstance(uses, int) and uses == 0):
                    wait(a, f"m_{name}_out{j % 2}", 32 * uses)

            def first_rows(i, j):
                stored("y1", i, j)
                count(a, "m_s2", i, j, 2)
                count(a, "m_rate", i, j)
                count(a, "m_s1", i, j)
                for k in range(DK):
                    ins = nc.scalar.activation(y[0][j % 2][:, k, :], xin[j][:, k, :], ACT.Identity,
                                               bias=rate[:, j, 1, k:k + 1], scale=rate[:, j, 0, k:k + 1])
                ins.then_inc(S("m_y1"), 1)

            def middle_rows(i, j):
                stored("y3", i, j)
                count(a, "m_s3", i, j)
                for k in range(DH):
                    ins = nc.scalar.activation(y[1][j % 2][:, k, :], s23[:, k, :], ACT.Copy,
                                               scale=rate[:, j, 3, k:k + 1])
                ins.then_inc(S("m_y3"), 1)

            pipeline(a, [(0, first_rows), (0, copy), (1, middle_rows)])

        def attend_vector(v, tag, frm, width, kind, rev):
            index_first(v, tag + "_ix", (kind,), rev)
            if width < P:
                v.memset(G[width:width + 1, :, :], 1.0).then_inc(S(tag + "_ones"), 1)

            def columns(i, j):
                if not is_last(i):
                    index_columns(v, tag + "_ix", (kind,), tag + "_sc", GT * 16, i, j, rev)

            def residual(i, j):
                s = j % 2
                count(v, tag + "_mm", i, j)
                wait(v, f"{tag}_ld{s}", 16 * (2 * i + j // 2 + 1))
                count(v, tag + "_row", i, j, 2)
                v.tensor_tensor(z[:, s], bank[2 + s][:].rearrange("p (t f) -> p t f", f=F), xload[:, s], ALU.add) \
                    .then_inc(S(tag + "_z"), 1)
            pipeline(v, [(0, scanning(v, tag, width, rev)), (2, norm_rate(v, tag)),
                         (-1, weighing(v, tag, frm, width, 1, rev)), (2, norm_shift(v, tag)), (1, residual),
                         (2, columns), (1, norm_stats(v, tag))] +
                     ([(0, last_sum(v, "p"))] if tag == "d" else []) + [(1, norm_var(v, tag))])

        def attend_tensor(pe, tag, width, W, b):
            def project(i, j):
                s = j % 2
                count(pe, tag + "_scan", i, j)
                count(pe, tag + "_z", i, j, 2)
                if b:
                    nc.tensor.matmul(bank[2 + s][:], ones[0:1, 0:P], brow[:], start=True, stop=False)
                k = width if b else width + 1
                for c in range(GT):
                    ins = nc.tensor.matmul(bank[2 + s][:, c * F:(c + 1) * F], G[0:k, s, c * P:(c + 1) * P], W[:],
                                           start=not b, stop=not b or c == GT - 1)
                ins.then_inc(S(tag + "_mm"), 1)
            if not b:
                wait(pe, tag + "_ones", 1)
            pipeline(pe, [(0, turning(pe, tag, width)), (1, project)])

        def attend_scalar(a, tag, stored):
            def step(i, j):
                s = j % 2
                norm_sqrt(a, tag, i, j)
                if stored:
                    last_rows(a, "p")(i, j)
                count(a, tag + "_st", i, j)
                slot_done(a, tag + "_sc", i, j, GT * 16, 1)
                if stored:
                    slot_done(a, tag + "_out", i, j, 16, 1)
                norm_apply(z[:, s], outr[:, j], rn[:, s]).then_inc(S(tag + "_row"), 1)
            groups(a, step)

        def attend_pool(pool, tag, table):
            def step(i, j):
                count(pool, tag + "_row", i, j)
                indices(pool, tag + "_ix", 1, i, j)
                pause(pool)
                scatter(pool, lambda c: outr[:, j, c, :], table, j, 0, S(f"{tag}_sc{j}"))
            groups(pool, step)
            for j in range(RING):
                wait(pool, f"{tag}_sc{j}", GT * 16 * (BODIES + (j == 0)))

        def linear_sync(sp, tag, table, to, rev, used, more=None, last=None):
            def load(i, j):
                s = j % 2
                g = RING * i + j
                count(sp, tag + used, i, j, 2)
                sp.dma_start(xloadf[:, s, :], edge_row(table, NG - 1 - g if rev else g)) \
                    .then_inc(S(f"{tag}_ld{s}"), 16)

            def rows(i, j):
                g = RING * i + j
                count(sp, tag + "_msg", i, j, RING)
                sp.dma_start(ringf[:, j, 0, :], edge_row(more, NG - 1 - g if rev else g)) \
                    .then_inc(S(f"{tag}_xs{j}"), 16)

            def store(i, j):
                g = RING * i + j
                count(sp, tag + "_row", i, j)
                sp.dma_start(edge_row(to, NG - 1 - g if rev else g), outf[:, j, :]).then_inc(S(f"{tag}_out{j}"), 16)
            if more is None:
                last_load, last_store = last_sync(sp, last)
                pipeline(sp, [(0, load), (0, last_load), (3, last_store), (3, store)])
                last_ended(sp, last)
            else:
                pipeline(sp, [(-1, rows), (1, load)])
            if to is not None:
                for j in range(RING):
                    wait(sp, f"{tag}_out{j}", 16 * (BODIES + (j == 0)))

        def e_pool(pool):
            def step(i, j):
                count(pool, "e_tr", i, j, RING)
                indices(pool, "e_ix", 1, i, j)
                pause(pool)
                gather(pool, lambda c: ring[:, j, 0, c, :], x1_t, j, 0, S(f"e_in{j}"))
            groups(pool, step)

        def e_tensor(pe):
            def turn(i, j):
                s = j % 2
                slot_done(pe, "e_in", i, j, GT * 16)
                count(pe, "e_scan", i, j, 2)
                for c in range(GT):
                    ins = nc.tensor.transpose(bank[s][:, c * P:(c + 1) * P], ring[:, j, 0, c, :], ident[:])
                ins.then_inc(S("e_tr"), 1)

            def project(i, j):
                s = j % 2
                count(pe, "e_scan", i, j)
                count(pe, "e_zp", i, j, 2)
                for c in range(GT):
                    ins = nc.tensor.matmul(bank[2 + s][:, c * F:(c + 1) * F], G[:, s, c * P:(c + 1) * P], L1T[:],
                                           start=True, stop=True)
                ins.then_inc(S("e_mm"), 1)
            pipeline(pe, [(0, turn), (1, project)])

        def e_vector(v):
            index_first(v, "e_ix", (SRC,))

            def columns(i, j):
                if not is_last(i):
                    index_columns(v, "e_ix", (SRC,), "e_in", GT * 16, i, j)

            def residual(i, j):
                s = j % 2
                g = RING * i + j
                count(v, "e_mm", i, j)
                wait(v, f"e_ld{s}", 16 * (2 * i + j // 2 + 1))
                count(v, "e_row", i, j, 2)
                for k in range(GT):
                    ins = v.scalar_tensor_tensor(z[:, s, k, :], bank[2 + s][:, k * F:(k + 1) * F],
                                                 invR[:, bass.ds(g * GT + k, 1)], xload[:, s, k, :],
                                                 ALU.mult, ALU.add)
                ins.then_inc(S("e_zp"), 1)

            def add_bias(i, j):
                s = j % 2
                count(v, "e_zp", i, j)
                v.tensor_tensor(z[:, s], z[:, s], bias[:, 1:2, :].to_broadcast([P, GT, F]), ALU.add) \
                    .then_inc(S("e_z"), 1)
            pipeline(v, [(0, columns), (0, scanning(v, "e", P)), (2, norm_rate(v, "e")), (1, residual),
                         (2, norm_shift(v, "e", True)), (1, add_bias), (2, norm_mask(v)), (1, norm_stats(v, "e")),
                         (0, last_sum(v, "q")), (1, norm_var(v, "e"))])

        def e_scalar(a):
            def step(i, j):
                s = j % 2
                norm_sqrt(a, "e", i, j)
                last_rows(a, "q")(i, j)
                count(a, "e_st", i, j)
                slot_done(a, "e_out", i, j, 16, 1)
                norm_apply(z[:, s], outr[:, j], rn[:, s]).then_inc(S("e_row"), 1)
            groups(a, step)

        eaR = ring[:, 0:2, 1, :, 0:EF]

        def f_sync(sp):
            sp.dma_start(cont[:].rearrange("p (q c) -> p q c", c=CH),
                         cont_d[1, :].rearrange("(q c) -> q c", c=CH)[::-1, :].partition_broadcast(P)) \
                .then_inc(S("cont_in"), 16)
            def load(i, j):
                s = j % 2
                g = NG - 1 - (RING * i + j)
                count(sp, "f_tr", i, j, 2)
                sp.dma_start(ring[:, s, 0].rearrange("p t f -> p (t f)"), edge_row(x2_e, g)) \
                    .then_inc(S(f"f_x{s}"), 16)
                if isinstance(i, int) and i == 0 and j == 0:
                    full = (E - (NG - 1) * GE) // P
                    base = (NG - 1) * GE
                    wait(sp, "f_pad", 1)
                    sp.dma_start(eaR[:, s, 0:full, :], ea[base:base + full * P, :].rearrange("(c p) f -> p c f", p=P)) \
                        .then_inc(S(f"f_ea{s}"), 16)
                    sp.dma_start(eaR[0:E - base - full * P, s, full, :], ea[base + full * P:E, :]) \
                        .then_inc(S(f"f_ea{s}"), 16)
                else:
                    sp.dma_start(eaR[:, s], ea[bass.ds(g * GE, GE), :].rearrange("(c p) f -> p c f", p=P)) \
                        .then_inc(S(f"f_ea{s}"), 32)

            def store(i, j):
                g = NG - 1 - (RING * i + j)
                count(sp, "f_row", i, j)
                sp.dma_start(edge_row(x3_e, g), outf[:, j, :]).then_inc(S(f"f_out{j}"), 16)
            pipeline(sp, [(-1, load), (3, store)])
            for j in range(RING):
                wait(sp, f"f_out{j}", 16 * (BODIES + (j == 0)))

        def f_tensor(pe):
            def turn(i, j):
                s = j % 2
                uses = 2 * i + j // 2 + 1
                wait(pe, f"f_x{s}", 16 * uses)
                wait(pe, f"f_ea{s}", 32 * uses)
                count(pe, "f_spread", i, j, 1)
                for c in range(GT):
                    nc.tensor.transpose(bank[0][:, c * P:(c + 1) * P], ring[:, s, 0, c, :], ident[:])
                count(pe, "f_eaT", i, j, 1)
                pause(pe)
                for c in range(GT):
                    ins = nc.tensor.transpose(bank[1][0:EF, c * P:(c + 1) * P], eaR[:, s, c, :], ident[:])
                ins.then_inc(S("f_tr"), 1)

            def hidden(i, j):
                s = j % 2
                count(pe, "f_spread", i, j)
                count(pe, "f_eaT", i, j)
                count(pe, "f_relu", i, j, 1)
                nc.tensor.matmul(bank[2][:], M1a[:], X2T[:, j, :], start=True, stop=False)
                nc.tensor.matmul(bank[2][:], M1b[:], eaT[:, s, :], start=False, stop=True).then_inc(S("f_m1"), 1)

            def message(i, j):
                s = j % 2
                count(pe, "f_relu", i, j)
                count(pe, "f_msg", i, j, 1)
                nc.tensor.matmul(bank[3][:], M2_s[:], hT[:, s, 0, :], start=True, stop=True).then_inc(S("f_m2"), 1)

            def combine(i, j):
                s = j % 2
                count(pe, "f_max", i, j)
                count(pe, "f_aT", i, j, 1)
                count(pe, "f_bT", i, j, 1)
                nc.tensor.matmul(bank[4][:], Mm_s[:], G[:, s, :], start=True, stop=True)
                nc.tensor.matmul(bank[5][:], Ms_s[:], G[:, s, :], start=True, stop=False)
                nc.tensor.matmul(bank[5][:], Mx_s[:], MX[:, s, :], start=False, stop=True).then_inc(S("f_mm2"), 1)

            def rows(i, j):
                s = j % 2
                count(pe, "f_aT", i, j)
                count(pe, "f_bT", i, j)
                count(pe, "f_zA", i, j, 1)
                count(pe, "f_z", i, j, 1)
                for n, t in ((6, aT), (7, bT2)):
                    for c in range(GT):
                        ins = nc.tensor.transpose(bank[n][:, c * P:(c + 1) * P], t[:, s, c * P:(c + 1) * P], ident[:])
                ins.then_inc(S("f_back"), 1)
            pipeline(pe, [(0, hidden), (-1, turn), (2, rows), (0, message), (1, combine)])

        def f_scalar(a):
            def relu(i, j):
                s = j % 2
                count(a, "f_m1", i, j)
                count(a, "f_m2", i, j, 2)
                nc.scalar.activation(hT[:, s, 0, :], bank[2][:], ACT.Relu, bias=m1c[:]).then_inc(S("f_relu"), 1)

            def edges(i, j):
                s = j % 2
                count(a, "f_tr", i, j)
                count(a, "f_m1", i, j, 2)
                nc.scalar.activation(eaT[:, s, :], bank[1][0:EF, :], ACT.Copy).then_inc(S("f_eaT"), 1)

            def message(i, j):
                s = j % 2
                count(a, "f_m2", i, j)
                count(a, "f_max", i, j, 2)
                nc.scalar.activation(hT[:, s, 1, :], bank[3][:], ACT.Identity, bias=m2c[:]).then_inc(S("f_msg"), 1)

            def means(i, j):
                s = j % 2
                g = NG - 1 - (RING * i + j)
                count(a, "f_back", i, j)
                count(a, "f_z", i, j, 2)
                pause(a)
                for c in range(GT):
                    ins = nc.scalar.activation(zA[:, s, c, :], bank[6][:, c * F:(c + 1) * F], ACT.Copy,
                                               scale=invR[:, bass.ds(g * GT + c, 1)])
                ins.then_inc(S("f_zA"), 1)

            def columns(i, j):
                s = j % 2
                count(a, "f_mm2", i, j)
                count(a, "f_back", i, j, 2)
                nc.scalar.activation(aT[:, s, :], bank[4][:], ACT.Copy).then_inc(S("f_aT"), 1)

            def root(i, j):
                norm_sqrt(a, "f", i, j)

            def apply(i, j):
                s = j % 2
                count(a, "f_st", i, j)
                slot_done(a, "f_sc", i, j, GT * 16, 1)
                slot_done(a, "f_out", i, j, 16, 1)
                norm_apply(z[:, s], outr[:, j], rn[:, s]).then_inc(S("f_row"), 1)
            pipeline(a, [(0, relu), (-1, edges), (3, apply), (0, message), (2, means), (1, columns), (2, root)])

        def f_vector(v):
            v.memset(eaR[:, 0], 0.0).then_inc(S("f_pad"), 1)
            index_first(v, "f_ix", (FIRST,), True)

            def scale(i, j):
                if not is_last(i):
                    index_columns(v, "f_ix", (FIRST,), "f_sc", GT * 16, i, j, True)
                norm_rate(v, "f")(i, j)
                norm_shift(v, "f")(i, j)

            def spread(i, j):
                start = isinstance(i, int) and i == 0 and j == 0
                if start:
                    v.wait_ge(S("cont_in"), 32)
                else:
                    count(v, "f_spread", i, j, 1)
                count(v, "f_tr", i, j)
                count(v, "f_m1", i, j, RING)
                m = cont[:, bass.ds((RING * i + j) * GE, GE)]
                ini = 0.0 if start else X2T[:, (j - 1) % RING, 0:1]
                v.tensor_tensor_scan(X2T[:, j, ::-1], m, bank[0][:, ::-1], ini, ALU.mult, ALU.add) \
                    .then_inc(S("f_spread"), 1)

            def penalty(i, j):
                m = cont[:, bass.ds((RING * i + j) * GE, GE)]
                count(v, "f_max", i, j, 2)
                pause(v)
                v.tensor_scalar(neg[:, j % 2, :], m, -1.0, -FAR, ALU.add, ALU.mult).then_inc(S("f_neg"), 1)

            def totals(i, j):
                s = j % 2
                start = isinstance(i, int) and i == 0 and j == 0
                count(v, "f_msg", i, j)
                count(v, "f_mm2", i, j, 2)
                if not start:
                    count(v, "f_sum", i, j, 1)
                scan_sum(v, "f", i, j, P, hT[:, s, 1, :], G, True).then_inc(S("f_sum"), 1)
                count(v, "f_neg", i, j)
                if not start:
                    count(v, "f_max", i, j, 1)
                ini = FAR if start else MX[:, 1 - s, 0:1]
                v.tensor_tensor_scan(MX[:, s, ::-1], neg[:, s, :], hT[:, s, 1, ::-1], ini, ALU.add, ALU.max) \
                    .then_inc(S("f_max"), 1)

            def columns(i, j):
                s = j % 2
                count(v, "f_mm2", i, j)
                count(v, "f_back", i, j, 2)
                v.scalar_tensor_tensor(bT2[:, s, :], bank[5][:], m3c[:], X2T[:, j, :], ALU.add, ALU.add) \
                    .then_inc(S("f_bT"), 1)

            def residual(i, j):
                s = j % 2
                count(v, "f_back", i, j)
                count(v, "f_zA", i, j)
                count(v, "f_row", i, j, 2)
                v.tensor_tensor(z[:, s], bank[7][:].rearrange("p (t f) -> p t f", f=F), zA[:, s], ALU.add) \
                    .then_inc(S("f_z"), 1)
            pipeline(v, [(3, scale), (-1, spread), (0, penalty), (0, totals), (2, residual), (2, norm_stats(v, "f")),
                         (2, norm_var(v, "f")), (1, columns)])

        def g_pool(pool):
            def step(i, j):
                slot_done(pool, "g_out", i, j, 16, 1)
                count(pool, "g_dot", i, j, RING)
                indices(pool, "g_ix", 1, i, j)
                pause(pool)
                gather(pool, lambda c: ring[:, j, 0, c, :], x3_t, j, 0, S(f"g_in{j}"))
            groups(pool, step)

        def g_vector(v):
            c = Chain(v, "g_dve")
            index_first(v, "g_ix", (SRC,))

            def step(i, j):
                s = j % 2
                g = RING * i + j
                c.at(i, j)
                if not is_last(i):
                    index_columns(v, "g_ix", (SRC,), "g_in", GT * 16, i, j)
                wait(v, f"g_ld{s}", 16 * (2 * i + j // 2 + 1))
                slot_done(v, "g_in", i, j, GT * 16)
                for n in range(2):
                    for k in range(GT):
                        frm = ring[:, j, 0, k, :] if n else xload[:, s, k, :]
                        c.do(v.tensor_tensor_reduce(msg[:, n, k, :], frm, attb[:, n, :], 1.0, 0.0, ALU.mult, ALU.add,
                                                    dots[:, k, n:n + 1]))
                c.hold()
                pause(v)
                v.tensor_copy(own[:, four(g)], dots[:, 0:GT, 0])
                v.tensor_copy(logit[:, four(g), 0], dots[:, 0:GT, 1]).then_inc(S("g_dot"), 1)
                count(v, "g_dot", i, j)
            groups(v, step)

        def g_sync(sp):
            def load(i, j):
                s = j % 2
                count(sp, "g_dot", i, j, 2)
                sp.dma_start(xloadf[:, s, :], edge_row(x3_e, RING * i + j)).then_inc(S(f"g_ld{s}"), 16)
            load(0, 0)

            def step(i, j):
                if not is_last(i):
                    load(*next_of(i, j))
                slot_done(sp, "g_in", i, j, GT * 16)
                sp.dma_start(edge_row(xs_e, RING * i + j), ringf[:, j, 0, :]).then_inc(S(f"g_out{j}"), 16)
            groups(sp, step)
            for j in range(RING):
                wait(sp, f"g_out{j}", 16 * (BODIES + (j == 0)))

        block = ctx.enter_context(nc.Block())

        @block.sync
        def _(sp):
            prep_sync(sp)
            assert prep_sync.loads == LOADS
            barrier(sp)
            a_sync(sp)
            barrier(sp)
            barrier(sp)
            c_sync(sp)
            barrier(sp)
            barrier(sp)
            linear_sync(sp, "d", xd_e, x1_e, False, "_z", last="p")
            barrier(sp)
            linear_sync(sp, "e", x1_e, x2_e, False, "_z", last="q")
            barrier(sp)
            f_sync(sp)
            barrier(sp)
            g_sync(sp)
            barrier(sp)
            linear_sync(sp, "h", x3_e, None, True, "_z", xs_e)
            barrier(sp)

        @block.gpsimd
        def _(pool):
            prep_pool(pool)
            arrive(pool)
            a_pool(pool)
            barrier(pool)
            b_pool(pool)
            barrier(pool)
            c_pool(pool)
            barrier(pool)
            barrier(pool)
            attend_pool(pool, "d", x1_t)
            barrier(pool)
            e_pool(pool)
            barrier(pool)
            attend_pool(pool, "f", x3_t)
            barrier(pool)
            g_pool(pool)
            barrier(pool)
            attend_pool(pool, "h", out)
            barrier(pool)

        @block.tensor
        def _(pe):
            prep_tensor(pe)
            barrier(pe)
            a_tensor(pe)
            barrier(pe)
            softmax_tensor(pe, 0, HEADS, feat[:, :, HF:FW], wide, None)
            b_tensor(pe)
            barrier(pe)
            barrier(pe)
            softmax_tensor(pe, 1, 1, logit[:, :, 0:1], slim, (last,))
            barrier(pe)
            attend_tensor(pe, "d", HF, W2_s, 0)
            barrier(pe)
            e_tensor(pe)
            barrier(pe)
            f_tensor(pe)
            barrier(pe)
            barrier(pe)
            softmax_tensor(pe, 2, 1, logit[:, :, 0:1], slim, (first,))
            attend_tensor(pe, "h", P, W3_s, 1)
            barrier(pe)

        @block.scalar
        def _(a):
            prep_scalar(a)
            barrier(a)
            a_scalar(a)
            barrier(a)
            softmax_scalar(a, 0, HEADS, wide)
            b_scalar(a)
            barrier(a)
            c_scalar(a)
            barrier(a)
            softmax_scalar(a, 1, 1, slim)
            barrier(a)
            attend_scalar(a, "d", True)
            barrier(a)
            e_scalar(a)
            barrier(a)
            f_scalar(a)
            barrier(a)
            barrier(a)
            softmax_scalar(a, 2, 1, slim)
            attend_scalar(a, "h", False)
            barrier(a)

        @block.vector
        def _(v):
            prep_vector(v)
            barrier(v)
            a_vector(v)
            barrier(v)
            softmax_vector(v, 0, HEADS, wide, None, None, alpha[:, :, 0:HEADS])
            b_vector(v)
            barrier(v)
            c_vector(v)
            barrier(v)
            softmax_vector(v, 1, 1, slim, (last,), None, alpha[:, :, 0:1])
            barrier(v)
            attend_vector(v, "d", feat, HF, LAST, False)
            barrier(v)
            e_vector(v)
            barrier(v)
            f_vector(v)
            barrier(v)
            g_vector(v)
            barrier(v)
            softmax_vector(v, 2, 1, slim, (first,), 1e-16, alpha[:, :, 0:1])
            attend_vector(v, "h", None, P, FIRST, True)
            barrier(v)


_INS = ['x', 'src', 'dst', 'edge_attr_64', 'L0_gnn_W1', 'L0_gnn_al1', 'L0_gnn_ar1', 'L0_gnn_b1', 'L0_gnn_W2',
        'L0_gnn_al2', 'L0_gnn_ar2', 'L0_gnn_b2', 'L1_gnn_W', 'L1_gnn_b', 'L2_gnn_W1', 'L2_gnn_b1', 'L2_gnn_W2',
        'L2_gnn_b2', 'L2_gnn_Wm', 'L2_gnn_bm', 'L2_gnn_Wx', 'L2_gnn_bx', 'L2_gnn_Ws', 'L2_gnn_bs', 'L3_gnn_W',
        'L3_gnn_att', 'L3_gnn_bias']


def kernel(**inputs):
    import numpy as _np
    import concourse.bacc as _bacc
    from concourse import mybir as _mybir
    from concourse.bass_utils import run_bass_kernel_spmd as _run

    nc = _bacc.Bacc("TRN2", target_bir_lowering=False, num_devices=1)
    arrays, args = {}, []
    for name in _INS:
        a = _np.ascontiguousarray(inputs[name])
        arrays[f"in_{name}_dram"] = a
        args.append(nc.dram_tensor(f"in_{name}_dram", a.shape, _mybir.dt.from_np(a.dtype), kind="ExternalInput").ap())
    args.append(nc.dram_tensor("out_0_dram", (N, F), _mybir.dt.float32, kind="ExternalOutput").ap())
    program(nc, *args)
    r = _run(nc, [arrays], core_ids=[0])
    return r.results[0]["out_0_dram"]
```
